# Optimizing a Trainium2 kernel written in Bass

```python
import numpy as np
import jax
import jax.numpy as jnp

def _softmax(x, axis=-1):
    return jax.nn.softmax(x, axis=axis)

def _gelu(x):
    return jax.nn.gelu(x, approximate=True)

def _silu(x):
    return jax.nn.silu(x)

def _sigmoid(x):
    return jax.nn.sigmoid(x)

def _layernorm(x, axis=-1, eps=1e-05):
    m = jnp.mean(x, axis=axis, keepdims=True)
    v = jnp.var(x, axis=axis, keepdims=True)
    return (x - m) / jnp.sqrt(v + eps)

def _scatter_add(tgt, idx, src, axis=0):
    return tgt.at[idx].add(src)

def _segment_sum(src, seg, n):
    return jax.ops.segment_sum(src, seg, n)
kernel_name = 'mk_perceiver_d2_seqx_r8_28f47f'

def setup_inputs(seed: int=0):
    np.random.seed(seed)
    _w = jnp.asarray

    def _rec_inputs():
        import jax
        import jax.numpy as jnp
        _rk = jax.random.key(seed)
        x = 0.0002417 + 0.9998 * jax.random.normal(jax.random.fold_in(_rk, 1), (1, 64, 128), jnp.float32)
        _lenS = 64 - jax.random.randint(jax.random.fold_in(_rk, 7), (1,), 0, max(1, 64 // 4) + 1, jnp.int32)
        _lenS2 = 6272 - jax.random.randint(jax.random.fold_in(_rk, 8), (1,), 0, max(1, 6272 // 4) + 1, jnp.int32)
        _ctx_1024P = jax.random.normal(jax.random.fold_in(_rk, 11), (1, 16, 128), jnp.float32)
        _ctx_1024c = jax.random.dirichlet(jax.random.fold_in(_rk, 511), 0.3 * jnp.ones((16,), jnp.float32), (1, 6272))
        _ctx_1024t = jnp.einsum('bsk,bkd->bsd', _ctx_1024c, _ctx_1024P)
        _ctx_1024t = _ctx_1024t * jax.lax.rsqrt(jnp.mean(jnp.square(_ctx_1024t)) + 1e-12) * 0.953939
        ctx_1024 = 7.22013e-05 + 1.00017 * (_ctx_1024t + 0.3 * jax.random.normal(jax.random.fold_in(_rk, 611), (1, 6272, 128), jnp.float32))
        return (x, ctx_1024)
    x, ctx_1024 = _rec_inputs()

    def _L0_xattn_setup():
        import jax, jax.numpy as jnp
        import numpy as np
        D_MODEL = 128
        B, S = (4, 256)
        key = jax.random.key(seed)
        ks = jax.random.split(key, 10)
        s = 1.0 / np.sqrt(D_MODEL)
        return {'k': jax.random.normal(ks[0], (B, S, D_MODEL), jnp.float32), 'v': jax.random.normal(ks[1], (B, S, D_MODEL), jnp.float32), 'q': jax.random.normal(ks[2], (B, S, D_MODEL), jnp.float32), 'Wk': jax.random.normal(ks[3], (D_MODEL, D_MODEL), jnp.float32) * s, 'Wv': jax.random.normal(ks[4], (D_MODEL, D_MODEL), jnp.float32) * s, 'bv': jnp.zeros((D_MODEL,), jnp.float32), 'Wq': jax.random.normal(ks[5], (D_MODEL, D_MODEL), jnp.float32) * s, 'bq': jnp.zeros((D_MODEL,), jnp.float32), 'Wo': jax.random.normal(ks[6], (D_MODEL, D_MODEL), jnp.float32) * s, 'bo': jnp.zeros((D_MODEL,), jnp.float32)}
    _L0_xattn_all = _L0_xattn_setup()
    _L0_xattn_in = {k: v for k, v in _L0_xattn_all.items() if k in ('Wk', 'Wv', 'bv', 'Wq', 'bq', 'Wo', 'bo')}
    del _L0_xattn_all

    def _L0_attn_setup():
        import jax, jax.numpy as jnp
        import numpy as np
        H = 8
        LN_EPS = 1e-05
        key = jax.random.key(seed)
        ks = jax.random.split(key, 4)
        B, S, D = (4, 256, 128)
        x = jax.random.normal(ks[0], (B, S, D), dtype=jnp.float32)
        sc = 1.0 / np.sqrt(D)
        Wq = jax.random.normal(ks[1], (D, D), dtype=jnp.float32) * sc
        Wk = jax.random.normal(ks[2], (D, D), dtype=jnp.float32) * sc
        Wv = jax.random.normal(ks[3], (D, D * H), dtype=jnp.float32) * sc
        return {'x': x, 'Wq': Wq, 'bq': jnp.zeros((D,), jnp.float32), 'Wk': Wk, 'bk': jnp.zeros((D,), jnp.float32), 'Wv': Wv, 'bv': jnp.zeros((D * H,), jnp.float32), 'gamma': jnp.ones((D,), jnp.float32), 'beta': jnp.zeros((D,), jnp.float32)}
    _L0_attn_all = _L0_attn_setup()
    _L0_attn_in = {k: v for k, v in _L0_attn_all.items() if k in ('Wq', 'bq', 'Wk', 'bk', 'Wv', 'bv', 'gamma', 'beta')}
    del _L0_attn_all

    def _L0_ffn_setup():
        import jax, jax.numpy as jnp
        import numpy as np
        NUM_HEADS = 16
        TOP_K = 2
        ROPE_BASE = 10000.0
        LN_EPS = 1e-05

        def _rope_sin_cos(S, D, dtype):
            inv_freq = 1.0 / ROPE_BASE ** (jnp.arange(0, D, 2, dtype=jnp.float32) / D)
            freqs = jnp.arange(S, dtype=jnp.float32)[:, None] * inv_freq[None, :]
            sin = jnp.sin(freqs).astype(dtype)[None, :, None, :]
            cos = jnp.cos(freqs).astype(dtype)[None, :, None, :]
            return (sin, cos)

        def _apply_rope(x, sin, cos):
            x1, x2 = (x[..., 0::2], x[..., 1::2])
            r1 = x1 * cos - x2 * sin
            r2 = x1 * sin + x2 * cos
            return jnp.stack([r1, r2], axis=-1).reshape(x.shape)

        def _layer_norm(x, w, b):
            mu = jnp.mean(x, axis=-1, keepdims=True)
            var = jnp.mean(jnp.square(x - mu), axis=-1, keepdims=True)
            return (x - mu) * jax.lax.rsqrt(var + LN_EPS) * w + b
        key = jax.random.key(seed)
        ks = jax.random.split(key, 8)
        B, S, E, NE = (2, 256, 128, 8)
        s = 0.02
        return {'x': jax.random.normal(ks[0], (B, S, E), dtype=jnp.float32), 'in_proj_w': jax.random.normal(ks[1], (3 * E, E), dtype=jnp.float32) * s, 'in_proj_b': jnp.zeros((3 * E,), dtype=jnp.float32), 'out_proj_w': jax.random.normal(ks[2], (E, E), dtype=jnp.float32) * s, 'out_proj_b': jnp.zeros((E,), dtype=jnp.float32), 'gate_w': jax.random.normal(ks[3], (NE, E), dtype=jnp.float32) * s, 'gate_b': jnp.zeros((NE,), dtype=jnp.float32), 'expert_w': jax.random.normal(ks[4], (NE, E, E), dtype=jnp.float32) * s, 'expert_b': jnp.zeros((NE, E), dtype=jnp.float32), 'ln1_w': jnp.ones((E,), dtype=jnp.float32), 'ln1_b': jnp.zeros((E,), dtype=jnp.float32), 'ln2_w': jnp.ones((E,), dtype=jnp.float32), 'ln2_b': jnp.zeros((E,), dtype=jnp.float32)}
    _L0_ffn_all = _L0_ffn_setup()
    _L0_ffn_in = {k: v for k, v in _L0_ffn_all.items() if k in ('in_proj_w', 'in_proj_b', 'out_proj_w', 'out_proj_b', 'gate_w', 'gate_b', 'expert_w', 'expert_b', 'ln1_w', 'ln1_b', 'ln2_w', 'ln2_b')}
    del _L0_ffn_all

    def _L1_xattn_setup():
        import jax, jax.numpy as jnp
        import numpy as np
        N_HEAD, DIM, D_K, D_V = (16, 128, 64, 64)
        B, L = (4, 256)
        key = jax.random.key(seed)
        ks = jax.random.split(key, 8)

        def xavier(k, shape, fan_in, fan_out):
            std = float(np.sqrt(2.0 / (fan_in + fan_out)))
            return jax.random.normal(k, shape, dtype=jnp.float32) * std
        return {'q': jax.random.normal(ks[0], (B, L, DIM), dtype=jnp.float32), 'k': jax.random.normal(ks[1], (B, L, DIM), dtype=jnp.float32), 'v': jax.random.normal(ks[2], (B, L, DIM), dtype=jnp.float32), 'w_q': xavier(ks[3], (N_HEAD, DIM, D_K), DIM, D_K), 'w_k': xavier(ks[4], (N_HEAD, DIM, D_K), DIM, D_K), 'w_v': xavier(ks[5], (N_HEAD, DIM, D_V), DIM, D_V), 'proj_w': xavier(ks[6], (DIM, N_HEAD * D_V), N_HEAD * D_V, DIM), 'proj_b': jnp.zeros((DIM,), dtype=jnp.float32)}
    _L1_xattn_all = _L1_xattn_setup()
    _L1_xattn_in = {k: v for k, v in _L1_xattn_all.items() if k in ('w_q', 'w_k', 'w_v', 'proj_w', 'proj_b')}
    del _L1_xattn_all

    def _L1_attn_setup():
        import jax, jax.numpy as jnp
        import numpy as np
        DIM = 128
        HEADS = 16
        HEAD_DIM = DIM // HEADS
        B, N = (4, 512)

        def _reference_tuple_inner(x, Wq, bq, Wk, bk, Wv, bv, Wo, bo, stdp):
            b, n, d = x.shape
            h, dh = (HEADS, HEAD_DIM)

            def proj(W, bias):
                return (x @ W.T + bias).reshape(b, n, h, dh).transpose(0, 2, 1, 3)
            Q = jax.nn.elu(proj(Wq, bq)) + 1.0
            K = jax.nn.elu(proj(Wk, bk)) + 1.0
            V = proj(Wv, bv)
            stdp_w = jax.nn.sigmoid(stdp).reshape(1, h, 1, 1)
            KV = jnp.einsum('bhnd,bhnv->bhdv', K, V)
            K_sum = K.sum(axis=2)
            numerator = jnp.einsum('bhnd,bhdv->bhnv', Q, KV)
            denominator = jnp.einsum('bhnd,bhd->bhn', Q, K_sum)[..., None] + 1e-06
            attn_out = numerator / denominator * stdp_w
            out = attn_out.transpose(0, 2, 1, 3).reshape(b, n, d)
            out = out @ Wo.T + bo
            return (out, jax.lax.stop_gradient(stdp))
        key = jax.random.key(seed)
        ks = jax.random.split(key, 10)
        s = 1.0 / np.sqrt(DIM)
        return {'x': jax.random.normal(ks[0], (B, N, DIM), dtype=jnp.float32), 'Wq': jax.random.uniform(ks[1], (DIM, DIM), jnp.float32, -s, s), 'bq': jax.random.uniform(ks[2], (DIM,), jnp.float32, -s, s), 'Wk': jax.random.uniform(ks[3], (DIM, DIM), jnp.float32, -s, s), 'bk': jax.random.uniform(ks[4], (DIM,), jnp.float32, -s, s), 'Wv': jax.random.uniform(ks[5], (DIM, DIM), jnp.float32, -s, s), 'bv': jax.random.uniform(ks[6], (DIM,), jnp.float32, -s, s), 'Wo': jax.random.uniform(ks[7], (DIM, DIM), jnp.float32, -s, s), 'bo': jax.random.uniform(ks[8], (DIM,), jnp.float32, -s, s), 'stdp': jnp.ones((HEADS,), dtype=jnp.float32)}
    _L1_attn_all = _L1_attn_setup()
    _L1_attn_in = {k: v for k, v in _L1_attn_all.items() if k in ('Wq', 'bq', 'Wk', 'bk', 'Wv', 'bv', 'Wo', 'bo', 'stdp')}
    del _L1_attn_all

    def _L1_ffn_setup():
        import jax, jax.numpy as jnp
        import numpy as np
        E, K, D = (8, 2, 128)
        B, S = (2, 512)

        def _layernorm(x, g, b, eps=1e-06):
            m = jnp.mean(x, axis=-1, keepdims=True)
            v = jnp.var(x, axis=-1, keepdims=True)
            return (x - m) * jax.lax.rsqrt(v + eps) * g + b
        key = jax.random.key(seed)
        ks = jax.random.split(key, 6)
        n = lambda k, shape, scale: jax.random.normal(k, shape, jnp.float32) * scale
        return {'x': n(ks[0], (B, S, D), 1.0), 'gate_w': n(ks[1], (D, E), 0.02), 'w1': n(ks[2], (E, D, 2 * D), 0.02), 'b1': jnp.zeros((E, 2 * D), jnp.float32), 'w2': n(ks[3], (E, 2 * D, D), 0.02), 'b2': jnp.zeros((E, D), jnp.float32), 'ln_g': jnp.ones((E, D), jnp.float32), 'ln_b': jnp.zeros((E, D), jnp.float32)}
    _L1_ffn_all = _L1_ffn_setup()
    _L1_ffn_in = {k: v for k, v in _L1_ffn_all.items() if k in ('gate_w', 'w1', 'b1', 'w2', 'b2', 'ln_g', 'ln_b')}
    del _L1_ffn_all
    return {'x': x, 'ctx_1024': ctx_1024, 'L0_xattn_Wk': _L0_xattn_in['Wk'], 'L0_xattn_Wv': _L0_xattn_in['Wv'], 'L0_xattn_bv': _L0_xattn_in['bv'], 'L0_xattn_Wq': _L0_xattn_in['Wq'], 'L0_xattn_bq': _L0_xattn_in['bq'], 'L0_xattn_Wo': _L0_xattn_in['Wo'], 'L0_xattn_bo': _L0_xattn_in['bo'], 'L0_attn_Wq': _L0_attn_in['Wq'], 'L0_attn_bq': _L0_attn_in['bq'], 'L0_attn_Wk': _L0_attn_in['Wk'], 'L0_attn_bk': _L0_attn_in['bk'], 'L0_attn_Wv': _L0_attn_in['Wv'], 'L0_attn_bv': _L0_attn_in['bv'], 'L0_attn_gamma': _L0_attn_in['gamma'], 'L0_attn_beta': _L0_attn_in['beta'], 'L0_ffn_in_proj_w': _L0_ffn_in['in_proj_w'], 'L0_ffn_in_proj_b': _L0_ffn_in['in_proj_b'], 'L0_ffn_out_proj_w': _L0_ffn_in['out_proj_w'], 'L0_ffn_out_proj_b': _L0_ffn_in['out_proj_b'], 'L0_ffn_gate_w': _L0_ffn_in['gate_w'], 'L0_ffn_gate_b': _L0_ffn_in['gate_b'], 'L0_ffn_expert_w': _L0_ffn_in['expert_w'], 'L0_ffn_expert_b': _L0_ffn_in['expert_b'], 'L0_ffn_ln1_w': _L0_ffn_in['ln1_w'], 'L0_ffn_ln1_b': _L0_ffn_in['ln1_b'], 'L0_ffn_ln2_w': _L0_ffn_in['ln2_w'], 'L0_ffn_ln2_b': _L0_ffn_in['ln2_b'], 'L1_xattn_w_q': _L1_xattn_in['w_q'], 'L1_xattn_w_k': _L1_xattn_in['w_k'], 'L1_xattn_w_v': _L1_xattn_in['w_v'], 'L1_xattn_proj_w': _L1_xattn_in['proj_w'], 'L1_xattn_proj_b': _L1_xattn_in['proj_b'], 'L1_attn_Wq': _L1_attn_in['Wq'], 'L1_attn_bq': _L1_attn_in['bq'], 'L1_attn_Wk': _L1_attn_in['Wk'], 'L1_attn_bk': _L1_attn_in['bk'], 'L1_attn_Wv': _L1_attn_in['Wv'], 'L1_attn_bv': _L1_attn_in['bv'], 'L1_attn_Wo': _L1_attn_in['Wo'], 'L1_attn_bo': _L1_attn_in['bo'], 'L1_attn_stdp': _L1_attn_in['stdp'], 'L1_ffn_gate_w': _L1_ffn_in['gate_w'], 'L1_ffn_w1': _L1_ffn_in['w1'], 'L1_ffn_b1': _L1_ffn_in['b1'], 'L1_ffn_w2': _L1_ffn_in['w2'], 'L1_ffn_b2': _L1_ffn_in['b2'], 'L1_ffn_ln_g': _L1_ffn_in['ln_g'], 'L1_ffn_ln_b': _L1_ffn_in['ln_b']}

def reference(x, ctx_1024, L0_xattn_Wk, L0_xattn_Wv, L0_xattn_bv, L0_xattn_Wq, L0_xattn_bq, L0_xattn_Wo, L0_xattn_bo, L0_attn_Wq, L0_attn_bq, L0_attn_Wk, L0_attn_bk, L0_attn_Wv, L0_attn_bv, L0_attn_gamma, L0_attn_beta, L0_ffn_in_proj_w, L0_ffn_in_proj_b, L0_ffn_out_proj_w, L0_ffn_out_proj_b, L0_ffn_gate_w, L0_ffn_gate_b, L0_ffn_expert_w, L0_ffn_expert_b, L0_ffn_ln1_w, L0_ffn_ln1_b, L0_ffn_ln2_w, L0_ffn_ln2_b, L1_xattn_w_q, L1_xattn_w_k, L1_xattn_w_v, L1_xattn_proj_w, L1_xattn_proj_b, L1_attn_Wq, L1_attn_bq, L1_attn_Wk, L1_attn_bk, L1_attn_Wv, L1_attn_bv, L1_attn_Wo, L1_attn_bo, L1_attn_stdp, L1_ffn_gate_w, L1_ffn_w1, L1_ffn_b1, L1_ffn_w2, L1_ffn_b2, L1_ffn_ln_g, L1_ffn_ln_b):
    import jax
    import jax.numpy as jnp

    def _L0_xattn_ref(k, v, q, Wk, Wv, bv, Wq, bq, Wo, bo):
        import jax, jax.numpy as jnp
        import numpy as np
        D_MODEL = 128
        B, S = (4, 256)
        kp = jnp.einsum('bsd,ed->bse', k, Wk)
        vp = jnp.einsum('bsd,ed->bse', v, Wv) + bv
        qp = jnp.einsum('bsd,ed->bse', q, Wq) + bq
        scale = 1.0 / jnp.sqrt(jnp.float32(kp.shape[-1]))
        scores = jnp.einsum('bqd,bkd->bqk', qp, kp) * scale
        probs = jax.nn.softmax(scores, axis=-1)
        ctx = jnp.einsum('bqk,bkd->bqd', probs, vp)
        return jnp.einsum('bqd,ed->bqe', ctx, Wo) + bo

    def _L0_attn_ref(x, Wq, bq, Wk, bk, Wv, bv, gamma, beta):
        import jax, jax.numpy as jnp
        import numpy as np
        H = 8
        LN_EPS = 1e-05
        B, S, D = x.shape
        dk = D // H
        mu = jnp.mean(x, axis=-1, keepdims=True)
        var = jnp.mean(jnp.square(x - mu), axis=-1, keepdims=True)
        xn = (x - mu) * jax.lax.rsqrt(var + LN_EPS) * gamma + beta
        q = (xn @ Wq + bq).reshape(B, S, H, dk).transpose(0, 2, 1, 3)
        k = (xn @ Wk + bk).reshape(B, S, H, dk).transpose(0, 2, 1, 3)
        v = (xn @ Wv + bv).reshape(B, S, H, D).transpose(0, 2, 1, 3)
        scores = jnp.einsum('bhsd,bhtd->bhst', q, k) / jnp.sqrt(jnp.asarray(dk, x.dtype))
        p = jax.nn.softmax(scores, axis=-1)
        att = jnp.einsum('bhst,bhtd->bhsd', p, v)
        out = att.reshape(S, B, D, H).sum(axis=-1).reshape(B, S, D)
        return out

    def _L0_ffn_ref(x, in_proj_w, in_proj_b, out_proj_w, out_proj_b, gate_w, gate_b, expert_w, expert_b, ln1_w, ln1_b, ln2_w, ln2_b):
        import jax, jax.numpy as jnp
        import numpy as np
        NUM_HEADS = 16
        TOP_K = 2
        ROPE_BASE = 10000.0
        LN_EPS = 1e-05

        def _rope_sin_cos(S, D, dtype):
            inv_freq = 1.0 / ROPE_BASE ** (jnp.arange(0, D, 2, dtype=jnp.float32) / D)
            freqs = jnp.arange(S, dtype=jnp.float32)[:, None] * inv_freq[None, :]
            sin = jnp.sin(freqs).astype(dtype)[None, :, None, :]
            cos = jnp.cos(freqs).astype(dtype)[None, :, None, :]
            return (sin, cos)

        def _apply_rope(x, sin, cos):
            x1, x2 = (x[..., 0::2], x[..., 1::2])
            r1 = x1 * cos - x2 * sin
            r2 = x1 * sin + x2 * cos
            return jnp.stack([r1, r2], axis=-1).reshape(x.shape)

        def _layer_norm(x, w, b):
            mu = jnp.mean(x, axis=-1, keepdims=True)
            var = jnp.mean(jnp.square(x - mu), axis=-1, keepdims=True)
            return (x - mu) * jax.lax.rsqrt(var + LN_EPS) * w + b
        B, S, E = x.shape
        H = NUM_HEADS
        D = E // H
        xh = x.reshape(B, S, H, D)
        sin, cos = _rope_sin_cos(S, D, x.dtype)
        q_in = _apply_rope(xh, sin, cos).reshape(B, S, E)
        k_in = q_in
        v_in = x
        Wq, Wk, Wv = jnp.split(in_proj_w, 3, axis=0)
        bq, bk, bv = jnp.split(in_proj_b, 3, axis=0)
        q = (q_in @ Wq.T + bq).reshape(B, S, H, D)
        k = (k_in @ Wk.T + bk).reshape(B, S, H, D)
        v = (v_in @ Wv.T + bv).reshape(B, S, H, D)
        scale = 1.0 / jnp.sqrt(jnp.asarray(D, dtype=x.dtype))
        scores = jnp.einsum('bqhd,bkhd->bhqk', q, k) * scale
        causal = jnp.tril(jnp.ones((S, S), dtype=bool))
        scores = jnp.where(causal[None, None], scores, jnp.asarray(-jnp.inf, dtype=scores.dtype))
        attn = jax.nn.softmax(scores, axis=-1)
        ctx = jnp.einsum('bhqk,bkhd->bqhd', attn, v).reshape(B, S, E)
        attn_out = ctx @ out_proj_w.T + out_proj_b
        x1 = _layer_norm(x + attn_out, ln1_w, ln1_b)
        gates = jax.nn.softmax(x1 @ gate_w.T + gate_b, axis=-1)
        _, top_idx = jax.lax.top_k(gates, TOP_K)
        top_gates = jnp.take_along_axis(gates, top_idx, axis=-1)
        expert_outputs = jnp.einsum('bsd,efd->bsef', x1, expert_w) + expert_b[None, None]
        sel = jnp.take_along_axis(expert_outputs, top_idx[..., None], axis=2)
        moe_out = jnp.sum(sel * top_gates[..., None], axis=2)
        return _layer_norm(x1 + moe_out, ln2_w, ln2_b)

    def _L1_xattn_ref(q, k, v, w_q, w_k, w_v, proj_w, proj_b):
        import jax, jax.numpy as jnp
        import numpy as np
        N_HEAD, DIM, D_K, D_V = (16, 128, 64, 64)
        B, L = (4, 256)
        batch, len_q, dim = q.shape
        scale = jnp.asarray(np.sqrt(dim), dtype=q.dtype)
        qh = jnp.einsum('bqd,hdk->hbqk', q, w_q)
        kh = jnp.einsum('bsd,hdk->hbsk', k, w_k)
        vh = jnp.einsum('bsd,hdv->hbsv', v, w_v)
        scores = jnp.einsum('hbqk,hbsk->hbqs', qh, kh) / scale
        attn = jax.nn.softmax(scores, axis=-1)
        out = jnp.einsum('hbqs,hbsv->hbqv', attn, vh)
        out = jnp.transpose(out, (1, 2, 0, 3)).reshape(batch, len_q, -1)
        return out @ proj_w.T + proj_b

    def _L1_attn_ref(x, Wq, bq, Wk, bk, Wv, bv, Wo, bo, stdp):
        import jax, jax.numpy as jnp
        import numpy as np
        DIM = 128
        HEADS = 16
        HEAD_DIM = DIM // HEADS
        B, N = (4, 512)

        def _reference_tuple_inner(x, Wq, bq, Wk, bk, Wv, bv, Wo, bo, stdp):
            b, n, d = x.shape
            h, dh = (HEADS, HEAD_DIM)

            def proj(W, bias):
                return (x @ W.T + bias).reshape(b, n, h, dh).transpose(0, 2, 1, 3)
            Q = jax.nn.elu(proj(Wq, bq)) + 1.0
            K = jax.nn.elu(proj(Wk, bk)) + 1.0
            V = proj(Wv, bv)
            stdp_w = jax.nn.sigmoid(stdp).reshape(1, h, 1, 1)
            KV = jnp.einsum('bhnd,bhnv->bhdv', K, V)
            K_sum = K.sum(axis=2)
            numerator = jnp.einsum('bhnd,bhdv->bhnv', Q, KV)
            denominator = jnp.einsum('bhnd,bhd->bhn', Q, K_sum)[..., None] + 1e-06
            attn_out = numerator / denominator * stdp_w
            out = attn_out.transpose(0, 2, 1, 3).reshape(b, n, d)
            out = out @ Wo.T + bo
            return (out, jax.lax.stop_gradient(stdp))
        return _reference_tuple_inner(x, Wq, bq, Wk, bk, Wv, bv, Wo, bo, stdp)[0]

    def _L1_ffn_ref(x, gate_w, w1, b1, w2, b2, ln_g, ln_b):
        import jax, jax.numpy as jnp
        import numpy as np
        E, K, D = (8, 2, 128)
        B, S = (2, 512)

        def _layernorm(x, g, b, eps=1e-06):
            m = jnp.mean(x, axis=-1, keepdims=True)
            v = jnp.var(x, axis=-1, keepdims=True)
            return (x - m) * jax.lax.rsqrt(v + eps) * g + b
        orig_shape = x.shape
        xt = x.reshape(-1, orig_shape[-1])
        scores = xt @ gate_w
        ew, ei = jax.lax.top_k(scores, K)
        ew = jax.nn.softmax(ew, axis=-1)
        mask = ei[None, :, :] == jnp.arange(E)[:, None, None]
        wE = jnp.sum(ew[None, :, :] * mask, axis=-1)
        h = jax.nn.gelu(jnp.einsum('td,edf->etf', xt, w1) + b1[:, None, :], approximate=False)
        o = jnp.einsum('etf,efd->etd', h, w2) + b2[:, None, :]
        y = _layernorm(xt[None, :, :] + o, ln_g[:, None, :], ln_b[:, None, :])
        out = jnp.einsum('et,etd->td', wE, y)
        return out.reshape(orig_shape)
    x = x + _L0_xattn_ref(ctx_1024, ctx_1024, _layernorm(x, axis=-1), L0_xattn_Wk, L0_xattn_Wv, L0_xattn_bv, L0_xattn_Wq, L0_xattn_bq, L0_xattn_Wo, L0_xattn_bo)
    x = x + _L0_attn_ref(_layernorm(x, axis=-1), L0_attn_Wq, L0_attn_bq, L0_attn_Wk, L0_attn_bk, L0_attn_Wv, L0_attn_bv, L0_attn_gamma, L0_attn_beta)
    x = x + _L0_ffn_ref(_layernorm(x, axis=-1), L0_ffn_in_proj_w, L0_ffn_in_proj_b, L0_ffn_out_proj_w, L0_ffn_out_proj_b, L0_ffn_gate_w, L0_ffn_gate_b, L0_ffn_expert_w, L0_ffn_expert_b, L0_ffn_ln1_w, L0_ffn_ln1_b, L0_ffn_ln2_w, L0_ffn_ln2_b)
    x = x + _L1_xattn_ref(_layernorm(x, axis=-1), ctx_1024, ctx_1024, L1_xattn_w_q, L1_xattn_w_k, L1_xattn_w_v, L1_xattn_proj_w, L1_xattn_proj_b)
    x = x + _L1_attn_ref(_layernorm(x, axis=-1), L1_attn_Wq, L1_attn_bq, L1_attn_Wk, L1_attn_bk, L1_attn_Wv, L1_attn_bv, L1_attn_Wo, L1_attn_bo, L1_attn_stdp)
    x = x + _L1_ffn_ref(_layernorm(x, axis=-1), L1_ffn_gate_w, L1_ffn_w1, L1_ffn_b1, L1_ffn_w2, L1_ffn_b2, L1_ffn_ln_g, L1_ffn_ln_b)
    return x

_drawn_inputs = setup_inputs


def setup_inputs(seed=0):
    import zlib

    import numpy as np

    out = dict(_drawn_inputs(seed))
    spreads = {'L0_xattn_bv': (0.0, 0.1),
     'L0_xattn_bq': (0.0, 0.1),
     'L0_xattn_bo': (0.0, 0.1),
     'L0_attn_bq': (0.0, 0.321),
     'L0_attn_bk': (0.0, 2.0),
     'L0_attn_bv': (0.0, 0.1),
     'L0_attn_gamma': (1.0, 0.2),
     'L0_attn_beta': (0.0, 0.1),
     'L0_ffn_in_proj_b': (0.0, 0.8),
     'L0_ffn_out_proj_b': (0.0, 0.1),
     'L0_ffn_gate_b': (0.0, 0.602),
     'L0_ffn_expert_b': (0.0, 0.8),
     'L0_ffn_ln1_w': (1.0, 0.2),
     'L0_ffn_ln1_b': (0.0, 0.1),
     'L0_ffn_ln2_w': (1.0, 0.2),
     'L0_ffn_ln2_b': (0.0, 0.1),
     'L1_xattn_proj_b': (0.0, 0.1),
     'L1_attn_stdp': (1.0, 0.6),
     'L1_ffn_b1': (0.0, 0.8),
     'L1_ffn_b2': (0.0, 1.15),
     'L1_ffn_ln_g': (1.0, 0.2),
     'L1_ffn_ln_b': (0.0, 0.438)}
    factors = {'L0_ffn_in_proj_w': 5.876,
     'L0_ffn_out_proj_w': 4.546,
     'L0_ffn_gate_w': 3.661,
     'L0_ffn_expert_w': 3.039,
     'L1_attn_Wq': 49.859,
     'L1_attn_bq': 64.0,
     'L1_attn_Wk': 8.0,
     'L1_attn_bk': 64.0,
     'L1_attn_bv': 7.421,
     'L1_attn_bo': 3.146,
     'L1_ffn_w1': 8.0,
     'L1_ffn_w2': 7.45}
    for name, (base, spread) in spreads.items():
        noise = np.random.default_rng([zlib.crc32(name.encode()), seed]).standard_normal(out[name].shape)
        drawn = base * np.exp(spread * noise) if base else spread * noise
        out[name] = jnp.asarray(drawn.astype(out[name].dtype))
    for name, factor in factors.items():
        out[name] = (out[name] * factor).astype(out[name].dtype)
    return out
```

```python
import math
import numpy as np
import concourse.bass as bass
from concourse import mybir
from contextlib import ExitStack

Q = 64
D = 128
KEYS = 6272
TILES = KEYS // D
CHUNK = 8
CHUNKS = TILES // CHUNK
H4 = 16
GROUP = 256
GROUPS = H4 * Q // GROUP
BLOCK = 4
E = 8

STEPS = {
    "vector_step": [
        "halfpow", "ones", "up16", "mv0", "bvrep", "xn1", "ident16", "a0", "b0", "xb1", "xnT1", "qk1", "max1",
        "shift1", "UT", "mv1", "xn2", "xd2", "kb2", "v2", "s2", "pt2", "turned", "mv2", "xf", "qin", "qinT",
        "kb3", "v3", "s3", "pt3", "att3", "attT3", "mv3", "y3", "y3T", "neg3", "moe3", "mv4", "x3", "mv5",
        "xn4", "xnT4", "mv6", "wo5", "xn5", "xnT5", "kmin5", "vv5", "qmin5", "k5", "q5", "kv5", "att5",
        "attT5", "mv7", "xt6", "xt6T", "d6", "w4_6", "mv6e", "o6c", "x6",
    ],
    "tensor_step": [
        "fold0", "fold0b", "xnT1_ps", "qk1_ps", "max1_row", "u1", "den1", "y1", "xnT2_ps", "k2_ps", "q2_ps",
        "v2_ps", "s2_ps", "pt2_ps", "att2_ps", "o2_ps", "xfT_ps", "qinT_ps", "k3_ps", "q3_ps", "s3_ps",
        "pt3_ps", "att3_ps", "att3T_ps", "proj3_ps", "y3T_ps", "lg3_ps", "exp3_ps", "z3b_ps", "xnT4_ps",
        "xnT5_ps", "kv5_ps", "q5_ps", "kvsum5_ps", "num5_ps", "att5T_ps", "o5_ps", "xt6T_ps", "lg6_ps",
        "o6_ps", "out6_ps",
    ],
}

CTX_UP = 64.0
QK_UP = 16.0
UP = CTX_UP * QK_UP
HEADROOM = 5.0
ROOT = math.sqrt(float(D))


def constants():
    p = np.arange(128)
    parts = {}
    parts["ident"] = np.eye(128)
    parts["fold"] = (p[:, None] % 64 == np.arange(64)[None])
    parts["half"] = (p[:, None] // 64 == np.arange(2)[None])
    parts["head_k2"] = ((p[:, None] // 16) % 4 == np.arange(4)[None])
    parts["head_k3"] = ((p[:, None] // 8) % 8 == np.arange(8)[None])
    parts["pair2"] = (p[:, None] // 64 == np.arange(8)[None] % 2)
    parts["pair3"] = (p[:, None] // 64 == np.arange(16)[None] % 2)
    own = np.zeros((128, 144))
    own[:, :128] = p[:, None] // 8 == p[None] // 8
    own[:, 128:] = p[:, None] // 8 == np.arange(16)[None]
    parts["own_head"] = own
    t = np.arange(64)
    parts["causal"] = np.where(t[None] <= (p[:, None] % 64), 0.0, -1e30)
    parts["iota8"] = np.tile(np.arange(8), (128, 1))
    halfrows = np.zeros((128, 128))
    halfrows[0, :64] = 1
    halfrows[1, 64:] = 1
    parts["halfrows"] = halfrows
    dup = np.zeros((128, 128))
    dup[:64] = np.concatenate([np.eye(64), np.eye(64)], 1)
    parts["dup"] = dup
    inv = (1.0 / np.float32(10000.0) ** (np.arange(0, 8, 2, dtype=np.float32) / np.float32(8))).astype(np.float32)
    f = (t.astype(np.float32)[:, None] * inv[None]).astype(np.float32)
    cos, sin = np.zeros((128, 128)), np.zeros((128, 128))
    cos[:64] = np.tile(np.repeat(np.cos(f), 2, axis=1), (1, 16))
    sin[:64] = np.tile(np.stack([-np.sin(f), np.sin(f)], -1).reshape(64, 8), (1, 16))
    parts["cos"], parts["sin"] = cos, sin
    turn = np.zeros((128, 8))
    turn[:64] = t[:, None] % 8 == np.arange(8)[None]
    parts["turn"] = turn
    pick = np.zeros((128, 8, 64))
    for s in range(64):
        for h in range(8):
            pick[s, h, h * 8 + s // 8] = 1
    parts["pick"] = pick.reshape(128, 512)
    at, where = 0, {}
    for name, a in parts.items():
        where[name] = (at, at + a.shape[1])
        at += a.shape[1]
    return np.ascontiguousarray(np.concatenate(list(parts.values()), 1).astype(np.float32)), where


CONST, AT = constants()
EARLY = AT["half"][0]

COLS = ["L0_xattn_bq", "L0_xattn_bv", "L0_attn_gamma", "L0_attn_beta", "L0_attn_bq", "L0_attn_bk",
        "in_bq", "in_bk", "L1_attn_bq", "stdp"]
ROWS = {"L0_xattn_bo": 128, "L0_attn_bv": 1024, "in_bv": 128, "gate_b": 8, "L1_attn_bk": 128, "L1_attn_bv": 128}
WIDE = ["L0_ffn_out_proj_b", "L0_ffn_ln1_w", "L0_ffn_ln1_b", "L0_ffn_ln2_w", "L0_ffn_ln2_b",
        "L1_xattn_proj_b", "L1_attn_bo"]


def build(nc, t, out, debug=None):
    f32, f16, u32 = mybir.dt.float32, mybir.dt.float16, mybir.dt.uint32
    ALU = mybir.AluOpType
    ACT = mybir.ActivationFunctionType
    AX = mybir.AxisListType.X

    with ExitStack() as ctx:
        def sb(name, shape, dt=f32):
            return ctx.enter_context(nc.sbuf_tensor(name, shape, dt))

        sems = {}

        def sig(name):
            if name not in sems:
                sems[name] = ctx.enter_context(nc.semaphore(name))
            return sems[name]

        made = {name: 0 for name in STEPS}

        def counter(name):
            return next(c for c, names in STEPS.items() if name in names)

        def step(name):
            c = counter(name)
            assert STEPS[c][made[c]] == name, (name, STEPS[c][made[c]])
            made[c] += 1
            return sig(c)

        def after(name):
            return sig(counter(name)), STEPS[counter(name)].index(name) + 1

        bank = [ctx.enter_context(nc.psum_tensor(f"bank{i}", [128, 512], f32)) for i in range(8)]

        const = sb("const", list(CONST.shape))

        def k(name, rows=128):
            a, b = AT[name]
            return const[0:rows, a:b]

        ident = k("ident")
        x0 = sb("x0", [64, D])
        cols = sb("cols", [128, len(COLS)])
        rows = sb("rows", [1, sum(ROWS.values())])
        wide = sb("wide", [64, len(WIDE), D])

        def col(name):
            return cols[:, COLS.index(name):COLS.index(name) + 1]

        def row(name):
            names = list(ROWS)
            a = sum(ROWS[n] for n in names[:names.index(name)])
            return rows[0:1, a:a + ROWS[name]]

        def spread(name):
            return wide[:, WIDE.index(name), :]

        w0 = sb("w0", [128, 4, D])
        w2 = sb("w2", [128, 2, D])
        wv2 = sb("wv2", [128, 1024])
        w3 = sb("w3", [128, 4, D])
        gate3 = sb("gate3", [128, E])
        ew3 = sb("ew3", [128, E * D])
        eb3 = sb("eb3", [2, 512])
        w4 = sb("w4", [128, 4, 8, D])
        wq4t, wk4t, wv4t, wp4t = (w4[:, i] for i in range(4))
        w5 = sb("w5", [128, 4, D])
        gate6 = sb("gate6", [128, E])
        w16 = sb("w16", [128, E, 256])
        w26 = sb("w26", [128, E, 2, D])
        b16 = sb("b16", [16, D])
        b26 = sb("b26", [2, 512])
        lng6 = sb("lng6", [128, 512])
        lnb6 = sb("lnb6", [128, 512])

        ctx32 = sb("ctx32", [128, 2, CHUNK, D])
        late = w26[:].rearrange("p (c e) f d -> p c (e f) d", c=2)
        chunk = [ctx32[:, 0], ctx32[:, 1], late[:, 0], late[:, 1]]
        ctx_hi = sb("ctx_hi", [128, TILES, D], f16)
        ctx_lo = sb("ctx_lo", [128, TILES, D], f16)
        ctxT_hi = sb("ctxT_hi", [128, TILES, D], f16)
        ctxT_lo = sb("ctxT_lo", [128, TILES, D], f16)
        ones = sb("ones", [128, 128])
        up16 = sb("up16", [128, 128], f16)
        halfpow = sb("halfpow", [128, 4])

        block = ctx.enter_context(nc.Block())

        xn = sb("xn", [64, D])
        stat = sb("stat", [64, 8, 6])
        mv = sb("mv", [64, 8, 2])
        tiny = sb("tiny", [64, 16])
        xb1 = sb("xb1", [64, D])
        a0 = sb("a0", [128, D])
        c0 = sb("c0", [128, 1])
        b0 = sb("b0", [128, D])
        bvrep = sb("bvrep", [128, 64])
        xnT = sb("xnT", [128, 64])
        qkf = sb("qkf", [128, 64])
        qk1_hi = sb("qk1_hi", [128, 64], f16)
        qk1_lo = sb("qk1_lo", [128, 64], f16)
        cm1 = sb("cm1", [128, 8])
        m1 = sb("m1", [128, 1])
        mrow1 = sb("mrow1", [1, 3, 64])
        r1_hi = sb("r1_hi", [1, 64], f16)
        r1_lo = sb("r1_lo", [1, 64], f16)
        prob = sb("prob", [128, 8192], f16)
        P_hi = prob[:, 0:3584].rearrange("p (b n) -> p b n", b=7)
        P_lo = prob[:, 3584:7168].rearrange("p (b n) -> p b n", b=7)
        ph4 = prob[:, 0:2048].rearrange("p (s n) -> p s n", s=2)
        pl4 = prob[:, 2048:4096].rearrange("p (s n) -> p s n", s=2)
        P = prob[:, 4096:8192].bitcast(f32).rearrange("p (s n) -> p s n", s=2)
        big = sb("big", [128, 2 * H4 * D])
        p1 = big[:, 0:3584].rearrange("p (b n) -> p b n", b=7)
        a4 = big[:, 0:2048].rearrange("p (h d) -> p h d", h=H4)
        v4 = big[:, 2048:4096].rearrange("p (h d) -> p h d", h=H4)
        acc = sb("acc", [128, 2, 1024])
        UT = sb("UT", [128, 64])
        rden1 = sb("rden1", [64, 1])
        x1 = sb("x1", [64, D])
        wvg = sb("wvg", [128, D])
        bvg = sb("bvg", [1, D])
        xd2 = sb("xd2", [128, 2, 64])
        bqh = sb("bqh", [128, 4])
        Q2 = sb("Q2", [128, 2, 64])
        KT2 = sb("KT2", [128, 64])
        Kb2 = P[:, 0, 0:256].rearrange("p (h t) -> p h t", h=4)
        V2 = sb("V2", [128, 8, 17])
        mx2 = sb("mx2", [128, 8])
        s2, s3, e2, e3 = (ctx32[:, i // 2, 4 * (i % 2):4 * (i % 2) + 4, :].rearrange("p t d -> p (t d)")
                          for i in range(4))
        PT2, PT3 = (acc[:, 1, 512 * i:512 * i + 512].rearrange("p (c q) -> p c q", c=4) for i in range(2))
        rd2 = sb("rd2", [64, 16])
        att2 = sb("att2", [64, D])
        turned = acc[0:64, 0, :].rearrange("p (h b g) -> p h b g", h=8, b=8)
        x2 = sb("x2", [64, D])
        xf = sb("xf", [64, D])
        rope_a = sb("rope_a", [64, D])
        rope_b = sb("rope_b", [64, D])
        qin = sb("qin", [64, D])
        qinT = sb("qinT", [128, 64])
        xfT = sb("xfT", [128, 2, 64])
        Q3 = sb("Q3", [128, 2, 64])
        KT3 = sb("KT3", [128, 64])
        Kb3 = P[:, 0, 512:1024].rearrange("p (h t) -> p h t", h=8)
        V3 = sb("V3", [128, 16, 9])
        mx3 = sb("mx3", [128, 8])
        rd3 = sb("rd3", [64, 16])
        att3 = sb("att3", [64, D])
        attT3 = sb("attT3", [128, 64])
        xfb = sb("xfb", [64, D])
        z3 = sb("z3", [64, D])
        za3 = sb("za3", [64, D])
        y3 = sb("y3", [64, D])
        y3T = sb("y3T", [128, 3, 64])
        lg3 = sb("lg3", [128, 8])
        top3 = sb("top3", [128, 8])
        idx3 = sb("idx3", [128, 8], u32)
        idf3 = sb("idf3", [128, 2])
        neg3 = sb("neg3", [128, 1])
        eg3 = sb("eg3", [128, 8])
        sum3 = sb("sum3", [128, 2])
        hot3 = sb("hot3", [128, 3, 8])
        w4_3 = sb("w4_3", [128, 2, 4])
        moe3 = P[:, 1, 0:512].rearrange("p (e f) -> p e f", e=4)
        zb3 = sb("zb3", [64, D])
        x2b = sb("x2b", [64, D])
        x3 = sb("x3", [64, D])
        xnT4 = sb("xnT4", [128, 64])
        qk_hi = sb("qk_hi", [128, H4 * Q], f16)
        qk_lo = sb("qk_lo", [128, H4 * Q], f16)
        cm = sb("cm", [128, 2, 16])
        m4 = sb("m4", [128, 3, 2])
        shiftcols = sb("shiftcols", [128, 2, 64], f16)
        shiftrows = sb("shiftrows", [64, 2, GROUP], f16)
        rden4 = sb("rden4", [128, GROUP])
        un4 = sb("un4", [128, GROUP])
        ident16 = sb("ident16", [128, 128], f16)
        x3b = sb("x3b", [64, D])
        x4 = sb("x4", [64, D])
        wo5 = sb("wo5", [128, D])
        gate5 = sb("gate5", [128, 4])
        tq5 = sb("tq5", [128, 3, 64])
        q5 = sb("q5", [128, 64])
        tk5 = sb("tk5", [64, 2, D])
        k5 = sb("k5", [64, D])
        vv5 = sb("vv5", [64, 144])
        kv5 = sb("kv5", [128, 144])
        dn5 = sb("dn5", [64, 2, 16])
        att5 = sb("att5", [64, D])
        attT5 = sb("attT5", [128, 64])
        xnT5 = sb("xnT5", [128, 64])
        x4b = sb("x4b", [64, D])
        x5 = sb("x5", [64, D])
        xt6 = sb("xt6", [64, D])
        xt6T = sb("xt6T", [128, 3, 64])
        hz6 = w4[:, 0:2].rearrange("p i h d -> p (i h) d")
        o6 = w4[:, 2:4].rearrange("p i (j h) d -> p (i j) h d", j=2)
        lg6 = sb("lg6", [128, 8])
        top6 = sb("top6", [128, 8])
        idx6 = sb("idx6", [128, 8], u32)
        idf6 = sb("idf6", [128, 2])
        d6 = sb("d6", [128, 5])
        hot6 = sb("hot6", [128, 3, 8])
        w4_6 = sb("w4_6", [128, 3, 4])
        st6 = sb("st6", [128, 4, 6])
        mv6 = sb("mv6", [128, 4, 2])
        ve6 = sb("ve6", [128, 2, 4])
        o6a, o6b, o6c, wb6 = (o6[:, i] for i in range(4))
        x6 = sb("x6", [64, D])

        def over(ap, n):
            return ap.unsqueeze(1).broadcast_to([ap.shape[0], n, ap.shape[1]])

        def each(ap, n):
            return ap.unsqueeze(2).broadcast_to([ap.shape[0], ap.shape[1], n])

        @block.sync
        def _(sp):
            def load(dst, name, ready):
                sp.dma_start(dst, t[name]).then_inc(sig(ready), 16)

            sp.dma_start(x0[:], t["x"]).then_inc(sig("x_loaded"), 16)
            sp.dma_start(const[:, 0:EARLY], t["const"][:, 0:EARLY]).then_inc(sig("ident_loaded"), 16)
            load(cols[:], "cols", "w0_loaded")
            load(w0[:], "w0", "w0_loaded")
            load(rows[:], "rows", "w0_loaded")
            view = t["ctx"].rearrange("(p t) d -> p t d", t=TILES)
            for c in range(CHUNKS + 1):
                n = CHUNK if c < CHUNKS else TILES - CHUNK * CHUNKS
                if c >= 4:
                    sp.wait_ge(sig("chunk_half_transposed"), 2 * (c - 3))
                    sp.wait_ge(sig("chunk_lo"), c - 3)
                sp.dma_start(chunk[c % 4][:, 0:n, :], view[:, CHUNK * c:CHUNK * c + n, :]).then_inc(
                    sig(f"ctx_loaded{c % 4}"), 16)
            sp.dma_start(const[:, EARLY:], t["const"][:, EARLY:]).then_inc(sig("const_loaded"), 16)
            load(w2[:], "w2", "w2_loaded")
            load(wv2[:], "L0_attn_Wv", "w2_loaded")
            load(wide[:], "wide", "w3_loaded")
            load(w3[:], "w3", "w3_loaded")
            load(gate3[:], "gate3", "w3_loaded")
            load(ew3[:], "ew3", "w3_loaded")
            load(eb3[:], "eb3", "w3_loaded")
            load(wq4t[:], "wq4t", "w4_loaded")
            load(wk4t[:], "wk4t", "w4_loaded")
            load(wv4t[:], "wv4t", "w4_loaded")
            load(wp4t[:], "wp4t", "w4_loaded")
            load(w5[:], "w5", "w5_loaded")
            load(gate6[:], "L1_ffn_gate_w", "w6_loaded")
            load(w16[:], "w16", "w6_loaded")
            sp.wait_ge(sig("chunk_half_transposed"), 2 * CHUNKS + 1)
            sp.wait_ge(sig("chunk_lo"), CHUNKS + 1)
            load(w26[:], "w26", "w6_loaded")
            load(b16[:], "b16", "w6_loaded")
            load(b26[:], "b26", "w6_loaded")
            for half in range(2):
                for dst, name in ((lng6, "lng6"), (lnb6, "lnb6")):
                    sp.dma_start(dst[64 * half:64 * half + 64, :],
                                 t[name][half:half + 1, :].broadcast_to([64, 512])).then_inc(sig("w6_loaded"), 16)
            n = 1
            sp.wait_ge(*after("x6"))
            sp.dma_start(out, x6[:]).then_inc(sig("stored"), 16)
            if debug is not None:
                for i, v in enumerate([x1, x2, x3, x4, x5]):
                    sp.dma_start(debug[i], v[:]).then_inc(sig("stored"), 16)
                    n += 1
            sp.wait_ge(sig("stored"), 16 * n)

        @block.vector
        def _(dve):
            v = nc.vector
            count = [0]

            def own(ins):
                count[0] += 1
                ins.then_inc(sig("dve_own"), 1)
                dve.wait_ge(sig("dve_own"), count[0])

            def moments(src, s, name):
                own(v.bn_stats(stat[:, s, :], src))
                v.bn_aggr(mv[:, s, :], stat[:, s, :]).then_inc(step(name), 1)

            def normed(dst, src, s, scale, name):
                v.tensor_scalar(dst, src, mv[:, s, 0:1], scale, ALU.subtract, ALU.mult).then_inc(step(name), 1)

            v.memset(halfpow[:], -0.5).then_inc(step("halfpow"), 1)
            v.memset(ones[:], 1.0).then_inc(step("ones"), 1)
            v.memset(up16[:], UP).then_inc(step("up16"), 1)
            own(v.memset(cm1[:], -3.0e38))
            v.memset(y3T[:], 0.0).then_inc(sig("zeros"), 1)
            v.memset(xt6T[:], 0.0).then_inc(sig("zeros"), 1)
            v.memset(shiftcols[:], 0.0).then_inc(sig("zeros"), 1)
            own(v.memset(vv5[:], 1.0))

            dve.wait_ge(sig("x_loaded"), 16)
            moments(x0[:], 0, "mv0")
            dve.wait_ge(sig("w0_loaded"), 48)
            v.tensor_copy(bvrep[:], col("L0_xattn_bv").broadcast_to([128, 64])).then_inc(step("bvrep"), 1)
            dve.wait_ge(sig("rstd0"), 1)
            normed(xn[:], x0[:], 0, tiny[:, 0:1], "xn1")
            dve.wait_ge(sig("ident_loaded"), 16)
            v.tensor_copy(ident16[:], ident).then_inc(step("ident16"), 1)
            dve.wait_ge(*after("fold0"))
            v.tensor_copy(a0[:], bank[4][:, 0:128])
            v.tensor_copy(c0[:], bank[4][:, 128:129]).then_inc(step("a0"), 1)
            dve.wait_ge(*after("a0"))
            dve.wait_ge(*after("fold0b"))
            v.tensor_copy(b0[:], bank[5][:, 0:128]).then_inc(step("b0"), 1)
            v.tensor_tensor(xb1[:], x0[:], bank[5][0:64, 128:256], ALU.add).then_inc(step("xb1"), 1)
            dve.wait_ge(*after("xnT1_ps"))
            v.tensor_copy(xnT[:], bank[6][:, 0:64]).then_inc(step("xnT1"), 1)
            dve.wait_ge(*after("qk1_ps"))
            own(v.tensor_scalar(qkf[:], bank[7][:, 0:64], c0[:, 0:1], QK_UP, ALU.add, ALU.mult))
            own(v.tensor_copy(qk1_hi[:], qkf[:]))
            v.tensor_tensor(qk1_lo[:], qkf[:], qk1_hi[:], ALU.subtract).then_inc(step("qk1"), 1)

            def split_lo(c, n):
                for j in range(0, n, 4):
                    m = min(4, n - j)
                    b = bank[2 * (c % 2) + j // 4]
                    dve.wait_ge(sig("chunkT_hi"), 2 * c + j // 4 + 1)
                    v.scalar_tensor_tensor(
                        ctxT_lo[:, CHUNK * c + j:CHUNK * c + j + m, :].rearrange("p t k -> p (t k)"),
                        b[:, 0:128 * m], CTX_UP,
                        ctxT_hi[:, CHUNK * c + j:CHUNK * c + j + m, :].rearrange("p t k -> p (t k)"),
                        ALU.mult, ALU.subtract).then_inc(sig("chunkT_lo"), 1)

            for c in range(CHUNKS + 1):
                split_lo(c, CHUNK if c < CHUNKS else 1)
                dve.wait_ge(sig("scores1_hi"), c + 1)
                if c < CHUNKS:
                    ins = v.reduce_max(cm1[:, c:c + 1], bank[4 + c % 2][:], AX)
                else:
                    ins = v.reduce_max(cm1[0:64, c:c + 1], bank[4 + c % 2][0:64, 0:128], AX)
                ins.then_inc(sig("max1_part"), 1)
            dve.wait_ge(sig("max1_part"), CHUNKS + 1)
            v.reduce_max(m1[:], cm1[:], AX).then_inc(step("max1"), 1)
            dve.wait_ge(*after("max1_row"))
            own(v.reduce_max(mrow1[0:1, 0, :], bank[7][0:1, 0:128].rearrange("p (h q) -> p q h", h=2), AX))
            own(v.tensor_scalar(mrow1[0:1, 1, :], mrow1[0:1, 0, :], -1.0 / UP, HEADROOM * ROOT, ALU.mult, ALU.add))
            own(v.tensor_copy(r1_hi[:], mrow1[0:1, 1, :]))
            v.tensor_tensor(r1_lo[:], mrow1[0:1, 1, :], r1_hi[:], ALU.subtract).then_inc(step("shift1"), 1)
            for b in range(CHUNKS + 1):
                n = 512 if b < CHUNKS else 64
                dve.wait_ge(sig("prob1"), b + 1)
                v.tensor_tensor(P_lo[:, b, 0:n], p1[:, b, 0:n], P_hi[:, b, 0:n], ALU.subtract).then_inc(
                    sig("prob1_lo"), 1)
            dve.wait_ge(sig("w2_loaded"), 32)
            v.reduce_sum(wvg[:], wv2[:].rearrange("p (e j) -> p e j", j=8), AX).then_inc(sig("wvg"), 1)
            v.reduce_sum(bvg[:], row("L0_attn_bv").rearrange("p (e j) -> p e j", j=8), AX).then_inc(sig("wvg"), 1)
            dve.wait_ge(*after("u1"))
            v.tensor_copy(UT[:], bank[7][:, 0:64]).then_inc(step("UT"), 1)
            dve.wait_ge(*after("den1"))
            own(v.reciprocal(rden1[:], bank[1][0:64, 0:1]))
            dve.wait_ge(*after("y1"))
            own(v.scalar_tensor_tensor(x1[:], bank[0][0:64, 0:128], rden1[:, 0:1], xb1[:], ALU.mult, ALU.add))

            moments(x1[:], 1, "mv1")
            dve.wait_ge(sig("const_loaded"), 16)
            v.tensor_scalar(bqh[:, 0:2], k("half"), col("L0_attn_bq"), None, ALU.mult).then_inc(sig("bqh"), 1)
            v.tensor_scalar(bqh[:, 2:4], k("half"), col("in_bq"), None, ALU.mult).then_inc(sig("bqh"), 1)
            own(v.tensor_copy(V2[:, :, 16], k("pair2")))
            own(v.tensor_copy(V3[:, :, 8], k("pair3")))
            dve.wait_ge(sig("rstd1"), 1)
            normed(xn[:], x1[:], 1, tiny[:, 7:8], "xn2")
            dve.wait_ge(*after("xnT2_ps"))
            v.tensor_scalar(xd2[:], over(bank[0][:, 0:64], 2), col("L0_attn_gamma"), col("L0_attn_beta"),
                            ALU.mult, ALU.add).then_inc(step("xd2"), 1)
            dve.wait_ge(*after("k2_ps"))
            own(v.tensor_scalar(KT2[:], bank[2][:, 0:64], col("L0_attn_bk"), None, ALU.add))
            v.tensor_tensor(Kb2[:], over(KT2[:], 4), each(k("head_k2"), 64), ALU.mult).then_inc(step("kb2"), 1)
            dve.wait_ge(*after("v2_ps"))
            v.tensor_tensor(V2[:, :, 0:16], bank[3][:, 0:128].rearrange("p (h g) -> p h g", g=16),
                            each(k("pair2"), 16), ALU.mult).then_inc(step("v2"), 1)
            dve.wait_ge(*after("s2_ps"))
            sview = bank[4][:, 0:256].rearrange("p (h t) -> p h t", t=64)
            own(v.reduce_max(mx2[:, 0:4], sview, AX))
            v.tensor_tensor(s2[:, 0:256].rearrange("p (h t) -> p h t", t=64), sview, each(mx2[:, 0:4], 64),
                            ALU.subtract).then_inc(step("s2"), 1)
            dve.wait_ge(*after("pt2_ps"))
            v.tensor_copy(PT2[:, 0:2, :].rearrange("p c q -> p (c q)"), bank[0][:, 0:256]).then_inc(step("pt2"), 1)
            dve.wait_ge(*after("att2_ps"))
            attv = bank[1][0:64, 0:136].rearrange("p (h g) -> p h g", g=17)
            own(v.reciprocal(rd2[:, 0:8], attv[:, :, 16]))
            own(v.tensor_tensor(att2[:].rearrange("p (h g) -> p h g", g=16), attv[:, :, 0:16],
                                each(rd2[:, 0:8], 16), ALU.mult))
            for b in range(8):
                ins = v.tensor_scalar(turned[:, :, b, :], att2[:].rearrange("p (h g) -> p h g", g=16),
                                      k("turn", 64)[:, b:b + 1], None, ALU.mult)
            ins.then_inc(step("turned"), 1)
            dve.wait_ge(*after("o2_ps"))
            own(v.tensor_tensor(x2[:], x1[:], bank[2][0:64, 0:128], ALU.add))

            moments(x2[:], 2, "mv2")
            dve.wait_ge(sig("w3_loaded"), 80)
            dve.wait_ge(sig("rstd2"), 1)
            normed(xf[:], x2[:], 2, tiny[:, 9:10], "xf")
            dve.wait_ge(*after("xf"))
            pairs = xf[:].rearrange("p (i two) -> p i two", two=2)
            sin = k("sin", 64).rearrange("p (i two) -> p i two", two=2)
            rb = rope_b[:].rearrange("p (i two) -> p i two", two=2)
            v.tensor_tensor(rb[:, :, 0], pairs[:, :, 1], sin[:, :, 0], ALU.mult)
            own(v.tensor_tensor(rb[:, :, 1], pairs[:, :, 0], sin[:, :, 1], ALU.mult))
            own(v.tensor_tensor(rope_a[:], xf[:], k("cos", 64), ALU.mult))
            v.tensor_tensor(qin[:], rope_a[:], rope_b[:], ALU.add).then_inc(step("qin"), 1)
            dve.wait_ge(*after("qinT_ps"))
            v.tensor_copy(qinT[:], bank[0][:, 0:64]).then_inc(step("qinT"), 1)
            dve.wait_ge(*after("k3_ps"))
            own(v.tensor_scalar(KT3[:], bank[3][:, 0:64], col("in_bk"), None, ALU.add))
            v.tensor_tensor(Kb3[:], over(KT3[:], 8), each(k("head_k3"), 64), ALU.mult).then_inc(step("kb3"), 1)
            v.tensor_tensor(V3[:, :, 0:8], bank[4][:, 0:128].rearrange("p (h g) -> p h g", g=8),
                            each(k("pair3"), 8), ALU.mult).then_inc(step("v3"), 1)
            dve.wait_ge(*after("s3_ps"))
            sview = bank[5][:, :].rearrange("p (h t) -> p h t", t=64)
            s2v = s2[:].rearrange("p (h t) -> p h t", t=64)
            s3v = s3[:].rearrange("p (h t) -> p h t", t=64)
            own(v.tensor_tensor(s2v, sview, over(k("causal"), 8), ALU.add))
            own(v.reduce_max(mx3[:], s2v, AX))
            v.tensor_tensor(s3v, s2v, each(mx3[:], 64), ALU.subtract).then_inc(step("s3"), 1)
            dve.wait_ge(*after("pt3_ps"))
            v.tensor_copy(PT3[:].rearrange("p c q -> p (c q)"), bank[0][:, :]).then_inc(step("pt3"), 1)
            dve.wait_ge(*after("att3_ps"))
            attv = bank[1][0:64, 0:144].rearrange("p (h g) -> p h g", g=9)
            own(v.reciprocal(rd3[:], attv[:, :, 8]))
            v.tensor_tensor(att3[:].rearrange("p (h g) -> p h g", g=8), attv[:, :, 0:8],
                            each(rd3[:], 8), ALU.mult).then_inc(step("att3"), 1)
            dve.wait_ge(*after("att3T_ps"))
            v.tensor_copy(attT3[:], bank[2][:, 0:64]).then_inc(step("attT3"), 1)
            dve.wait_ge(*after("proj3_ps"))
            dve.wait_ge(sig("xfb"), 1)
            own(v.tensor_tensor(z3[:], bank[3][0:64, 0:128], xfb[:], ALU.add))
            moments(z3[:], 3, "mv3")
            dve.wait_ge(*after("mv3"))
            own(v.scalar_tensor_tensor(za3[:], z3[:], mv[:, 3, 0:1], spread("L0_ffn_ln1_w"),
                                       ALU.subtract, ALU.mult))
            dve.wait_ge(sig("rstd3"), 1)
            v.scalar_tensor_tensor(y3[:], za3[:], tiny[:, 11:12], spread("L0_ffn_ln1_b"),
                                   ALU.mult, ALU.add).then_inc(step("y3"), 1)
            dve.wait_ge(*after("y3T_ps"))
            v.tensor_copy(y3T[:, 1, :], bank[4][:, 0:64]).then_inc(step("y3T"), 1)

            def top_two(lg, top, idx, idf, hot):
                own(v.max(top, lg))
                own(v.max_index(idx, top, lg))
                own(v.tensor_copy(idf, idx[:, 0:2]))
                v.tensor_scalar(hot[:, 0, :], k("iota8"), idf[:, 0:1], None, ALU.is_equal)
                own(v.tensor_scalar(hot[:, 1, :], k("iota8"), idf[:, 1:2], None, ALU.is_equal))

            dve.wait_ge(*after("lg3_ps"))
            own(v.tensor_copy(lg3[:], bank[5][:, 0:8]))
            top_two(lg3[:], top3[:], idx3[:], idf3[:], hot3)
            v.tensor_scalar(neg3[:], top3[:, 0:1], -1.0, None, ALU.mult).then_inc(step("neg3"), 1)
            own(v.tensor_tensor(hot3[:, 2, :], hot3[:, 0, :], hot3[:, 1, :], ALU.add))
            dve.wait_ge(sig("eg3"), 1)
            own(v.reciprocal(sum3[:, 1:2], sum3[:, 0:1]))
            own(v.scalar_tensor_tensor(hot3[:, 0, :], eg3[:], sum3[:, 1:2], hot3[:, 2, :], ALU.mult, ALU.mult))
            own(v.tensor_scalar(w4_3[:, 0, :], hot3[:, 0, 0:4], k("half")[:, 0:1], None, ALU.mult))
            own(v.scalar_tensor_tensor(w4_3[:, 1, :], hot3[:, 0, 4:8], k("half")[:, 1:2], w4_3[:, 0, :],
                                       ALU.mult, ALU.add))
            dve.wait_ge(*after("exp3_ps"))
            v.tensor_tensor(moe3[:], bank[0][:, :].rearrange("p (e f) -> p e f", e=4), each(w4_3[:, 1, :], 128),
                            ALU.mult).then_inc(step("moe3"), 1)
            dve.wait_ge(*after("z3b_ps"))
            moments(bank[1][0:64, 0:128], 4, "mv4")
            dve.wait_ge(*after("mv4"))
            own(v.scalar_tensor_tensor(zb3[:], bank[1][0:64, 0:128], mv[:, 4, 0:1], spread("L0_ffn_ln2_w"),
                                       ALU.subtract, ALU.mult))
            dve.wait_ge(sig("rstd4"), 1)
            dve.wait_ge(sig("x2b"), 1)
            v.scalar_tensor_tensor(x3[:], zb3[:], tiny[:, 13:14], x2b[:], ALU.mult, ALU.add).then_inc(step("x3"), 1)
            dve.wait_ge(*after("x3"))

            moments(x3[:], 5, "mv5")
            dve.wait_ge(sig("rstd5"), 1)
            normed(xn[:], x3[:], 5, tiny[:, 15:16], "xn4")
            dve.wait_ge(*after("xnT4_ps"))
            v.tensor_copy(xnT4[:], bank[2][:, 0:64]).then_inc(step("xnT4"), 1)
            for b in range(2):
                dve.wait_ge(sig("qk4_hi"), b + 1)
                v.scalar_tensor_tensor(qk_lo[:, 512 * b:512 * b + 512], bank[b][:, :], QK_UP,
                                       qk_hi[:, 512 * b:512 * b + 512], ALU.mult, ALU.subtract).then_inc(
                    sig("qk4_lo"), 1)

            def chunk_max(value, dst, width=512, b=6):
                dve.wait_ge(sig("max4_scores"), value)
                v.reduce_max(dst, bank[b][:, 0:width], AX).then_inc(sig("max4_part"), 1)

            def shift_columns(g):
                dve.wait_ge(sig("max4_part"), MAXES * g + MAXES)
                own4(v.reduce_max(m4[:, 0, :], cm[:, :, 0:CHUNKS * 2 + 1], AX), g, 1)
                own4(v.tensor_scalar(m4[:, 1, :], m4[:, 0, :], -1.0 / UP, HEADROOM * ROOT, ALU.mult, ALU.add), g, 2)
                high, low_ = (shiftcols[:, :, part:part + 33:32] for part in range(2))
                own4(v.tensor_copy(high, each(m4[:, 1, :], 2)), g, 3)
                v.tensor_tensor(low_, each(m4[:, 1, :], 2), high, ALU.subtract).then_inc(sig("shiftcols"), 1)

            def shift_rows(g):
                dve.wait_ge(sig("shift_ps"), g + 1)
                v.tensor_copy(shiftrows[:, g % 2, :], bank[6][0:64, 0:256]).then_inc(sig("shiftrows"), 1)

            def own4(ins, g, n):
                ins.then_inc(sig("dve_shift"), 1)
                dve.wait_ge(sig("dve_shift"), 3 * g + n)

            def low(n, s, width=1024):
                dve.wait_ge(sig("prob4"), n + 1)
                v.tensor_tensor(pl4[:, s, 0:width], P[:, s, 0:width], ph4[:, s, 0:width], ALU.subtract).then_inc(
                    sig("prob4_lo"), 1)

            def add_output(g):
                dve.wait_ge(sig("y4_part"), g + 1)
                if g == 0:
                    dve.wait_ge(sig("x3b"), 1)
                else:
                    dve.wait_ge(sig("x4_part"), g)
                v.tensor_tensor(x4[:], bank[4 + g % 2][0:64, 0:128], x4[:] if g else x3b[:], ALU.add).then_inc(
                    sig("x4_part"), 1)

            with dve.Fori(0, CHUNKS) as i:
                for s in range(2):
                    for q in range(2):
                        chunk_max(i * 4 + (2 * s + q + 1), cm[:, q, bass.ds(i * 2 + s, 1)], b=3 + 2 * s + q)
            for q in range(2):
                chunk_max(CHUNKS * 4 + 1 + q, cm[:, q, CHUNKS * 2:CHUNKS * 2 + 1], 128, b=3 + q)
            shift_columns(0)
            shift_rows(0)

            for g in range(GROUPS):
                first = MAXES * (g + 1) + 1
                if g + 1 < GROUPS:
                    for q in range(2):
                        chunk_max(first + q, cm[:, q, 0:1], b=6 + q)
                low(g * BLOCKS, g % 2)
                if g + 1 < GROUPS:
                    for q in range(2):
                        chunk_max(first + 2 + q, cm[:, q, 1:2], b=6 + q)
                    for q in range(2):
                        chunk_max(first + 4 + q, cm[:, q, CHUNKS * 2:CHUNKS * 2 + 1], 128, b=6 + q)
                with dve.Fori(1, CHUNKS) as i:
                    for s in range(2):
                        low(i * 2 + (g * BLOCKS + s - 1), (g + s + 1) % 2)
                        if g + 1 < GROUPS:
                            for q in range(2):
                                chunk_max(i * 4 + (first + 2 * s + q + 2), cm[:, q, bass.ds(i * 2 + s, 1)], b=6 + q)
                low(g * BLOCKS + BLOCKS - 2, (g + 1) % 2)
                if g + 1 < GROUPS:
                    shift_columns(g + 1)
                low(g * BLOCKS + BLOCKS - 1, g % 2, GROUP)
                if g + 1 < GROUPS:
                    shift_rows(g + 1)
                if g:
                    add_output(g - 1)
                dve.wait_ge(sig("den4"), g + 1)
                v.reciprocal(rden4[:], bank[4 + g % 2][:, 256:512]).then_inc(sig("rden4"), 1)
                dve.wait_ge(sig("rden4"), g + 1)
                v.tensor_tensor(un4[:], bank[4 + g % 2][:, 0:256], rden4[:], ALU.mult).then_inc(sig("un4"), 1)
            add_output(GROUPS - 1)

            dve.wait_ge(sig("x4_part"), GROUPS)
            moments(x4[:], 6, "mv6")
            dve.wait_ge(sig("w5_loaded"), 16)
            own(v.tensor_scalar(gate5[:, 1:2], gate5[:, 0:1], 1.0, None, ALU.add))
            own(v.reciprocal(gate5[:, 2:3], gate5[:, 1:2]))
            v.tensor_scalar(wo5[:], w5[:, 3, :], gate5[:, 2:3], None, ALU.mult).then_inc(step("wo5"), 1)
            dve.wait_ge(sig("rstd6"), 1)
            normed(xn[:], x4[:], 6, tiny[:, 3:4], "xn5")
            dve.wait_ge(*after("xnT5_ps"))
            v.tensor_copy(xnT5[:], bank[0][:, 0:64]).then_inc(step("xnT5"), 1)
            dve.wait_ge(*after("kv5_ps"))
            v.tensor_scalar(tk5[:, 0, :], bank[2][0:64, 0:128], 0.0, None, ALU.min).then_inc(step("kmin5"), 1)
            v.tensor_copy(vv5[:, 0:128], bank[2][0:64, 128:256]).then_inc(step("vv5"), 1)
            dve.wait_ge(*after("q5_ps"))
            v.tensor_scalar(tq5[:, 0, :], bank[1][:, 0:64], col("L1_attn_bq"), 0.0, ALU.add, ALU.min).then_inc(
                step("qmin5"), 1)
            own(v.tensor_scalar(tq5[:, 1, :], bank[1][:, 0:64], col("L1_attn_bq"), 0.0, ALU.add, ALU.max))
            dve.wait_ge(sig("kexp5"), 1)
            v.scalar_tensor_tensor(k5[:], bank[2][0:64, 0:128], 0.0, tk5[:, 1, :], ALU.max, ALU.add).then_inc(
                step("k5"), 1)
            dve.wait_ge(sig("qexp5"), 1)
            v.tensor_tensor(q5[:], tq5[:, 1, :], tq5[:, 2, :], ALU.add).then_inc(step("q5"), 1)
            dve.wait_ge(*after("kvsum5_ps"))
            v.tensor_tensor(kv5[:], bank[3][:, 0:144], k("own_head"), ALU.mult).then_inc(step("kv5"), 1)
            dve.wait_ge(*after("num5_ps"))
            own(v.tensor_scalar(dn5[:, 0, :], bank[4][0:64, 128:144], 1e-6, None, ALU.add))
            own(v.reciprocal(dn5[:, 1, :], dn5[:, 0, :]))
            v.tensor_tensor(att5[:].rearrange("p (h g) -> p h g", g=8),
                            bank[4][0:64, 0:128].rearrange("p (h g) -> p h g", g=8),
                            each(dn5[:, 1, :], 8), ALU.mult).then_inc(step("att5"), 1)
            dve.wait_ge(*after("att5T_ps"))
            v.tensor_copy(attT5[:], bank[5][:, 0:64]).then_inc(step("attT5"), 1)
            dve.wait_ge(*after("o5_ps"))
            dve.wait_ge(sig("x4b"), 1)
            own(v.tensor_tensor(x5[:], bank[0][0:64, 0:128], x4b[:], ALU.add))

            moments(x5[:], 7, "mv7")
            dve.wait_ge(sig("rstd7"), 1)
            normed(xt6[:], x5[:], 7, tiny[:, 5:6], "xt6")
            dve.wait_ge(*after("xt6T_ps"))
            v.tensor_copy(xt6T[:, 1, :], bank[1][:, 0:64]).then_inc(step("xt6T"), 1)
            dve.wait_ge(*after("lg6_ps"))
            own(v.tensor_copy(lg6[:], bank[2][:, 0:8]))
            top_two(lg6[:], top6[:], idx6[:], idf6[:], hot6)
            v.tensor_tensor(d6[:, 0:1], top6[:, 1:2], top6[:, 0:1], ALU.subtract).then_inc(step("d6"), 1)
            dve.wait_ge(sig("e6"), 1)
            own(v.tensor_scalar(d6[:, 2:3], d6[:, 1:2], 1.0, None, ALU.add))
            own(v.reciprocal(d6[:, 3:4], d6[:, 2:3]))
            own(v.tensor_tensor(d6[:, 4:5], d6[:, 1:2], d6[:, 3:4], ALU.mult))
            own(v.tensor_scalar(hot6[:, 2, :], hot6[:, 0, :], d6[:, 3:4], None, ALU.mult))
            own(v.scalar_tensor_tensor(hot6[:, 0, :], hot6[:, 1, :], d6[:, 4:5], hot6[:, 2, :], ALU.mult, ALU.add))
            own(v.tensor_scalar(w4_6[:, 0, :], hot6[:, 0, 0:4], k("half")[:, 0:1], None, ALU.mult))
            v.scalar_tensor_tensor(w4_6[:, 1, :], hot6[:, 0, 4:8], k("half")[:, 1:2], w4_6[:, 0, :],
                                   ALU.mult, ALU.add).then_inc(step("w4_6"), 1)
            dve.wait_ge(*after("o6_ps"))
            zv = bank[5][:, :].rearrange("p (e f) -> p e f", e=4)
            for e in range(4):
                ins = v.bn_stats(st6[:, e, :], zv[:, e, :])
            own(ins)
            for e in range(4):
                ins = v.bn_aggr(mv6[:, e, :], st6[:, e, :])
            ins.then_inc(step("mv6e"), 1)
            dve.wait_ge(*after("mv6e"))
            own(v.tensor_tensor(o6a[:], zv, each(mv6[:, :, 0], 128), ALU.subtract))
            own(v.tensor_tensor(o6b[:], o6a[:], lng6[:].rearrange("p (e f) -> p e f", e=4), ALU.mult))
            dve.wait_ge(sig("rstd6e"), 1)
            v.tensor_tensor(o6c[:], o6b[:], each(w4_6[:, 2, :], 128), ALU.mult).then_inc(step("o6c"), 1)
            dve.wait_ge(*after("out6_ps"))
            v.tensor_tensor(x6[:], bank[6][0:64, 0:128], x5[:], ALU.add).then_inc(step("x6"), 1)

        @block.gpsimd
        def _(pool):
            g = nc.gpsimd
            count = [0]

            def own(ins):
                count[0] += 1
                ins.then_inc(sig("pool_own"), 1)
                pool.wait_ge(sig("pool_own"), count[0])

            def inverse_root(dst, tmp, var, eps, name, n=1):
                own(g.tensor_scalar(tmp, var, eps, None, ALU.add))
                g.tensor_tensor(dst, tmp, halfpow[0:dst.shape[0], 0:n], ALU.pow).then_inc(sig(name), 1)

            pool.wait_ge(*after("halfpow"))
            pool.wait_ge(*after("mv0"))
            inverse_root(tiny[:, 0:1], tiny[:, 1:2], mv[:, 0, 1:2], 1e-5, "rstd0")
            for c in range(CHUNKS + 1):
                n = CHUNK if c < CHUNKS else 1
                pool.wait_ge(sig("chunk_hi"), c + 1)
                g.tensor_tensor(ctx_lo[:, CHUNK * c:CHUNK * c + n, :], chunk[c % 4][:, 0:n, :],
                                ctx_hi[:, CHUNK * c:CHUNK * c + n, :], ALU.subtract).then_inc(sig("chunk_lo"), 1)
            for b in range(CHUNKS + 1):
                pool.wait_ge(sig("prob1"), b + 1)
                if b == 0:
                    own(g.tensor_copy(acc[:, 0, 0:512], p1[:, 0, :]))
                elif b < CHUNKS:
                    own(g.tensor_tensor(acc[:, 0, 0:512], acc[:, 0, 0:512], p1[:, b, :], ALU.add))
                else:
                    g.tensor_tensor(acc[:, 0, 0:64], acc[:, 0, 0:64], p1[:, b, 0:64], ALU.add).then_inc(
                        sig("acc1"), 1)
            pool.wait_ge(*after("mv1"))
            var = mv[:, 1, 1:2]
            own(g.tensor_scalar(tiny[:, 1:2], var, 1e-5, None, ALU.add))
            own(g.tensor_tensor(tiny[:, 2:3], tiny[:, 1:2], halfpow[0:64, 0:1], ALU.pow))
            own(g.tensor_tensor(tiny[:, 4:5], var, tiny[:, 2:3], ALU.mult))
            own(g.tensor_tensor(tiny[:, 4:5], tiny[:, 4:5], tiny[:, 2:3], ALU.mult))
            own(g.tensor_scalar(tiny[:, 4:5], tiny[:, 4:5], 1e-5, None, ALU.add))
            own(g.tensor_tensor(tiny[:, 6:7], tiny[:, 4:5], halfpow[0:64, 0:1], ALU.pow))
            g.tensor_tensor(tiny[:, 7:8], tiny[:, 6:7], tiny[:, 2:3], ALU.mult).then_inc(sig("rstd1"), 1)
            pool.wait_ge(*after("mv2"))
            inverse_root(tiny[:, 9:10], tiny[:, 8:9], mv[:, 2, 1:2], 1e-5, "rstd2")
            pool.wait_ge(sig("w3_loaded"), 80)
            pool.wait_ge(*after("xf"))
            g.tensor_tensor(xfb[:], xf[:], spread("L0_ffn_out_proj_b"), ALU.add).then_inc(sig("xfb"), 1)
            g.tensor_tensor(x2b[:], x2[:], spread("L0_ffn_ln2_b"), ALU.add).then_inc(sig("x2b"), 1)
            pool.wait_ge(*after("mv3"))
            inverse_root(tiny[:, 11:12], tiny[:, 10:11], mv[:, 3, 1:2], 1e-5, "rstd3")
            pool.wait_ge(*after("mv4"))
            inverse_root(tiny[:, 13:14], tiny[:, 12:13], mv[:, 4, 1:2], 1e-5, "rstd4")
            pool.wait_ge(*after("mv5"))
            inverse_root(tiny[:, 15:16], tiny[:, 14:15], mv[:, 5, 1:2], 1e-5, "rstd5")
            g.tensor_tensor(x3b[:], x3[:], spread("L1_xattn_proj_b"), ALU.add).then_inc(sig("x3b"), 1)

            def add_block(n, s, first=False, width=1024, to=0):
                pool.wait_ge(sig("prob4"), n + 1)
                a = acc[:, to, 0:width]
                if first:
                    g.tensor_copy(a, P[:, s, 0:width]).then_inc(sig("acc4"), 1)
                else:
                    pool.wait_ge(sig("acc4"), n)
                    g.tensor_tensor(a, a, P[:, s, 0:width], ALU.add).then_inc(sig("acc4"), 1)

            pool.wait_ge(sig("fold4_ps"), H4)
            g.memset(hz6[:], 0.0).then_inc(sig("hz6_zero"), 1)
            for grp in range(GROUPS):
                if grp >= 2:
                    pool.wait_ge(sig("den4"), grp - 1)
                n0 = BLOCKS * grp
                add_block(n0, grp % 2, first=True, to=grp % 2)
                add_block(n0 + 1, (grp + 1) % 2, to=grp % 2)
                with pool.Fori(1, CHUNKS) as i:
                    for s in range(2):
                        add_block(i * 2 + (n0 + s), (grp + s) % 2, to=grp % 2)
                add_block(n0 + BLOCKS - 1, grp % 2, width=GROUP, to=grp % 2)
            pool.wait_ge(*after("mv6"))
            inverse_root(tiny[:, 3:4], tiny[:, 2:3], mv[:, 6, 1:2], 1e-5, "rstd6")
            g.tensor_tensor(x4b[:], x4[:], spread("L1_attn_bo"), ALU.add).then_inc(sig("x4b"), 1)
            pool.wait_ge(*after("mv7"))
            inverse_root(tiny[:, 5:6], tiny[:, 4:5], mv[:, 7, 1:2], 1e-5, "rstd7")
            pool.wait_ge(sig("w6_loaded"), 16 * 9)
            pool.wait_ge(*after("w4_6"))
            g.tensor_tensor(wb6[:], lnb6[:].rearrange("p (e f) -> p e f", e=4), each(w4_6[:, 1, :], 128),
                            ALU.mult).then_inc(sig("wb6"), 1)
            pool.wait_ge(*after("mv6e"))
            own(g.tensor_scalar(ve6[:, 0, :], mv6[:, :, 1], 1e-6, None, ALU.add))
            own(g.tensor_tensor(ve6[:, 1, :], ve6[:, 0, :], halfpow[:, 0:4], ALU.pow))
            g.tensor_tensor(w4_6[:, 2, :], ve6[:, 1, :], w4_6[:, 1, :], ALU.mult).then_inc(sig("rstd6e"), 1)

        @block.scalar
        def _(act):
            a = nc.scalar

            for c in range(CHUNKS + 1):
                n = CHUNK if c < CHUNKS else 1
                act.wait_ge(sig(f"ctx_loaded{c % 4}"), 16 * (c // 4 + 1))
                a.activation(ctx_hi[:, CHUNK * c:CHUNK * c + n, :], chunk[c % 4][:, 0:n, :], ACT.Copy).then_inc(
                    sig("chunk_hi"), 1)
                for j in range(0, n, 4):
                    m = min(4, n - j)
                    act.wait_ge(sig("chunk_half_transposed"), 2 * c + j // 4 + 1)
                    a.activation(ctxT_hi[:, CHUNK * c + j:CHUNK * c + j + m, :].rearrange("p t k -> p (t k)"),
                                 bank[2 * (c % 2) + j // 4][:, 0:128 * m], ACT.Copy, scale=CTX_UP).then_inc(
                        sig("chunkT_hi"), 1)
            SOFT = 1.0 / (ROOT * UP)
            for b in range(CHUNKS + 1):
                n = 512 if b < CHUNKS else 64
                act.wait_ge(sig("scores1"), b + 1)
                a.activation(P_hi[:, b, 0:n], bank[b][:, 0:n], ACT.Exp, scale=SOFT).then_inc(sig("prob1_hi"), 1)
                a.activation(p1[:, b, 0:n], bank[b][:, 0:n], ACT.Exp, scale=SOFT).then_inc(sig("prob1"), 1)
            a.activation(gate5[:, 0:1], col("stdp"), ACT.Exp, scale=-1.0).then_inc(sig("gate5"), 1)

            def fold_copy(*heads):
                both = big[:].rearrange("p (w h d) -> p h w d", w=2, h=H4)
                for h in heads:
                    act.wait_ge(sig("fold4_ps"), h + 1)
                    a.activation(both[:, h], bank[6 + h % 2][:, 0:256].rearrange("p (w d) -> p w d", w=2),
                                 ACT.Copy).then_inc(sig("fold4"), 1)

            fold_copy(0)
            act.wait_ge(sig("bqh"), 2)
            act.wait_ge(*after("q2_ps"))
            for f in range(2):
                ins = a.activation(Q2[:, f, :], bank[1][:, 0:64], ACT.Identity, bias=bqh[:, f:f + 1],
                                   scale=k("half")[:, f:f + 1])
            ins.then_inc(sig("q2"), 1)
            fold_copy(1, 2)
            act.wait_ge(*after("s2"))
            a.activation(e2[:, 0:256], s2[:, 0:256], ACT.Exp, scale=0.25).then_inc(sig("e2"), 1)
            fold_copy(3, 4, 5, 6, 7, 8, 9)

            act.wait_ge(*after("xfT_ps"))
            a.activation(xfT[:], over(bank[1][:, 0:64], 2), ACT.Copy).then_inc(sig("xfT"), 1)
            fold_copy(10)
            act.wait_ge(*after("q3_ps"))
            for f in range(2):
                ins = a.activation(Q3[:, f, :], bank[2][:, 0:64], ACT.Identity, bias=bqh[:, 2 + f:3 + f],
                                   scale=k("half")[:, f:f + 1])
            ins.then_inc(sig("q3"), 1)
            fold_copy(11, 12)
            act.wait_ge(*after("s3"))
            a.activation(e3[:], s3[:], ACT.Exp, scale=1.0 / math.sqrt(8.0)).then_inc(sig("e3"), 1)
            fold_copy(13, 14, 15)
            act.wait_ge(*after("neg3"))
            a.activation(eg3[:], lg3[:], ACT.Exp, bias=neg3[:, 0:1], accum_out=sum3[:, 0:1]).then_inc(sig("eg3"), 1)

            for b in range(2):
                act.wait_ge(sig("qk4_ps"), b + 1)
                a.activation(qk_hi[:, 512 * b:512 * b + 512], bank[b][:, :], ACT.Copy, scale=QK_UP).then_inc(
                    sig("qk4_hi"), 1)

            def exponentials(n, s, width=1024):
                act.wait_ge(sig("scores4"), n + 1)
                half = min(width, 512)
                for j in range(0, width, 512):
                    a.activation(ph4[:, s, j:j + half], bank[2 * s + j // 512][:, 0:half], ACT.Exp, scale=SOFT)
                for j in range(0, width, 512):
                    ins = a.activation(P[:, s, j:j + half], bank[2 * s + j // 512][:, 0:half], ACT.Exp, scale=SOFT)
                ins.then_inc(sig("prob4"), 1)

            def used(n):
                act.wait_ge(sig("pv4"), n - 1)
                act.wait_ge(sig("acc4"), n - 1)
                act.wait_ge(sig("prob4_lo"), n - 1)

            for grp in range(GROUPS):
                n0 = BLOCKS * grp
                for s in range(2):
                    if n0 + s >= 2:
                        used(n0 + s)
                    exponentials(n0 + s, (grp + s) % 2)
                with act.Fori(1, CHUNKS) as i:
                    for s in range(2):
                        used(i * 2 + (n0 + s))
                        exponentials(i * 2 + (n0 + s), (grp + s) % 2)
                used(n0 + BLOCKS - 1)
                exponentials(n0 + BLOCKS - 1, grp % 2, GROUP)

            act.wait_ge(*after("kmin5"))
            a.activation(tk5[:, 1, :], tk5[:, 0, :], ACT.Exp).then_inc(sig("kexp5"), 1)
            act.wait_ge(*after("qmin5"))
            a.activation(tq5[:, 2, :], tq5[:, 0, :], ACT.Exp).then_inc(sig("qexp5"), 1)
            a.preload_act_table(ACT.Gelu)
            act.wait_ge(sig("hz6_zero"), 1)
            for half in range(2):
                act.wait_ge(sig("h6_ps"), half + 1)
                a.activation(hz6[:, 8 * half:8 * half + 8, 64 * half:64 * half + 64],
                             bank[3 + half][:, :].rearrange("p (c t) -> p c t", t=64), ACT.Gelu).then_inc(
                    sig("hz6"), 1)
            act.wait_ge(*after("d6"))
            a.activation(d6[:, 1:2], d6[:, 0:1], ACT.Exp).then_inc(sig("e6"), 1)

        @block.tensor
        def _(pe):
            mm = nc.tensor.matmul

            def one(o, lhsT, rhs):
                return mm(o, lhsT, rhs, start=True, stop=True)

            pe.wait_ge(sig("w0_loaded"), 48)
            one(bank[4][:, 0:128], w0[:, 0, :], w0[:, 1, :])
            one(bank[4][:, 128:129], w0[:, 1, :], col("L0_xattn_bq")).then_inc(step("fold0"), 1)
            one(bank[5][:, 0:128], w0[:, 2, :], w0[:, 3, :])
            pe.wait_ge(*after("bvrep"))
            mm(bank[5][0:64, 128:256], bvrep[:], w0[:, 3, :], start=True, stop=False)
            pe.wait_ge(*after("ones"))
            mm(bank[5][0:64, 128:256], ones[0:1, 0:64], row("L0_xattn_bo"), start=False, stop=True).then_inc(
                step("fold0b"), 1)
            pe.wait_ge(sig("ident_loaded"), 16)
            pe.wait_ge(*after("xn1"))
            nc.tensor.transpose(bank[6][:, 0:64], xn[:], ident[0:64, 0:64]).then_inc(step("xnT1_ps"), 1)
            pe.wait_ge(*after("xnT1"))
            pe.wait_ge(*after("a0"))
            one(bank[7][:, 0:64], a0[:], xnT[:]).then_inc(step("qk1_ps"), 1)

            def transposes(c):
                n = CHUNK if c < CHUNKS else 1
                pe.wait_ge(sig(f"ctx_loaded{c % 4}"), 16 * (c // 4 + 1))
                if c >= 2:
                    pe.wait_ge(sig("chunkT_lo"), 2 * (c - 1))
                for j in range(n):
                    ins = nc.tensor.transpose(bank[2 * (c % 2) + j // 4][:, 128 * (j % 4):128 * (j % 4) + 128],
                                              chunk[c % 4][:, j, :], ident)
                    if j % 4 == 3 or n == 1:
                        ins.then_inc(sig("chunk_half_transposed"), 1)

            def scores1_hi(c):
                if c == 0:
                    pe.wait_ge(*after("qk1"))
                    pe.wait_ge(*after("b0"))
                    pe.wait_ge(*after("xb1"))
                if c >= 2:
                    pe.wait_ge(sig("max1_part"), c - 1)
                pe.wait_ge(sig("chunkT_hi"), 2 * c + (2 if c < CHUNKS else 1))
                b = bank[4 + c % 2]
                for half in range(2 if c < CHUNKS else 1):
                    t0 = CHUNK * c + 4 * half
                    n = 4 if c < CHUNKS else 1
                    ins = mm(b[64 * half:64 * half + 64, 0:128 * n], qk1_hi[:],
                             ctxT_hi[:, t0:t0 + n, :].rearrange("p t k -> p (t k)"), start=True, stop=True)
                ins.then_inc(sig("scores1_hi"), 1)

            transposes(0)
            for c in range(CHUNKS + 1):
                if c < CHUNKS:
                    transposes(c + 1)
                scores1_hi(c)
            pe.wait_ge(*after("max1"))
            one(bank[7][0:1, 0:128], m1[:], ident).then_inc(step("max1_row"), 1)
            pe.wait_ge(*after("shift1"))
            pe.wait_ge(*after("up16"))
            pe.wait_ge(sig("chunkT_lo"), 2 * CHUNKS + 1)

            def scores1(b):
                n = CHUNK if b < CHUNKS else 1
                whole = bank[b][:, 0:64 * n].rearrange("p (t q) -> p t q", q=64)
                mm(whole, up16[0:1, :], over(r1_hi[:], n), start=True, stop=False)
                mm(whole, up16[0:1, :], over(r1_lo[:], n), start=False, stop=False)
                for j in range(n):
                    o = bank[b][:, 64 * j:64 * j + 64]
                    tile = CHUNK * b + j
                    mm(o, ctxT_hi[:, tile, :], qk1_hi[:], start=False, stop=False)
                    mm(o, ctxT_hi[:, tile, :], qk1_lo[:], start=False, stop=False)
                    ins = mm(o, ctxT_lo[:, tile, :], qk1_hi[:], start=False, stop=(j == n - 1))
                ins.then_inc(sig("scores1"), 1)

            def weighted1(b):
                n = CHUNK if b < CHUNKS else 1
                pe.wait_ge(sig("prob1_hi"), b + 1)
                pe.wait_ge(sig("prob1_lo"), b + 1)
                for j in range(n):
                    tile = CHUNK * b + j
                    at = slice(64 * j, 64 * j + 64)
                    mm(bank[7][:, 0:64], ctx_hi[:, tile, :], P_hi[:, b, at], start=(tile == 0), stop=False)
                    mm(bank[7][:, 0:64], ctx_hi[:, tile, :], P_lo[:, b, at], start=False, stop=False)
                    ins = mm(bank[7][:, 0:64], ctx_lo[:, tile, :], P_hi[:, b, at], start=False,
                             stop=(tile == TILES - 1))
                return ins

            pe.wait_ge(sig("chunk_lo"), CHUNKS + 1)
            for b in range(CHUNKS + 1):
                scores1(b)
            for b in range(CHUNKS + 1):
                ins = weighted1(b)
            ins.then_inc(step("u1"), 1)
            pe.wait_ge(sig("acc1"), 1)
            for j in range(CHUNK):
                ins = mm(bank[1][0:64, 0:1], acc[:, 0, 64 * j:64 * j + 64], ones[:, 0:1], start=(j == 0),
                         stop=(j == CHUNK - 1))
            ins.then_inc(step("den1"), 1)
            pe.wait_ge(*after("UT"))
            one(bank[0][0:64, 0:128], UT[:], b0[:]).then_inc(step("y1"), 1)

            def fold4(*heads):
                for h in heads:
                    if h == 0:
                        pe.wait_ge(sig("w4_loaded"), 64)
                    if h >= 2:
                        pe.wait_ge(sig("fold4"), h - 1)
                    j, head = h // 2, slice(64 * (h % 2), 64 * (h % 2) + 64)
                    one(bank[6 + h % 2][:, 0:128], wq4t[head, j, :], wk4t[head, j, :])
                    one(bank[6 + h % 2][:, 128:256], wv4t[head, j, :], wp4t[head, j, :]).then_inc(
                        sig("fold4_ps"), 1)

            pe.wait_ge(sig("w2_loaded"), 32)
            pe.wait_ge(sig("wvg"), 2)
            mm(bank[3][:, 0:128], ones[0:1, :], bvg[:], start=True, stop=False)
            pe.wait_ge(*after("xn2"))
            nc.tensor.transpose(bank[0][:, 0:64], xn[:], ident[0:64, 0:64]).then_inc(step("xnT2_ps"), 1)
            fold4(0)
            pe.wait_ge(*after("xd2"))
            one(bank[2][:, 0:64], w2[:, 1, :], xd2[:, 0, :]).then_inc(step("k2_ps"), 1)
            one(bank[1][:, 0:64], w2[:, 0, :], xd2[:, 0, :]).then_inc(step("q2_ps"), 1)
            mm(bank[3][:, 0:128], xd2[:].rearrange("p i t -> p (i t)"), wvg[:], start=False, stop=True).then_inc(
                step("v2_ps"), 1)
            fold4(1)
            pe.wait_ge(*after("kb2"))
            pe.wait_ge(sig("q2"), 1)
            one(bank[4][:, 0:256], Q2[:].rearrange("p i t -> p (i t)"), Kb2[:].rearrange("p h t -> p (h t)")).then_inc(
                step("s2_ps"), 1)
            fold4(2, 3)
            pe.wait_ge(sig("e2"), 1)
            for c in range(2):
                ins = nc.tensor.transpose(bank[0][:, 128 * c:128 * c + 128], e2[:, 128 * c:128 * c + 128], ident)
            ins.then_inc(step("pt2_ps"), 1)
            fold4(4)
            pe.wait_ge(*after("pt2"))
            pe.wait_ge(*after("v2"))
            for f in range(2):
                for c in range(2):
                    h = 4 * f + 2 * c
                    ins = one(bank[1][0:64, 17 * h:17 * h + 34], PT2[:, c, 64 * f:64 * f + 64],
                              V2[:, h:h + 2, :].rearrange("p h g -> p (h g)"))
            ins.then_inc(step("att2_ps"), 1)
            fold4(5, 6, 7)
            pe.wait_ge(*after("turned"))
            for h in range(8):
                ins = mm(bank[2][0:64, 0:128], k("pick", 64)[:, 64 * h:64 * h + 64],
                         turned[:, h, :, :].rearrange("p b g -> p (b g)"), start=(h == 0), stop=(h == 7))
            ins.then_inc(step("o2_ps"), 1)
            fold4(8, 9)

            pe.wait_ge(sig("w3_loaded"), 80)
            mm(bank[4][:, 0:128], ones[0:1, :], row("in_bv"), start=True, stop=False)
            pe.wait_ge(*after("xf"))
            nc.tensor.transpose(bank[1][:, 0:64], xf[:], ident[0:64, 0:64]).then_inc(step("xfT_ps"), 1)
            fold4(10)
            pe.wait_ge(*after("qin"))
            nc.tensor.transpose(bank[0][:, 0:64], qin[:], ident[0:64, 0:64]).then_inc(step("qinT_ps"), 1)
            pe.wait_ge(sig("xfT"), 1)
            mm(bank[4][:, 0:128], xfT[:].rearrange("p i t -> p (i t)"), w3[:, 2, :], start=False, stop=True)
            pe.wait_ge(*after("qinT"))
            one(bank[3][:, 0:64], w3[:, 1, :], qinT[:]).then_inc(step("k3_ps"), 1)
            one(bank[2][:, 0:64], w3[:, 0, :], qinT[:]).then_inc(step("q3_ps"), 1)
            pe.wait_ge(*after("kb3"))
            pe.wait_ge(sig("q3"), 1)
            one(bank[5][:, :], Q3[:].rearrange("p i t -> p (i t)"), Kb3[:].rearrange("p h t -> p (h t)")).then_inc(
                step("s3_ps"), 1)
            fold4(11, 12, 13)
            pe.wait_ge(sig("e3"), 1)
            for c in range(4):
                ins = nc.tensor.transpose(bank[0][:, 128 * c:128 * c + 128], e3[:, 128 * c:128 * c + 128], ident)
            ins.then_inc(step("pt3_ps"), 1)
            fold4(14)
            pe.wait_ge(*after("pt3"))
            pe.wait_ge(*after("v3"))
            for f in range(2):
                for c in range(4):
                    h = 8 * f + 2 * c
                    ins = one(bank[1][0:64, 9 * h:9 * h + 18], PT3[:, c, 64 * f:64 * f + 64],
                              V3[:, h:h + 2, :].rearrange("p h g -> p (h g)"))
            ins.then_inc(step("att3_ps"), 1)
            pe.wait_ge(*after("att3"))
            nc.tensor.transpose(bank[2][:, 0:64], att3[:], ident[0:64, 0:64]).then_inc(step("att3T_ps"), 1)
            pe.wait_ge(*after("attT3"))
            one(bank[3][0:64, 0:128], attT3[:], w3[:, 3, :]).then_inc(step("proj3_ps"), 1)
            fold4(15)
            mm(bank[5][:, 0:8], ones[0:1, :], row("gate_b"), start=True, stop=False)
            mm(bank[0][:, :], k("halfrows", 2), eb3[:], start=True, stop=False)
            pe.wait_ge(*after("y3"))
            nc.tensor.transpose(bank[4][:, 0:64], y3[:], ident[0:64, 0:64]).then_inc(step("y3T_ps"), 1)
            pe.wait_ge(*after("y3T"))
            lower = y3T[:, 1:3, :].rearrange("p i t -> p (i t)")
            upper = y3T[:, 0:2, :].rearrange("p i t -> p (i t)")
            mm(bank[5][:, 0:8], lower, gate3[:], start=False, stop=False)
            mm(bank[5][:, 0:8], upper, gate3[:], start=False, stop=True).then_inc(step("lg3_ps"), 1)
            mm(bank[0][:, :], lower, ew3[:, 0:512], start=False, stop=False)
            mm(bank[0][:, :], upper, ew3[:, 512:1024], start=False, stop=True).then_inc(step("exp3_ps"), 1)
            mm(bank[1][0:64, 0:128], ident[0:64, 0:64], y3[:], start=True, stop=False)
            pe.wait_ge(*after("moe3"))
            for e in range(4):
                ins = mm(bank[1][0:64, 0:128], k("fold"), moe3[:, e, :], start=False, stop=(e == 3))
            ins.then_inc(step("z3b_ps"), 1)

            pe.wait_ge(*after("xn4"))
            nc.tensor.transpose(bank[2][:, 0:64], xn[:], ident[0:64, 0:64]).then_inc(step("xnT4_ps"), 1)
            pe.wait_ge(*after("xnT4"))
            pe.wait_ge(sig("fold4"), H4)
            for h in range(H4):
                ins = one(bank[h // 8][:, 64 * (h % 8):64 * (h % 8) + 64], a4[:, h, :], xnT4[:])
                if h % 8 == 7:
                    ins.then_inc(sig("qk4_ps"), 1)

            def max_scores(value, q, keys, group, width=512, b=6):
                if value is not None:
                    pe.wait_ge(sig("max4_part"), value)
                a = GROUP * group + 128 * q
                mm(bank[b][:, 0:width], qk_hi[:, a:a + 128], keys, start=True, stop=True).then_inc(
                    sig("max4_scores"), 1)

            ctxT = ctxT_hi[:].rearrange("p t k -> p (t k)")

            def shift_to_rows(g):
                pe.wait_ge(sig("shiftcols"), g + 1)
                for q in range(2):
                    ins = mm(bank[6][0:64, 128 * q:128 * q + 128], shiftcols[:, q, :], ident16[:], start=True,
                             stop=True)
                ins.then_inc(sig("shift_ps"), 1)

            pe.wait_ge(sig("qk4_hi"), 1)
            pe.wait_ge(*after("ident16"))
            pe.wait_ge(sig("zeros"), 3)
            pe.wait_ge(sig("qk4_lo"), 2)
            for s in range(2):
                for q in range(2):
                    max_scores(None, q, ctxT[:, 512 * s:512 * s + 512], 0, b=3 + 2 * s + q)
            with pe.Fori(1, CHUNKS) as i:
                for s in range(2):
                    for q in range(2):
                        max_scores(i * 4 + (2 * s + q - 3), q, ctxT[:, bass.ds(i * 1024 + 512 * s, 512)], 0,
                                   b=3 + 2 * s + q)
            for q in range(2):
                max_scores(CHUNKS * 4 + q - 3, q, ctxT[:, CHUNKS * 1024:], 0, 128, b=3 + q)
            shift_to_rows(0)
            pe.wait_ge(sig("qk4_lo"), 2)

            def scores4(n, s, tile, g, tiles=BLOCK):
                for b in range((tiles + 1) // 2):
                    w = min(2, tiles)
                    mm(bank[2 * s + b][:, 0:256 * w].rearrange("p (t q) -> p t q", t=w), up16[32 * b:32 * b + 2, :],
                       over(shiftrows[32 * b:32 * b + 2, g % 2, :], w), start=True, stop=False)
                hi, lo = (x[:, GROUP * g:GROUP * g + GROUP] for x in (qk_hi, qk_lo))
                for j in range(tiles):
                    o = bank[2 * s + j // 2][:, 256 * (j % 2):256 * (j % 2) + 256]
                    kh = ctxT_hi[:, bass.ds(tile + j, 1), :].rearrange("p t k -> p (t k)")
                    kl = ctxT_lo[:, bass.ds(tile + j, 1), :].rearrange("p t k -> p (t k)")
                    mm(o, kh, hi, start=False, stop=False)
                    mm(o, kh, lo, start=False, stop=False)
                    ins = mm(o, kl, hi, start=False, stop=(j % 2 == 1 or tiles == 1))
                ins.then_inc(sig("scores4"), 1)

            def weighted4(n, s, tile, g, tiles=BLOCK, first=False, last=False):
                pe.wait_ge(sig("prob4_lo"), n + 1)
                o = bank[4 + g % 2][:, 0:256]
                for j in range(tiles):
                    at = slice(256 * j, 256 * j + 256)
                    kh = ctx_hi[:, bass.ds(tile + j, 1), :].rearrange("p t k -> p (t k)")
                    kl = ctx_lo[:, bass.ds(tile + j, 1), :].rearrange("p t k -> p (t k)")
                    mm(o, kh, ph4[:, s, at], start=(first and j == 0), stop=False)
                    mm(o, kl, ph4[:, s, at], start=False, stop=False)
                    ins = mm(o, kh, pl4[:, s, at], start=False, stop=(last and j == tiles - 1))
                ins.then_inc(sig("pv4"), 1)

            def finish4(g):
                pe.wait_ge(sig("acc4"), BLOCKS * (g + 1))
                for j in range(BLOCK):
                    ins = mm(bank[4 + g % 2][:, 256:512], ones[:], acc[:, g % 2, 256 * j:256 * j + 256],
                             start=(j == 0), stop=(j == BLOCK - 1))
                ins.then_inc(sig("den4"), 1)

            def output4(g):
                pe.wait_ge(sig("un4"), g + 1)
                for j in range(4):
                    h = 4 * g + j
                    ins = mm(bank[4 + g % 2][0:64, 0:128], un4[:, 64 * j:64 * j + 64], v4[:, h, :], start=(j == 0),
                             stop=(j == 3))
                ins.then_inc(sig("y4_part"), 1)

            for g in range(GROUPS):
                n0 = BLOCKS * g
                ahead = g + 1 < GROUPS

                def maxima(first, keys, width=512):
                    if ahead:
                        for q in range(2):
                            max_scores(first + (MAXES * (g + 1) + q - 1), q, keys, g + 1, width, b=6 + q)

                even, odd = g % 2, (g + 1) % 2
                pe.wait_ge(sig("shiftrows"), g + 1)
                if g:
                    pe.wait_ge(sig("prob4"), n0 - 1)
                scores4(n0, even, 0, g)
                maxima(0, ctxT[:, 0:512])
                if g:
                    pe.wait_ge(sig("prob4"), n0)
                    finish4(g - 1)
                scores4(n0 + 1, odd, 4, g)
                maxima(2, ctxT[:, 512:1024])
                if g >= 2:
                    pe.wait_ge(sig("x4_part"), g - 1)
                weighted4(n0, even, 0, g, first=True)
                maxima(4, ctxT[:, CHUNKS * 1024:], 128)
                if g:
                    output4(g - 1)
                with pe.Fori(1, CHUNKS) as i:
                    pe.wait_ge(sig("prob4"), i * 2 + (n0 - 1))
                    scores4(i * 2 + n0, even, i * 8, g)
                    maxima(i * 4 + 2, ctxT[:, bass.ds(i * 1024 + 0, 512)])
                    weighted4(i * 2 + (n0 - 1), odd, i * 8 - 4, g)
                    pe.wait_ge(sig("prob4"), i * 2 + n0)
                    scores4(i * 2 + (n0 + 1), odd, i * 8 + 4, g)
                    maxima(i * 4 + 4, ctxT[:, bass.ds(i * 1024 + 512, 512)])
                    weighted4(i * 2 + n0, even, i * 8, g)
                nl = n0 + BLOCKS - 1
                pe.wait_ge(sig("prob4"), nl - 1)
                scores4(nl, even, TILES - 1, g, 1)
                weighted4(nl - 1, odd, TILES - 5, g)
                if ahead:
                    shift_to_rows(g + 1)
                weighted4(nl, even, TILES - 1, g, 1, last=True)
            finish4(GROUPS - 1)
            output4(GROUPS - 1)

            pe.wait_ge(sig("w5_loaded"), 16)
            mm(bank[2][0:64, 0:128], ones[0:1, 0:64], row("L1_attn_bk"), start=True, stop=False)
            pe.wait_ge(*after("xn5"))
            nc.tensor.transpose(bank[0][:, 0:64], xn[:], ident[0:64, 0:64]).then_inc(step("xnT5_ps"), 1)
            pe.wait_ge(*after("xnT5"))
            mm(bank[2][0:64, 0:128], xnT5[:], w5[:, 1, :], start=False, stop=True)
            mm(bank[2][0:64, 128:256], ones[0:1, 0:64], row("L1_attn_bv"), start=True, stop=False)
            mm(bank[2][0:64, 128:256], xnT5[:], w5[:, 2, :], start=False, stop=True).then_inc(step("kv5_ps"), 1)
            one(bank[1][:, 0:64], w5[:, 0, :], xnT5[:]).then_inc(step("q5_ps"), 1)
            pe.wait_ge(*after("k5"))
            pe.wait_ge(*after("vv5"))
            one(bank[3][:, 0:144], k5[:], vv5[:]).then_inc(step("kvsum5_ps"), 1)
            pe.wait_ge(*after("kv5"))
            pe.wait_ge(*after("q5"))
            one(bank[4][0:64, 0:144], q5[:], kv5[:]).then_inc(step("num5_ps"), 1)
            pe.wait_ge(*after("att5"))
            nc.tensor.transpose(bank[5][:, 0:64], att5[:], ident[0:64, 0:64]).then_inc(step("att5T_ps"), 1)
            pe.wait_ge(*after("attT5"))
            pe.wait_ge(*after("wo5"))
            one(bank[0][0:64, 0:128], attT5[:], wo5[:]).then_inc(step("o5_ps"), 1)

            pe.wait_ge(sig("w6_loaded"), 16 * 9)
            for half in range(2):
                mm(bank[3 + half][:, :].rearrange("p (c t) -> p c t", t=64), b16[:],
                   each(ident[0:16, 8 * half:8 * half + 8], 64), start=True, stop=False)
            mm(bank[5][:, :], k("halfrows", 2), b26[:], start=True, stop=False)
            pe.wait_ge(*after("xt6"))
            nc.tensor.transpose(bank[1][:, 0:64], xt6[:], ident[0:64, 0:64]).then_inc(step("xt6T_ps"), 1)
            mm(bank[5][:, :].rearrange("p (e f) -> p e f", e=4), k("dup", 64), over(xt6[:], 4), start=False,
               stop=False)
            pe.wait_ge(*after("xt6T"))
            lower = xt6T[:, 1:3, :].rearrange("p i t -> p (i t)")
            upper = xt6T[:, 0:2, :].rearrange("p i t -> p (i t)")
            for half in range(2):
                for c in range(8):
                    e, f = 4 * half + c // 2, c % 2
                    ins = mm(bank[3 + half][:, 64 * c:64 * c + 64], w16[:, e, 128 * f:128 * f + 128],
                             xt6T[:, 1, :], start=False, stop=(c == 7))
                ins.then_inc(sig("h6_ps"), 1)
            mm(bank[2][:, 0:8], lower, gate6[:], start=True, stop=False)
            mm(bank[2][:, 0:8], upper, gate6[:], start=False, stop=True).then_inc(step("lg6_ps"), 1)
            for half in range(2):
                pe.wait_ge(sig("hz6"), half + 1)
                for c in range(8):
                    e, f = c // 2, c % 2
                    ins = mm(bank[5][:, 128 * e:128 * e + 128], hz6[:, 8 * half + c, :],
                             w26[:, 4 * half + e, f, :], start=False, stop=(half == 1 and c == 7))
            ins.then_inc(step("o6_ps"), 1)
            pe.wait_ge(sig("wb6"), 1)
            for e in range(4):
                mm(bank[6][0:64, 0:128], k("fold"), wb6[:, e, :], start=(e == 0), stop=False)
            pe.wait_ge(*after("o6c"))
            for e in range(4):
                ins = mm(bank[6][0:64, 0:128], k("fold"), o6c[:, e, :], start=False, stop=(e == 3))
            ins.then_inc(step("out6_ps"), 1)


BLOCKS = (TILES + BLOCK - 1) // BLOCK
MAXES = 2 * (2 * CHUNKS + 1)


def kernel(debug=False, **inputs):
    import numpy as _np
    import concourse.bacc as _bacc
    from concourse import mybir as _mybir
    from concourse.bass_utils import run_bass_kernel_spmd as _run

    a = {n: _np.asarray(v) for n, v in inputs.items()}

    def stack(*xs):
        return _np.stack(xs, 1)

    def pairs(w):
        return w.reshape(8, 2, 128, 64).transpose(1, 3, 0, 2).reshape(128, 8, 128)

    wqkv = a["L0_ffn_in_proj_w"]
    bqkv = a["L0_ffn_in_proj_b"]
    vectors = dict(a, in_bq=bqkv[0:128], in_bk=bqkv[128:256], in_bv=bqkv[256:384], gate_b=a["L0_ffn_gate_b"],
                   stdp=_np.repeat(a["L1_attn_stdp"], 8))
    lay = {
        "x": a["x"][0], "ctx": a["ctx_1024"][0], "const": CONST,
        "cols": _np.stack([vectors[n] for n in COLS], 1),
        "rows": _np.concatenate([vectors[n] for n in ROWS])[None],
        "wide": _np.broadcast_to(_np.stack([vectors[n] for n in WIDE])[None], (64, len(WIDE), 128)),
        "w0": stack(a["L0_xattn_Wq"], a["L0_xattn_Wk"], a["L0_xattn_Wv"], a["L0_xattn_Wo"].T),
        "w2": stack(a["L0_attn_Wq"], a["L0_attn_Wk"]),
        "L0_attn_Wv": a["L0_attn_Wv"],
        "w3": stack(wqkv[0:128].T, wqkv[128:256].T, wqkv[256:384].T, a["L0_ffn_out_proj_w"].T),
        "gate3": a["L0_ffn_gate_w"].T,
        "ew3": a["L0_ffn_expert_w"].transpose(2, 0, 1).reshape(128, 1024),
        "eb3": a["L0_ffn_expert_b"].reshape(2, 512),
        "wq4t": pairs(a["L1_xattn_w_q"]), "wk4t": pairs(a["L1_xattn_w_k"]), "wv4t": pairs(a["L1_xattn_w_v"]),
        "wp4t": a["L1_xattn_proj_w"].reshape(128, 8, 128).transpose(2, 1, 0),
        "w5": stack(a["L1_attn_Wq"].T, a["L1_attn_Wk"].T, a["L1_attn_Wv"].T, a["L1_attn_Wo"].T),
        "L1_ffn_gate_w": a["L1_ffn_gate_w"],
        "w16": a["L1_ffn_w1"].transpose(1, 0, 2),
        "w26": a["L1_ffn_w2"].reshape(8, 2, 128, 128).transpose(2, 0, 1, 3),
        "b16": a["L1_ffn_b1"].reshape(16, 128), "b26": a["L1_ffn_b2"].reshape(2, 512),
        "lng6": a["L1_ffn_ln_g"].reshape(2, 512), "lnb6": a["L1_ffn_ln_b"].reshape(2, 512),
    }
    nc = _bacc.Bacc("TRN2", target_bir_lowering=False, num_devices=1)
    arrays, t = {}, {}
    for name, v in lay.items():
        v = _np.ascontiguousarray(v)
        arrays[f"in_{name}"] = v
        t[name] = nc.dram_tensor(f"in_{name}", v.shape, _mybir.dt.from_np(v.dtype), kind="ExternalInput").ap()
    out = nc.dram_tensor("out", (64, 128), _mybir.dt.float32, kind="ExternalOutput").ap()
    dbg = [nc.dram_tensor(f"dbg{i}", (64, 128), _mybir.dt.float32, kind="ExternalOutput").ap()
           for i in range(5)] if debug else None
    build(nc, t, out, dbg)
    r = _run(nc, [arrays], core_ids=[0])
    got = r.results[0]["out"].reshape(1, 64, 128)
    if debug:
        return (got,) + tuple(r.results[0][f"dbg{i}"].reshape(1, 64, 128) for i in range(5))
    return got
```

```python
import math
import numpy as np
import concourse.bass as bass
from concourse import mybir
from contextlib import ExitStack

Q = 64
D = 128
KEYS = 6272
TILES = KEYS // D
CHUNK = 8
CHUNKS = TILES // CHUNK
H4 = 16
GROUP = 256
GROUPS = H4 * Q // GROUP
BLOCK = 4
E = 8

STEPS = {
    "vector_step": [
        "halfpow", "ones", "up16", "mv0", "bvrep", "xn1", "ident16", "a0", "b0", "xb1", "xnT1", "qk1", "max1",
        "shift1", "UT", "mv1", "xn2", "xd2", "kb2", "v2", "s2", "pt2", "turned", "mv2", "xf", "qin", "qinT",
        "kb3", "v3", "s3", "pt3", "att3", "attT3", "mv3", "y3", "y3T", "neg3", "moe3", "mv4", "x3", "mv5",
        "xn4", "xnT4", "mv6", "wo5", "xn5", "xnT5", "kmin5", "vv5", "qmin5", "k5", "q5", "kv5", "att5",
        "attT5", "mv7", "xt6", "xt6T", "d6", "w4_6", "mv6e", "o6c", "x6",
    ],
    "tensor_step": [
        "fold0", "fold0b", "xnT1_ps", "qk1_ps", "max1_row", "u1", "den1", "y1", "xnT2_ps", "k2_ps", "q2_ps",
        "v2_ps", "s2_ps", "pt2_ps", "att2_ps", "o2_ps", "xfT_ps", "qinT_ps", "k3_ps", "q3_ps", "s3_ps",
        "pt3_ps", "att3_ps", "att3T_ps", "proj3_ps", "y3T_ps", "lg3_ps", "exp3_ps", "z3b_ps", "xnT4_ps",
        "xnT5_ps", "kv5_ps", "q5_ps", "kvsum5_ps", "num5_ps", "att5T_ps", "o5_ps", "xt6T_ps", "lg6_ps",
        "o6_ps", "out6_ps",
    ],
}

CTX_UP = 64.0
QK_UP = 16.0
UP = CTX_UP * QK_UP
HEADROOM = 5.0
ROOT = math.sqrt(float(D))


def constants():
    p = np.arange(128)
    parts = {}
    parts["ident"] = np.eye(128)
    parts["fold"] = (p[:, None] % 64 == np.arange(64)[None])
    parts["half"] = (p[:, None] // 64 == np.arange(2)[None])
    parts["head_k2"] = ((p[:, None] // 16) % 4 == np.arange(4)[None])
    parts["head_k3"] = ((p[:, None] // 8) % 8 == np.arange(8)[None])
    parts["pair2"] = (p[:, None] // 64 == np.arange(8)[None] % 2)
    parts["pair3"] = (p[:, None] // 64 == np.arange(16)[None] % 2)
    own = np.zeros((128, 144))
    own[:, :128] = p[:, None] // 8 == p[None] // 8
    own[:, 128:] = p[:, None] // 8 == np.arange(16)[None]
    parts["own_head"] = own
    t = np.arange(64)
    parts["causal"] = np.where(t[None] <= (p[:, None] % 64), 0.0, -1e30)
    parts["iota8"] = np.tile(np.arange(8), (128, 1))
    halfrows = np.zeros((128, 128))
    halfrows[0, :64] = 1
    halfrows[1, 64:] = 1
    parts["halfrows"] = halfrows
    dup = np.zeros((128, 128))
    dup[:64] = np.concatenate([np.eye(64), np.eye(64)], 1)
    parts["dup"] = dup
    inv = (1.0 / np.float32(10000.0) ** (np.arange(0, 8, 2, dtype=np.float32) / np.float32(8))).astype(np.float32)
    f = (t.astype(np.float32)[:, None] * inv[None]).astype(np.float32)
    cos, sin = np.zeros((128, 128)), np.zeros((128, 128))
    cos[:64] = np.tile(np.repeat(np.cos(f), 2, axis=1), (1, 16))
    sin[:64] = np.tile(np.stack([-np.sin(f), np.sin(f)], -1).reshape(64, 8), (1, 16))
    parts["cos"], parts["sin"] = cos, sin
    turn = np.zeros((128, 8))
    turn[:64] = t[:, None] % 8 == np.arange(8)[None]
    parts["turn"] = turn
    pick = np.zeros((128, 8, 64))
    for s in range(64):
        for h in range(8):
            pick[s, h, h * 8 + s // 8] = 1
    parts["pick"] = pick.reshape(128, 512)
    at, where = 0, {}
    for name, a in parts.items():
        where[name] = (at, at + a.shape[1])
        at += a.shape[1]
    return np.ascontiguousarray(np.concatenate(list(parts.values()), 1).astype(np.float32)), where


CONST, AT = constants()
EARLY = AT["half"][0]

COLS = ["L0_xattn_bq", "L0_xattn_bv", "L0_attn_gamma", "L0_attn_beta", "L0_attn_bq", "L0_attn_bk",
        "in_bq", "in_bk", "L1_attn_bq", "stdp"]
ROWS = {"L0_xattn_bo": 128, "L0_attn_bv": 1024, "in_bv": 128, "gate_b": 8, "L1_attn_bk": 128, "L1_attn_bv": 128}
WIDE = ["L0_ffn_out_proj_b", "L0_ffn_ln1_w", "L0_ffn_ln1_b", "L0_ffn_ln2_w", "L0_ffn_ln2_b",
        "L1_xattn_proj_b", "L1_attn_bo"]


def build(nc, t, out, debug=None):
    f32, f16, u32 = mybir.dt.float32, mybir.dt.float16, mybir.dt.uint32
    ALU = mybir.AluOpType
    ACT = mybir.ActivationFunctionType
    AX = mybir.AxisListType.X

    with ExitStack() as ctx:
        def sb(name, shape, dt=f32):
            return ctx.enter_context(nc.sbuf_tensor(name, shape, dt))

        sems = {}

        def sig(name):
            if name not in sems:
                sems[name] = ctx.enter_context(nc.semaphore(name))
            return sems[name]

        made = {name: 0 for name in STEPS}

        def counter(name):
            return next(c for c, names in STEPS.items() if name in names)

        def step(name):
            c = counter(name)
            assert STEPS[c][made[c]] == name, (name, STEPS[c][made[c]])
            made[c] += 1
            return sig(c)

        def after(name):
            return sig(counter(name)), STEPS[counter(name)].index(name) + 1

        bank = [ctx.enter_context(nc.psum_tensor(f"bank{i}", [128, 512], f32)) for i in range(8)]

        const = sb("const", list(CONST.shape))

        def k(name, rows=128):
            a, b = AT[name]
            return const[0:rows, a:b]

        ident = k("ident")
        x0 = sb("x0", [64, D])
        cols = sb("cols", [128, len(COLS)])
        rows = sb("rows", [1, sum(ROWS.values())])
        wide = sb("wide", [64, len(WIDE), D])

        def col(name):
            return cols[:, COLS.index(name):COLS.index(name) + 1]

        def row(name):
            names = list(ROWS)
            a = sum(ROWS[n] for n in names[:names.index(name)])
            return rows[0:1, a:a + ROWS[name]]

        def spread(name):
            return wide[:, WIDE.index(name), :]

        w0 = sb("w0", [128, 4, D])
        w2 = sb("w2", [128, 2, D])
        wv2 = sb("wv2", [128, 1024])
        w3 = sb("w3", [128, 4, D])
        gate3 = sb("gate3", [128, E])
        ew3 = sb("ew3", [128, E * D])
        eb3 = sb("eb3", [2, 512])
        w4 = sb("w4", [128, 4, 8, D])
        wq4t, wk4t, wv4t, wp4t = (w4[:, i] for i in range(4))
        w5 = sb("w5", [128, 4, D])
        gate6 = sb("gate6", [128, E])
        w16 = sb("w16", [128, E, 256])
        w26 = sb("w26", [128, E, 2, D])
        b16 = sb("b16", [16, D])
        b26 = sb("b26", [2, 512])
        lng6 = sb("lng6", [128, 512])
        lnb6 = sb("lnb6", [128, 512])

        ctx32 = sb("ctx32", [128, 2, CHUNK, D])
        late = w26[:].rearrange("p (c e) f d -> p c (e f) d", c=2)
        chunk = [ctx32[:, 0], ctx32[:, 1], late[:, 0], late[:, 1]]
        ctx_hi = sb("ctx_hi", [128, TILES, D], f16)
        ctx_lo = sb("ctx_lo", [128, TILES, D], f16)
        ctxT_hi = sb("ctxT_hi", [128, TILES, D], f16)
        ctxT_lo = sb("ctxT_lo", [128, TILES, D], f16)
        ones = sb("ones", [128, 128])
        up16 = sb("up16", [128, 128], f16)
        halfpow = sb("halfpow", [128, 4])

        block = ctx.enter_context(nc.Block())

        xn = sb("xn", [64, D])
        stat = sb("stat", [64, 8, 6])
        mv = sb("mv", [64, 8, 2])
        tiny = sb("tiny", [64, 16])
        xb1 = sb("xb1", [64, D])
        a0 = sb("a0", [128, D])
        c0 = sb("c0", [128, 1])
        b0 = sb("b0", [128, D])
        bvrep = sb("bvrep", [128, 64])
        xnT = sb("xnT", [128, 64])
        qkf = sb("qkf", [128, 64])
        qk1_hi = sb("qk1_hi", [128, 64], f16)
        qk1_lo = sb("qk1_lo", [128, 64], f16)
        cm1 = sb("cm1", [128, 8])
        m1 = sb("m1", [128, 1])
        mrow1 = sb("mrow1", [1, 64])
        shift1 = sb("shift1", [1, 64], f16)
        prob = sb("prob", [128, 8192], f16)
        P_hi = prob[:, 0:3584].rearrange("p (b n) -> p b n", b=7)
        P_lo = prob[:, 3584:7168].rearrange("p (b n) -> p b n", b=7)
        ph4 = prob[:, 0:2048].rearrange("p (s n) -> p s n", s=2)
        pl4 = prob[:, 2048:4096].rearrange("p (s n) -> p s n", s=2)
        P = prob[:, 4096:8192].bitcast(f32).rearrange("p (s n) -> p s n", s=2)
        big = sb("big", [128, 2 * H4 * D])
        p1 = big[:, 0:3584].rearrange("p (b n) -> p b n", b=7)
        a4 = big[:, 0:2048].rearrange("p (h d) -> p h d", h=H4)
        v4 = big[:, 2048:4096].rearrange("p (h d) -> p h d", h=H4)
        acc = sb("acc", [128, 2, 1024])
        UT = sb("UT", [128, 64])
        rden1 = sb("rden1", [64, 1])
        x1 = sb("x1", [64, D])
        wvg = sb("wvg", [128, D])
        bvg = sb("bvg", [1, D])
        xd2 = sb("xd2", [128, 2, 64])
        bqh = sb("bqh", [128, 4])
        Q2 = sb("Q2", [128, 2, 64])
        KT2 = sb("KT2", [128, 64])
        Kb2 = P[:, 0, 0:256].rearrange("p (h t) -> p h t", h=4)
        V2 = sb("V2", [128, 8, 17])
        mx2 = sb("mx2", [128, 8])
        s2, s3, e2, e3 = (ctx32[:, i // 2, 4 * (i % 2):4 * (i % 2) + 4, :].rearrange("p t d -> p (t d)")
                          for i in range(4))
        PT2, PT3 = (acc[:, 1, 512 * i:512 * i + 512].rearrange("p (c q) -> p c q", c=4) for i in range(2))
        rd2 = sb("rd2", [64, 16])
        att2 = sb("att2", [64, D])
        turned = acc[0:64, 0, :].rearrange("p (h b g) -> p h b g", h=8, b=8)
        x2 = sb("x2", [64, D])
        xf = sb("xf", [64, D])
        rope_a = sb("rope_a", [64, D])
        rope_b = sb("rope_b", [64, D])
        qin = sb("qin", [64, D])
        qinT = sb("qinT", [128, 64])
        xfT = sb("xfT", [128, 2, 64])
        Q3 = sb("Q3", [128, 2, 64])
        KT3 = sb("KT3", [128, 64])
        Kb3 = P[:, 0, 512:1024].rearrange("p (h t) -> p h t", h=8)
        V3 = sb("V3", [128, 16, 9])
        mx3 = sb("mx3", [128, 8])
        rd3 = sb("rd3", [64, 16])
        att3 = sb("att3", [64, D])
        attT3 = sb("attT3", [128, 64])
        xfb = sb("xfb", [64, D])
        z3 = sb("z3", [64, D])
        za3 = sb("za3", [64, D])
        y3 = sb("y3", [64, D])
        y3T = sb("y3T", [128, 3, 64])
        lg3 = sb("lg3", [128, 8])
        top3 = sb("top3", [128, 8])
        idx3 = sb("idx3", [128, 8], u32)
        idf3 = sb("idf3", [128, 2])
        neg3 = sb("neg3", [128, 1])
        eg3 = sb("eg3", [128, 8])
        sum3 = sb("sum3", [128, 2])
        hot3 = sb("hot3", [128, 3, 8])
        w4_3 = sb("w4_3", [128, 2, 4])
        moe3 = P[:, 1, 0:512].rearrange("p (e f) -> p e f", e=4)
        zb3 = sb("zb3", [64, D])
        x2b = sb("x2b", [64, D])
        x3 = sb("x3", [64, D])
        xnT4 = sb("xnT4", [128, 64])
        qk_hi = sb("qk_hi", [128, H4 * Q], f16)
        qk_lo = sb("qk_lo", [128, H4 * Q], f16)
        qk32 = acc[:, 0, :]
        cm = sb("cm", [128, 2, 2 * CHUNKS + 1])
        m4 = sb("m4", [128, 2])
        shiftcols = sb("shiftcols", [128, 2, 128], f16)
        shiftrow = sb("shiftrow", [1, GROUP], f16)
        shift4 = sb("shift4", [128, GROUP])
        rden4 = sb("rden4", [128, GROUP])
        un4 = sb("un4", [128, GROUP])
        ident16 = sb("ident16", [128, 128], f16)
        x3b = sb("x3b", [64, D])
        x4 = sb("x4", [64, D])
        wo5 = sb("wo5", [128, D])
        gate5 = sb("gate5", [128, 4])
        tq5 = sb("tq5", [128, 3, 64])
        q5 = sb("q5", [128, 64])
        tk5 = sb("tk5", [64, 2, D])
        k5 = sb("k5", [64, D])
        vv5 = sb("vv5", [64, 144])
        kv5 = sb("kv5", [128, 144])
        dn5 = sb("dn5", [64, 2, 16])
        att5 = sb("att5", [64, D])
        attT5 = sb("attT5", [128, 64])
        xnT5 = sb("xnT5", [128, 64])
        x4b = sb("x4b", [64, D])
        x5 = sb("x5", [64, D])
        xt6 = sb("xt6", [64, D])
        xt6T = sb("xt6T", [128, 3, 64])
        hz6 = w4[:, 0:2].rearrange("p i h d -> p (i h) d")
        o6 = w4[:, 2:4].rearrange("p i (j h) d -> p (i j) h d", j=2)
        lg6 = sb("lg6", [128, 8])
        top6 = sb("top6", [128, 8])
        idx6 = sb("idx6", [128, 8], u32)
        idf6 = sb("idf6", [128, 2])
        d6 = sb("d6", [128, 5])
        hot6 = sb("hot6", [128, 3, 8])
        w4_6 = sb("w4_6", [128, 3, 4])
        st6 = sb("st6", [128, 4, 6])
        mv6 = sb("mv6", [128, 4, 2])
        ve6 = sb("ve6", [128, 2, 4])
        o6a, o6b, o6c, wb6 = (o6[:, i] for i in range(4))
        x6 = sb("x6", [64, D])

        def over(ap, n):
            return ap.unsqueeze(1).broadcast_to([ap.shape[0], n, ap.shape[1]])

        def each(ap, n):
            return ap.unsqueeze(2).broadcast_to([ap.shape[0], ap.shape[1], n])

        @block.sync
        def _(sp):
            def load(dst, name, ready):
                sp.dma_start(dst, t[name]).then_inc(sig(ready), 16)

            sp.dma_start(x0[:], t["x"]).then_inc(sig("x_loaded"), 16)
            sp.dma_start(const[:, 0:EARLY], t["const"][:, 0:EARLY]).then_inc(sig("ident_loaded"), 16)
            load(cols[:], "cols", "w0_loaded")
            load(w0[:], "w0", "w0_loaded")
            load(rows[:], "rows", "w0_loaded")
            view = t["ctx"].rearrange("(p t) d -> p t d", t=TILES)
            for c in range(CHUNKS + 1):
                n = CHUNK if c < CHUNKS else TILES - CHUNK * CHUNKS
                if c >= 4:
                    sp.wait_ge(sig("chunk_half_transposed"), 2 * (c - 3))
                    sp.wait_ge(sig("chunk_lo"), c - 3)
                sp.dma_start(chunk[c % 4][:, 0:n, :], view[:, CHUNK * c:CHUNK * c + n, :]).then_inc(
                    sig(f"ctx_loaded{c % 4}"), 16)
            sp.dma_start(const[:, EARLY:], t["const"][:, EARLY:]).then_inc(sig("const_loaded"), 16)
            load(w2[:], "w2", "w2_loaded")
            load(wv2[:], "L0_attn_Wv", "w2_loaded")
            load(wide[:], "wide", "w3_loaded")
            load(w3[:], "w3", "w3_loaded")
            load(gate3[:], "gate3", "w3_loaded")
            load(ew3[:], "ew3", "w3_loaded")
            load(eb3[:], "eb3", "w3_loaded")
            load(wq4t[:], "wq4t", "w4_loaded")
            load(wk4t[:], "wk4t", "w4_loaded")
            load(wv4t[:], "wv4t", "w4_loaded")
            load(wp4t[:], "wp4t", "w4_loaded")
            load(w5[:], "w5", "w5_loaded")
            load(gate6[:], "L1_ffn_gate_w", "w6_loaded")
            load(w16[:], "w16", "w6_loaded")
            sp.wait_ge(sig("chunk_half_transposed"), 2 * CHUNKS + 1)
            sp.wait_ge(sig("chunk_lo"), CHUNKS + 1)
            load(w26[:], "w26", "w6_loaded")
            load(b16[:], "b16", "w6_loaded")
            load(b26[:], "b26", "w6_loaded")
            for half in range(2):
                for dst, name in ((lng6, "lng6"), (lnb6, "lnb6")):
                    sp.dma_start(dst[64 * half:64 * half + 64, :],
                                 t[name][half:half + 1, :].broadcast_to([64, 512])).then_inc(sig("w6_loaded"), 16)
            n = 1
            sp.wait_ge(*after("x6"))
            sp.dma_start(out, x6[:]).then_inc(sig("stored"), 16)
            if debug is not None:
                for i, v in enumerate([x1, x2, x3, x4, x5]):
                    sp.dma_start(debug[i], v[:]).then_inc(sig("stored"), 16)
                    n += 1
            sp.wait_ge(sig("stored"), 16 * n)

        @block.vector
        def _(dve):
            v = nc.vector
            count = [0]

            def own(ins):
                count[0] += 1
                ins.then_inc(sig("dve_own"), 1)
                dve.wait_ge(sig("dve_own"), count[0])

            def moments(src, s, name):
                own(v.bn_stats(stat[:, s, :], src))
                v.bn_aggr(mv[:, s, :], stat[:, s, :]).then_inc(step(name), 1)

            def normed(dst, src, s, scale, name):
                v.tensor_scalar(dst, src, mv[:, s, 0:1], scale, ALU.subtract, ALU.mult).then_inc(step(name), 1)

            v.memset(halfpow[:], -0.5).then_inc(step("halfpow"), 1)
            v.memset(ones[:], 1.0).then_inc(step("ones"), 1)
            v.memset(up16[:], UP).then_inc(step("up16"), 1)
            own(v.memset(cm1[:], -3.0e38))
            v.memset(y3T[:], 0.0).then_inc(sig("zeros"), 1)
            v.memset(xt6T[:], 0.0).then_inc(sig("zeros"), 1)
            own(v.memset(vv5[:], 1.0))

            dve.wait_ge(sig("x_loaded"), 16)
            moments(x0[:], 0, "mv0")
            dve.wait_ge(sig("w0_loaded"), 48)
            v.reduce_sum(bvg[:], row("L0_attn_bv").rearrange("p (e j) -> p e j", j=8), AX).then_inc(sig("wvg"), 1)
            v.tensor_copy(bvrep[:], col("L0_xattn_bv").broadcast_to([128, 64])).then_inc(step("bvrep"), 1)
            dve.wait_ge(sig("rstd0"), 1)
            normed(xn[:], x0[:], 0, tiny[:, 0:1], "xn1")
            dve.wait_ge(sig("ident_loaded"), 16)
            v.tensor_copy(ident16[:], ident).then_inc(step("ident16"), 1)
            dve.wait_ge(*after("fold0"))
            v.tensor_copy(a0[:], bank[4][:, 0:128])
            v.tensor_copy(c0[:], bank[4][:, 128:129]).then_inc(step("a0"), 1)
            dve.wait_ge(*after("a0"))
            dve.wait_ge(*after("fold0b"))
            v.tensor_copy(b0[:], bank[5][:, 0:128]).then_inc(step("b0"), 1)
            v.tensor_tensor(xb1[:], x0[:], bank[5][0:64, 128:256], ALU.add).then_inc(step("xb1"), 1)
            dve.wait_ge(*after("xnT1_ps"))
            v.tensor_copy(xnT[:], bank[6][:, 0:64]).then_inc(step("xnT1"), 1)
            dve.wait_ge(*after("qk1_ps"))
            own(v.tensor_scalar(qkf[:], bank[7][:, 0:64], c0[:, 0:1], QK_UP, ALU.add, ALU.mult))
            own(v.tensor_copy(qk1_hi[:], qkf[:]))
            v.tensor_tensor(qk1_lo[:], qkf[:], qk1_hi[:], ALU.subtract).then_inc(step("qk1"), 1)

            def split_lo(c, n):
                for j in range(0, n, 4):
                    m = min(4, n - j)
                    b = bank[2 * (c % 2) + j // 4]
                    dve.wait_ge(sig("chunkT_hi"), 2 * c + j // 4 + 1)
                    v.scalar_tensor_tensor(
                        ctxT_lo[:, CHUNK * c + j:CHUNK * c + j + m, :].rearrange("p t k -> p (t k)"),
                        b[:, 0:128 * m], CTX_UP,
                        ctxT_hi[:, CHUNK * c + j:CHUNK * c + j + m, :].rearrange("p t k -> p (t k)"),
                        ALU.mult, ALU.subtract).then_inc(sig("chunkT_lo"), 1)

            for c in range(CHUNKS + 1):
                split_lo(c, CHUNK if c < CHUNKS else 1)
                dve.wait_ge(sig("scores1_hi"), c + 1)
                if c < CHUNKS:
                    ins = v.reduce_max(cm1[:, c:c + 1], bank[4 + c % 2][:], AX)
                else:
                    ins = v.reduce_max(cm1[0:64, c:c + 1], bank[4 + c % 2][0:64, 0:128], AX)
                ins.then_inc(sig("max1_part"), 1)
            dve.wait_ge(sig("max1_part"), CHUNKS + 1)
            v.reduce_max(m1[:], cm1[:], AX).then_inc(step("max1"), 1)
            dve.wait_ge(*after("max1_row"))
            own(v.reduce_max(mrow1[:], bank[7][0:1, 0:128].rearrange("p (h q) -> p q h", h=2), AX))
            v.tensor_scalar(shift1[:], mrow1[:], -1.0 / UP, HEADROOM * ROOT, ALU.mult, ALU.add).then_inc(
                step("shift1"), 1)
            dve.wait_ge(sig("w2_loaded"), 32)
            v.reduce_sum(wvg[:], wv2[:].rearrange("p (e j) -> p e j", j=8), AX).then_inc(sig("wvg"), 1)
            for b in range(CHUNKS + 1):
                n = 512 if b < CHUNKS else 64
                dve.wait_ge(sig("prob1"), b + 1)
                v.tensor_tensor(P_lo[:, b, 0:n], p1[:, b, 0:n], P_hi[:, b, 0:n], ALU.subtract).then_inc(
                    sig("prob1_lo"), 1)
            dve.wait_ge(*after("u1"))
            v.tensor_copy(UT[:], bank[7][:, 0:64]).then_inc(step("UT"), 1)
            dve.wait_ge(*after("den1"))
            own(v.reciprocal(rden1[:], bank[1][0:64, 0:1]))
            dve.wait_ge(*after("y1"))
            own(v.scalar_tensor_tensor(x1[:], bank[0][0:64, 0:128], rden1[:, 0:1], xb1[:], ALU.mult, ALU.add))

            moments(x1[:], 1, "mv1")
            dve.wait_ge(sig("const_loaded"), 16)
            v.tensor_scalar(bqh[:, 0:2], k("half"), col("L0_attn_bq"), None, ALU.mult).then_inc(sig("bqh"), 1)
            v.tensor_scalar(bqh[:, 2:4], k("half"), col("in_bq"), None, ALU.mult).then_inc(sig("bqh"), 1)
            own(v.tensor_copy(V2[:, :, 16], k("pair2")))
            own(v.tensor_copy(V3[:, :, 8], k("pair3")))
            dve.wait_ge(sig("rstd1"), 1)
            normed(xn[:], x1[:], 1, tiny[:, 7:8], "xn2")
            dve.wait_ge(*after("xnT2_ps"))
            v.tensor_scalar(xd2[:], over(bank[0][:, 0:64], 2), col("L0_attn_gamma"), col("L0_attn_beta"),
                            ALU.mult, ALU.add).then_inc(step("xd2"), 1)
            dve.wait_ge(*after("k2_ps"))
            own(v.tensor_scalar(KT2[:], bank[2][:, 0:64], col("L0_attn_bk"), None, ALU.add))
            v.tensor_tensor(Kb2[:], over(KT2[:], 4), each(k("head_k2"), 64), ALU.mult).then_inc(step("kb2"), 1)
            dve.wait_ge(*after("v2_ps"))
            v.tensor_tensor(V2[:, :, 0:16], bank[3][:, 0:128].rearrange("p (h g) -> p h g", g=16),
                            each(k("pair2"), 16), ALU.mult).then_inc(step("v2"), 1)
            dve.wait_ge(*after("s2_ps"))
            sview = bank[4][:, 0:256].rearrange("p (h t) -> p h t", t=64)
            own(v.reduce_max(mx2[:, 0:4], sview, AX))
            v.tensor_tensor(s2[:, 0:256].rearrange("p (h t) -> p h t", t=64), sview, each(mx2[:, 0:4], 64),
                            ALU.subtract).then_inc(step("s2"), 1)
            dve.wait_ge(*after("pt2_ps"))
            v.tensor_copy(PT2[:, 0:2, :].rearrange("p c q -> p (c q)"), bank[0][:, 0:256]).then_inc(step("pt2"), 1)
            dve.wait_ge(*after("att2_ps"))
            attv = bank[1][0:64, 0:136].rearrange("p (h g) -> p h g", g=17)
            own(v.reciprocal(rd2[:, 0:8], attv[:, :, 16]))
            own(v.tensor_tensor(att2[:].rearrange("p (h g) -> p h g", g=16), attv[:, :, 0:16],
                                each(rd2[:, 0:8], 16), ALU.mult))
            v.tensor_tensor(turned, att2[:].rearrange("p (h g) -> p h g", g=16).unsqueeze(2).broadcast_to([64, 8, 8, 16]),
                            k("turn", 64).unsqueeze(1).unsqueeze(3).broadcast_to([64, 8, 8, 16]),
                            ALU.mult).then_inc(step("turned"), 1)
            dve.wait_ge(*after("o2_ps"))
            own(v.tensor_tensor(x2[:], x1[:], bank[2][0:64, 0:128], ALU.add))

            moments(x2[:], 2, "mv2")
            dve.wait_ge(sig("w3_loaded"), 80)
            dve.wait_ge(sig("rstd2"), 1)
            normed(xf[:], x2[:], 2, tiny[:, 9:10], "xf")
            dve.wait_ge(*after("xf"))
            pairs = xf[:].rearrange("p (i two) -> p i two", two=2)
            sin = k("sin", 64).rearrange("p (i two) -> p i two", two=2)
            rb = rope_b[:].rearrange("p (i two) -> p i two", two=2)
            v.tensor_tensor(rb[:, :, 0], pairs[:, :, 1], sin[:, :, 0], ALU.mult)
            own(v.tensor_tensor(rb[:, :, 1], pairs[:, :, 0], sin[:, :, 1], ALU.mult))
            own(v.tensor_tensor(rope_a[:], xf[:], k("cos", 64), ALU.mult))
            v.tensor_tensor(qin[:], rope_a[:], rope_b[:], ALU.add).then_inc(step("qin"), 1)
            dve.wait_ge(*after("qinT_ps"))
            v.tensor_copy(qinT[:], bank[0][:, 0:64]).then_inc(step("qinT"), 1)
            dve.wait_ge(*after("k3_ps"))
            own(v.tensor_scalar(KT3[:], bank[3][:, 0:64], col("in_bk"), None, ALU.add))
            v.tensor_tensor(Kb3[:], over(KT3[:], 8), each(k("head_k3"), 64), ALU.mult).then_inc(step("kb3"), 1)
            v.tensor_tensor(V3[:, :, 0:8], bank[4][:, 0:128].rearrange("p (h g) -> p h g", g=8),
                            each(k("pair3"), 8), ALU.mult).then_inc(step("v3"), 1)
            dve.wait_ge(*after("s3_ps"))
            sview = bank[5][:, :].rearrange("p (h t) -> p h t", t=64)
            s2v = s2[:].rearrange("p (h t) -> p h t", t=64)
            s3v = s3[:].rearrange("p (h t) -> p h t", t=64)
            own(v.tensor_tensor(s2v, sview, over(k("causal"), 8), ALU.add))
            own(v.reduce_max(mx3[:], s2v, AX))
            v.tensor_tensor(s3v, s2v, each(mx3[:], 64), ALU.subtract).then_inc(step("s3"), 1)
            dve.wait_ge(*after("pt3_ps"))
            v.tensor_copy(PT3[:].rearrange("p c q -> p (c q)"), bank[0][:, :]).then_inc(step("pt3"), 1)
            dve.wait_ge(*after("att3_ps"))
            attv = bank[1][0:64, 0:144].rearrange("p (h g) -> p h g", g=9)
            own(v.reciprocal(rd3[:], attv[:, :, 8]))
            v.tensor_tensor(att3[:].rearrange("p (h g) -> p h g", g=8), attv[:, :, 0:8],
                            each(rd3[:], 8), ALU.mult).then_inc(step("att3"), 1)
            dve.wait_ge(*after("att3T_ps"))
            v.tensor_copy(attT3[:], bank[2][:, 0:64]).then_inc(step("attT3"), 1)
            dve.wait_ge(*after("proj3_ps"))
            dve.wait_ge(sig("xfb"), 1)
            own(v.tensor_tensor(z3[:], bank[3][0:64, 0:128], xfb[:], ALU.add))
            moments(z3[:], 3, "mv3")
            dve.wait_ge(*after("mv3"))
            own(v.scalar_tensor_tensor(za3[:], z3[:], mv[:, 3, 0:1], spread("L0_ffn_ln1_w"),
                                       ALU.subtract, ALU.mult))
            dve.wait_ge(sig("rstd3"), 1)
            v.scalar_tensor_tensor(y3[:], za3[:], tiny[:, 11:12], spread("L0_ffn_ln1_b"),
                                   ALU.mult, ALU.add).then_inc(step("y3"), 1)
            dve.wait_ge(*after("y3T_ps"))
            v.tensor_copy(y3T[:, 1, :], bank[4][:, 0:64]).then_inc(step("y3T"), 1)

            def top_two(lg, top, idx, idf, hot):
                own(v.max(top, lg))
                own(v.max_index(idx, top, lg))
                own(v.tensor_copy(idf, idx[:, 0:2]))
                v.tensor_scalar(hot[:, 0, :], k("iota8"), idf[:, 0:1], None, ALU.is_equal)
                own(v.tensor_scalar(hot[:, 1, :], k("iota8"), idf[:, 1:2], None, ALU.is_equal))

            dve.wait_ge(*after("lg3_ps"))
            own(v.tensor_copy(lg3[:], bank[5][:, 0:8]))
            top_two(lg3[:], top3[:], idx3[:], idf3[:], hot3)
            v.tensor_scalar(neg3[:], top3[:, 0:1], -1.0, None, ALU.mult).then_inc(step("neg3"), 1)
            own(v.tensor_tensor(hot3[:, 2, :], hot3[:, 0, :], hot3[:, 1, :], ALU.add))
            dve.wait_ge(sig("eg3"), 1)
            own(v.reciprocal(sum3[:, 1:2], sum3[:, 0:1]))
            own(v.scalar_tensor_tensor(hot3[:, 0, :], eg3[:], sum3[:, 1:2], hot3[:, 2, :], ALU.mult, ALU.mult))
            own(v.tensor_scalar(w4_3[:, 0, :], hot3[:, 0, 0:4], k("half")[:, 0:1], None, ALU.mult))
            own(v.scalar_tensor_tensor(w4_3[:, 1, :], hot3[:, 0, 4:8], k("half")[:, 1:2], w4_3[:, 0, :],
                                       ALU.mult, ALU.add))
            dve.wait_ge(*after("exp3_ps"))
            v.tensor_tensor(moe3[:], bank[0][:, :].rearrange("p (e f) -> p e f", e=4), each(w4_3[:, 1, :], 128),
                            ALU.mult).then_inc(step("moe3"), 1)
            dve.wait_ge(*after("z3b_ps"))
            moments(bank[1][0:64, 0:128], 4, "mv4")
            dve.wait_ge(*after("mv4"))
            own(v.scalar_tensor_tensor(zb3[:], bank[1][0:64, 0:128], mv[:, 4, 0:1], spread("L0_ffn_ln2_w"),
                                       ALU.subtract, ALU.mult))
            dve.wait_ge(sig("rstd4"), 1)
            dve.wait_ge(sig("x2b"), 1)
            v.scalar_tensor_tensor(x3[:], zb3[:], tiny[:, 13:14], x2b[:], ALU.mult, ALU.add).then_inc(step("x3"), 1)
            dve.wait_ge(*after("x3"))

            moments(x3[:], 5, "mv5")
            dve.wait_ge(sig("rstd5"), 1)
            normed(xn[:], x3[:], 5, tiny[:, 15:16], "xn4")
            dve.wait_ge(*after("xnT4_ps"))
            v.tensor_copy(xnT4[:], bank[2][:, 0:64]).then_inc(step("xnT4"), 1)

            def edge_max(g):
                dve.wait_ge(sig("edge4_scores"), g + 1)
                v.reduce_max(cm[:, :, 2 * CHUNKS], bank[6][:, 0:256].rearrange("p (q k) -> p q k", q=2), AX).then_inc(
                    sig("edge4_max"), 1)

            def strip_max(n, dst, b):
                dve.wait_ge(sig("strip_scores"), n + 1)
                v.reduce_max(dst, bank[b][:, :], AX).then_inc(sig("strip_max"), 1)

            def shift_columns(g):
                dve.wait_ge(sig("strip_max"), STRIPS * (g + 1))
                dve.wait_ge(sig("edge4_max"), g + 1)
                own4(v.reduce_max(m4[:], cm[:], AX), g, 1)
                if g:
                    dve.wait_ge(sig("shift_ps"), g)
                v.tensor_scalar(shiftcols[:], each(m4[:], 128), -1.0 / UP, HEADROOM * ROOT,
                                ALU.mult, ALU.add).then_inc(sig("shiftcols"), 1)

            def shift_rows(g):
                dve.wait_ge(sig("shift_ps"), g + 1)
                if g < LAST:
                    if g:
                        dve.wait_ge(sig("scores4_0"), BLOCKS * g)
                    v.tensor_copy(shiftrow[:], bank[7][0:1, 0:GROUP]).then_inc(sig("shiftrow"), 1)
                v.tensor_scalar(shift4[:], bank[7][:, 0:GROUP], UP, None, ALU.mult).then_inc(sig("shift4"), 1)
                dve.wait_ge(sig("shift4"), g + 1)

            def shifted(g, i, s, j, tiles=2):
                dve.wait_ge(sig(f"scores4_{j}"), nth(g, i, s, j))
                o = bank[2 * ((g + s) % 2) + j][:, 0:256 * tiles].rearrange("p (t q) -> p t q", t=tiles)
                v.tensor_tensor(o, o, over(shift4[:], tiles), ALU.add).then_inc(sig(f"shifted4_{j}"), 1)

            def own4(ins, g, n):
                ins.then_inc(sig("dve_shift"), 1)
                dve.wait_ge(sig("dve_shift"), g + n)

            def low(m, s, width=1024, before=None):
                dve.wait_ge(sig("prob4"), m + 1)
                if before is not None:
                    dve.wait_ge(sig("weighted_lo"), before)
                v.tensor_tensor(pl4[:, s, 0:width], P[:, s, 0:width], ph4[:, s, 0:width], ALU.subtract).then_inc(
                    sig("prob4_lo"), 1)

            def average(g):
                dve.wait_ge(sig("den4"), g + 1)
                if g:
                    dve.wait_ge(sig("y4_part"), g)
                v.reciprocal(rden4[:], bank[4 + g % 2][:, 256:512]).then_inc(sig("rden4"), 1)
                dve.wait_ge(sig("rden4"), g + 1)
                v.tensor_tensor(un4[:], bank[4 + g % 2][:, 0:256], rden4[:], ALU.mult).then_inc(sig("un4"), 1)

            def add_output(g):
                dve.wait_ge(sig("y4_part"), g + 1)
                if g == 0:
                    dve.wait_ge(sig("x3b"), 1)
                else:
                    dve.wait_ge(sig("x4_part"), g)
                v.tensor_tensor(x4[:], bank[4 + g % 2][0:64, 0:128], x4[:] if g else x3b[:], ALU.add).then_inc(
                    sig("x4_part"), 1)

            edge_max(0)
            with dve.Fori(0, CHUNKS) as i:
                for q in range(2):
                    for half in range(2):
                        strip_max(i * 4 + (2 * q + half), cm[:, q, bass.ds(i * 2 + half, 1)], 4 + 2 * q + half)
            shift_columns(0)
            shift_rows(0)

            def block4(g, s, i, low_width=1024):
                slot = (g + s) % 2
                m = i * 4 + (BANKS * g + 2 * s)
                strip = i * 4 + (STRIPS * (g + 1) + 2 * s)
                for j in vector_banks(g):
                    shifted(g, i, s, j)
                if g < LAST:
                    strip_max(strip, cm[:, s, bass.ds(i * 2, 1)], 6)
                    strip_max(strip + 1, cm[:, s, bass.ds(i * 2 + 1, 1)], 7)
                n = i * 2 + (BLOCKS * g + s)
                if low_width:
                    low(m - 1, 1 - slot, low_width, before=n - 2 if g or not isinstance(i, int) else None)

            for g in range(GROUPS):
                m0 = BANKS * g
                ahead = g + 1 < GROUPS
                if ahead:
                    edge_max(g + 1)
                block4(g, 0, 0, GROUP if g else 0)
                block4(g, 1, 0)
                if g:
                    average(g - 1)
                with dve.Fori(1, CHUNKS) as i:
                    for s in range(2):
                        block4(g, s, i)
                if ahead:
                    shift_columns(g + 1)
                if g == LAST:
                    shifted(g, CHUNKS, 0, 0, 1)
                low(m0 + BANKS - 2, (g + 1) % 2, before=BLOCKS * (g + 1) - 3)
                if ahead:
                    shift_rows(g + 1)
                if g:
                    add_output(g - 1)
            low(GROUPS * BANKS - 1, LAST % 2, GROUP, before=GROUPS * BLOCKS - 2)
            average(GROUPS - 1)
            add_output(GROUPS - 1)

            dve.wait_ge(sig("x4_part"), GROUPS)
            moments(x4[:], 6, "mv6")
            dve.wait_ge(sig("w5_loaded"), 16)
            own(v.tensor_scalar(gate5[:, 1:2], gate5[:, 0:1], 1.0, None, ALU.add))
            own(v.reciprocal(gate5[:, 2:3], gate5[:, 1:2]))
            v.tensor_scalar(wo5[:], w5[:, 3, :], gate5[:, 2:3], None, ALU.mult).then_inc(step("wo5"), 1)
            dve.wait_ge(sig("rstd6"), 1)
            normed(xn[:], x4[:], 6, tiny[:, 3:4], "xn5")
            dve.wait_ge(*after("xnT5_ps"))
            v.tensor_copy(xnT5[:], bank[0][:, 0:64]).then_inc(step("xnT5"), 1)
            dve.wait_ge(*after("kv5_ps"))
            v.tensor_scalar(tk5[:, 0, :], bank[2][0:64, 0:128], 0.0, None, ALU.min).then_inc(step("kmin5"), 1)
            v.tensor_copy(vv5[:, 0:128], bank[2][0:64, 128:256]).then_inc(step("vv5"), 1)
            dve.wait_ge(*after("q5_ps"))
            v.tensor_scalar(tq5[:, 0, :], bank[1][:, 0:64], col("L1_attn_bq"), 0.0, ALU.add, ALU.min).then_inc(
                step("qmin5"), 1)
            own(v.tensor_scalar(tq5[:, 1, :], bank[1][:, 0:64], col("L1_attn_bq"), 0.0, ALU.add, ALU.max))
            dve.wait_ge(sig("kexp5"), 1)
            v.scalar_tensor_tensor(k5[:], bank[2][0:64, 0:128], 0.0, tk5[:, 1, :], ALU.max, ALU.add).then_inc(
                step("k5"), 1)
            dve.wait_ge(sig("qexp5"), 1)
            v.tensor_tensor(q5[:], tq5[:, 1, :], tq5[:, 2, :], ALU.add).then_inc(step("q5"), 1)
            dve.wait_ge(*after("kvsum5_ps"))
            v.tensor_tensor(kv5[:], bank[6][:, 0:144], k("own_head"), ALU.mult).then_inc(step("kv5"), 1)
            dve.wait_ge(*after("num5_ps"))
            own(v.tensor_scalar(dn5[:, 0, :], bank[7][0:64, 128:144], 1e-6, None, ALU.add))
            own(v.reciprocal(dn5[:, 1, :], dn5[:, 0, :]))
            v.tensor_tensor(att5[:].rearrange("p (h g) -> p h g", g=8),
                            bank[7][0:64, 0:128].rearrange("p (h g) -> p h g", g=8),
                            each(dn5[:, 1, :], 8), ALU.mult).then_inc(step("att5"), 1)
            dve.wait_ge(*after("att5T_ps"))
            v.tensor_copy(attT5[:], bank[2][:, 0:64]).then_inc(step("attT5"), 1)
            dve.wait_ge(*after("o5_ps"))
            dve.wait_ge(sig("x4b"), 1)
            own(v.tensor_tensor(x5[:], bank[0][0:64, 0:128], x4b[:], ALU.add))

            moments(x5[:], 7, "mv7")
            dve.wait_ge(sig("rstd7"), 1)
            normed(xt6[:], x5[:], 7, tiny[:, 5:6], "xt6")
            dve.wait_ge(*after("xt6T_ps"))
            v.tensor_copy(xt6T[:, 1, :], bank[1][:, 0:64]).then_inc(step("xt6T"), 1)
            dve.wait_ge(*after("lg6_ps"))
            own(v.tensor_copy(lg6[:], bank[2][:, 0:8]))
            top_two(lg6[:], top6[:], idx6[:], idf6[:], hot6)
            v.tensor_tensor(d6[:, 0:1], top6[:, 1:2], top6[:, 0:1], ALU.subtract).then_inc(step("d6"), 1)
            dve.wait_ge(sig("e6"), 1)
            own(v.tensor_scalar(d6[:, 2:3], d6[:, 1:2], 1.0, None, ALU.add))
            own(v.reciprocal(d6[:, 3:4], d6[:, 2:3]))
            own(v.tensor_tensor(d6[:, 4:5], d6[:, 1:2], d6[:, 3:4], ALU.mult))
            own(v.tensor_scalar(hot6[:, 2, :], hot6[:, 0, :], d6[:, 3:4], None, ALU.mult))
            own(v.scalar_tensor_tensor(hot6[:, 0, :], hot6[:, 1, :], d6[:, 4:5], hot6[:, 2, :], ALU.mult, ALU.add))
            own(v.tensor_scalar(w4_6[:, 0, :], hot6[:, 0, 0:4], k("half")[:, 0:1], None, ALU.mult))
            v.scalar_tensor_tensor(w4_6[:, 1, :], hot6[:, 0, 4:8], k("half")[:, 1:2], w4_6[:, 0, :],
                                   ALU.mult, ALU.add).then_inc(step("w4_6"), 1)
            dve.wait_ge(*after("o6_ps"))
            zv = bank[5][:, :].rearrange("p (e f) -> p e f", e=4)
            for e in range(4):
                ins = v.bn_stats(st6[:, e, :], zv[:, e, :])
            own(ins)
            for e in range(4):
                ins = v.bn_aggr(mv6[:, e, :], st6[:, e, :])
            ins.then_inc(step("mv6e"), 1)
            dve.wait_ge(*after("mv6e"))
            own(v.tensor_tensor(o6a[:], zv, each(mv6[:, :, 0], 128), ALU.subtract))
            own(v.tensor_tensor(o6b[:], o6a[:], lng6[:].rearrange("p (e f) -> p e f", e=4), ALU.mult))
            dve.wait_ge(sig("rstd6e"), 1)
            v.tensor_tensor(o6c[:], o6b[:], each(w4_6[:, 2, :], 128), ALU.mult).then_inc(step("o6c"), 1)
            dve.wait_ge(*after("out6_ps"))
            v.tensor_tensor(x6[:], bank[6][0:64, 0:128], x5[:], ALU.add).then_inc(step("x6"), 1)

        @block.gpsimd
        def _(pool):
            g = nc.gpsimd
            count = [0]

            def own(ins):
                count[0] += 1
                ins.then_inc(sig("pool_own"), 1)
                pool.wait_ge(sig("pool_own"), count[0])

            def inverse_root(dst, tmp, var, eps, name, n=1):
                own(g.tensor_scalar(tmp, var, eps, None, ALU.add))
                g.tensor_tensor(dst, tmp, halfpow[0:dst.shape[0], 0:n], ALU.pow).then_inc(sig(name), 1)

            pool.wait_ge(*after("halfpow"))
            pool.wait_ge(*after("mv0"))
            inverse_root(tiny[:, 0:1], tiny[:, 1:2], mv[:, 0, 1:2], 1e-5, "rstd0")
            for c in range(CHUNKS + 1):
                n = CHUNK if c < CHUNKS else 1
                pool.wait_ge(sig("chunk_hi"), c + 1)
                g.tensor_tensor(ctx_lo[:, CHUNK * c:CHUNK * c + n, :], chunk[c % 4][:, 0:n, :],
                                ctx_hi[:, CHUNK * c:CHUNK * c + n, :], ALU.subtract).then_inc(sig("chunk_lo"), 1)
            for b in range(CHUNKS + 1):
                pool.wait_ge(sig("prob1"), b + 1)
                if b == 0:
                    own(g.tensor_copy(acc[:, 0, 0:512], p1[:, 0, :]))
                elif b < CHUNKS:
                    own(g.tensor_tensor(acc[:, 0, 0:512], acc[:, 0, 0:512], p1[:, b, :], ALU.add))
                else:
                    g.tensor_tensor(acc[:, 0, 0:64], acc[:, 0, 0:64], p1[:, b, 0:64], ALU.add).then_inc(
                        sig("acc1"), 1)
            pool.wait_ge(*after("mv1"))
            var = mv[:, 1, 1:2]
            own(g.tensor_scalar(tiny[:, 1:2], var, 1e-5, None, ALU.add))
            own(g.tensor_tensor(tiny[:, 2:3], tiny[:, 1:2], halfpow[0:64, 0:1], ALU.pow))
            own(g.tensor_tensor(tiny[:, 4:5], var, tiny[:, 2:3], ALU.mult))
            own(g.tensor_tensor(tiny[:, 4:5], tiny[:, 4:5], tiny[:, 2:3], ALU.mult))
            own(g.tensor_scalar(tiny[:, 4:5], tiny[:, 4:5], 1e-5, None, ALU.add))
            own(g.tensor_tensor(tiny[:, 6:7], tiny[:, 4:5], halfpow[0:64, 0:1], ALU.pow))
            g.tensor_tensor(tiny[:, 7:8], tiny[:, 6:7], tiny[:, 2:3], ALU.mult).then_inc(sig("rstd1"), 1)
            pool.wait_ge(*after("mv2"))
            inverse_root(tiny[:, 9:10], tiny[:, 8:9], mv[:, 2, 1:2], 1e-5, "rstd2")
            pool.wait_ge(sig("w3_loaded"), 80)
            pool.wait_ge(*after("xf"))
            g.tensor_tensor(xfb[:], xf[:], spread("L0_ffn_out_proj_b"), ALU.add).then_inc(sig("xfb"), 1)
            g.tensor_tensor(x2b[:], x2[:], spread("L0_ffn_ln2_b"), ALU.add).then_inc(sig("x2b"), 1)
            pool.wait_ge(*after("mv3"))
            inverse_root(tiny[:, 11:12], tiny[:, 10:11], mv[:, 3, 1:2], 1e-5, "rstd3")
            pool.wait_ge(*after("mv4"))
            inverse_root(tiny[:, 13:14], tiny[:, 12:13], mv[:, 4, 1:2], 1e-5, "rstd4")
            pool.wait_ge(*after("mv5"))
            inverse_root(tiny[:, 15:16], tiny[:, 14:15], mv[:, 5, 1:2], 1e-5, "rstd5")
            g.tensor_tensor(x3b[:], x3[:], spread("L1_xattn_proj_b"), ALU.add).then_inc(sig("x3b"), 1)

            for grp in range(GROUPS):
                pool.wait_ge(sig("qk4_32"), grp + 1)
                at = slice(GROUP * grp, GROUP * grp + GROUP)
                g.tensor_tensor(qk_lo[:, at], qk32[:, at], qk_hi[:, at], ALU.subtract).then_inc(sig("qk4_lo"), 1)
            pool.wait_ge(sig("qk4_lo"), GROUPS)

            def add_block(n, s, m, first=False, width=1024, to=0):
                pool.wait_ge(sig("prob4"), m + 1)
                a = acc[:, to, 0:width]
                if first:
                    g.tensor_copy(a, P[:, s, 0:width]).then_inc(sig("acc4"), 1)
                else:
                    pool.wait_ge(sig("acc4"), n)
                    g.tensor_tensor(a, a, P[:, s, 0:width], ALU.add).then_inc(sig("acc4"), 1)

            pool.wait_ge(sig("fold4_ps"), H4)
            g.memset(hz6[:], 0.0).then_inc(sig("hz6_zero"), 1)
            for grp in range(GROUPS):
                if grp >= 2:
                    pool.wait_ge(sig("den4"), grp - 1)
                n0, m0 = BLOCKS * grp, BANKS * grp
                add_block(n0, grp % 2, m0 + 1, first=True, to=grp % 2)
                add_block(n0 + 1, (grp + 1) % 2, m0 + 3, to=grp % 2)
                with pool.Fori(1, CHUNKS) as i:
                    for s in range(2):
                        add_block(i * 2 + (n0 + s), (grp + s) % 2, i * 4 + (m0 + 2 * s + 1), to=grp % 2)
                add_block(n0 + BLOCKS - 1, grp % 2, m0 + BANKS - 1, width=GROUP, to=grp % 2)
            pool.wait_ge(*after("mv6"))
            inverse_root(tiny[:, 3:4], tiny[:, 2:3], mv[:, 6, 1:2], 1e-5, "rstd6")
            g.tensor_tensor(x4b[:], x4[:], spread("L1_attn_bo"), ALU.add).then_inc(sig("x4b"), 1)
            pool.wait_ge(*after("mv7"))
            inverse_root(tiny[:, 5:6], tiny[:, 4:5], mv[:, 7, 1:2], 1e-5, "rstd7")
            pool.wait_ge(sig("w6_loaded"), 16 * 9)
            pool.wait_ge(*after("w4_6"))
            g.tensor_tensor(wb6[:], lnb6[:].rearrange("p (e f) -> p e f", e=4), each(w4_6[:, 1, :], 128),
                            ALU.mult).then_inc(sig("wb6"), 1)
            pool.wait_ge(*after("mv6e"))
            own(g.tensor_scalar(ve6[:, 0, :], mv6[:, :, 1], 1e-6, None, ALU.add))
            own(g.tensor_tensor(ve6[:, 1, :], ve6[:, 0, :], halfpow[:, 0:4], ALU.pow))
            g.tensor_tensor(w4_6[:, 2, :], ve6[:, 1, :], w4_6[:, 1, :], ALU.mult).then_inc(sig("rstd6e"), 1)

        @block.scalar
        def _(act):
            a = nc.scalar

            for c in range(CHUNKS + 1):
                n = CHUNK if c < CHUNKS else 1
                act.wait_ge(sig(f"ctx_loaded{c % 4}"), 16 * (c // 4 + 1))
                a.activation(ctx_hi[:, CHUNK * c:CHUNK * c + n, :], chunk[c % 4][:, 0:n, :], ACT.Copy).then_inc(
                    sig("chunk_hi"), 1)
                for j in range(0, n, 4):
                    m = min(4, n - j)
                    act.wait_ge(sig("chunk_half_transposed"), 2 * c + j // 4 + 1)
                    a.activation(ctxT_hi[:, CHUNK * c + j:CHUNK * c + j + m, :].rearrange("p t k -> p (t k)"),
                                 bank[2 * (c % 2) + j // 4][:, 0:128 * m], ACT.Copy, scale=CTX_UP).then_inc(
                        sig("chunkT_hi"), 1)
            SOFT = 1.0 / (ROOT * UP)
            for b in range(CHUNKS + 1):
                n = 512 if b < CHUNKS else 64
                act.wait_ge(sig("scores1"), b + 1)
                a.activation(P_hi[:, b, 0:n], bank[b][:, 0:n], ACT.Exp, scale=SOFT).then_inc(sig("prob1_hi"), 1)
                a.activation(p1[:, b, 0:n], bank[b][:, 0:n], ACT.Exp, scale=SOFT).then_inc(sig("prob1"), 1)
            a.activation(gate5[:, 0:1], col("stdp"), ACT.Exp, scale=-1.0).then_inc(sig("gate5"), 1)

            def fold_copy(*heads):
                both = big[:].rearrange("p (w h d) -> p h w d", w=2, h=H4)
                for h in heads:
                    act.wait_ge(sig("fold4_ps"), h + 1)
                    a.activation(both[:, h], bank[6 + h % 2][:, 0:256].rearrange("p (w d) -> p w d", w=2),
                                 ACT.Copy).then_inc(sig("fold4"), 1)

            fold_copy(0)
            act.wait_ge(sig("bqh"), 2)
            act.wait_ge(*after("q2_ps"))
            for f in range(2):
                ins = a.activation(Q2[:, f, :], bank[1][:, 0:64], ACT.Identity, bias=bqh[:, f:f + 1],
                                   scale=k("half")[:, f:f + 1])
            ins.then_inc(sig("q2"), 1)
            fold_copy(1, 2)
            act.wait_ge(*after("s2"))
            a.activation(e2[:, 0:256], s2[:, 0:256], ACT.Exp, scale=0.25).then_inc(sig("e2"), 1)
            fold_copy(3, 4, 5, 6, 7, 8, 9)

            act.wait_ge(*after("xfT_ps"))
            a.activation(xfT[:], over(bank[1][:, 0:64], 2), ACT.Copy).then_inc(sig("xfT"), 1)
            fold_copy(10)
            act.wait_ge(*after("q3_ps"))
            for f in range(2):
                ins = a.activation(Q3[:, f, :], bank[2][:, 0:64], ACT.Identity, bias=bqh[:, 2 + f:3 + f],
                                   scale=k("half")[:, f:f + 1])
            ins.then_inc(sig("q3"), 1)
            fold_copy(11, 12)
            act.wait_ge(*after("s3"))
            a.activation(e3[:], s3[:], ACT.Exp, scale=1.0 / math.sqrt(8.0)).then_inc(sig("e3"), 1)
            fold_copy(13, 14, 15)
            act.wait_ge(*after("neg3"))
            a.activation(eg3[:], lg3[:], ACT.Exp, bias=neg3[:, 0:1], accum_out=sum3[:, 0:1]).then_inc(sig("eg3"), 1)

            def queries4(grp):
                act.wait_ge(sig("qk4_ps"), grp + 1)
                at = slice(GROUP * grp, GROUP * grp + GROUP)
                a.activation(qk_hi[:, at], bank[grp][:, 0:GROUP], ACT.Copy, scale=QK_UP).then_inc(sig("qk4_hi"), 1)
                a.activation(qk32[:, at], bank[grp][:, 0:GROUP], ACT.Copy, scale=QK_UP).then_inc(sig("qk4_32"), 1)

            def exponentials(group, i, block, j, width=512):
                s = (group + block) % 2
                if j in vector_banks(group) and (group == LAST or width == 512):
                    act.wait_ge(sig(f"shifted4_{j}"), nth_shifted(group, i, block, j))
                else:
                    act.wait_ge(sig(f"scores4_{j}"), nth(group, i, block, j))
                at = slice(512 * j, 512 * j + width)
                a.activation(ph4[:, s, at], bank[2 * s + j][:, 0:width], ACT.Exp, scale=SOFT)
                a.activation(P[:, s, at], bank[2 * s + j][:, 0:width], ACT.Exp, scale=SOFT).then_inc(
                    sig("prob4"), 1)

            def used(n):
                act.wait_ge(sig("weighted_hi"), n - 1)
                act.wait_ge(sig("acc4"), n - 1)
                act.wait_ge(sig("prob4_lo"), n - 1)

            queries4(0)
            queries4(1)
            queries4(2)
            queries4(3)

            for grp in range(GROUPS):
                n0 = BLOCKS * grp
                for s in range(2):
                    if n0 + s >= 2:
                        used(n0 + s)
                    for j in range(2):
                        exponentials(grp, 0, s, j)
                with act.Fori(1, CHUNKS) as i:
                    for s in range(2):
                        used(i * 2 + (n0 + s))
                        for j in range(2):
                            exponentials(grp, i, s, j)
                used(n0 + BLOCKS - 1)
                exponentials(grp, CHUNKS, 0, 0, GROUP)

            act.wait_ge(*after("kmin5"))
            a.activation(tk5[:, 1, :], tk5[:, 0, :], ACT.Exp).then_inc(sig("kexp5"), 1)
            act.wait_ge(*after("qmin5"))
            a.activation(tq5[:, 2, :], tq5[:, 0, :], ACT.Exp).then_inc(sig("qexp5"), 1)
            a.preload_act_table(ACT.Gelu)
            act.wait_ge(sig("hz6_zero"), 1)
            for half in range(2):
                act.wait_ge(sig("h6_ps"), half + 1)
                a.activation(hz6[:, 8 * half:8 * half + 8, 64 * half:64 * half + 64],
                             bank[3 + half][:, :].rearrange("p (c t) -> p c t", t=64), ACT.Gelu).then_inc(
                    sig("hz6"), 1)
            act.wait_ge(*after("d6"))
            a.activation(d6[:, 1:2], d6[:, 0:1], ACT.Exp).then_inc(sig("e6"), 1)

        @block.tensor
        def _(pe):
            mm = nc.tensor.matmul

            def one(o, lhsT, rhs):
                return mm(o, lhsT, rhs, start=True, stop=True)

            pe.wait_ge(sig("w0_loaded"), 48)
            one(bank[4][:, 0:128], w0[:, 0, :], w0[:, 1, :])
            one(bank[4][:, 128:129], w0[:, 1, :], col("L0_xattn_bq")).then_inc(step("fold0"), 1)
            one(bank[5][:, 0:128], w0[:, 2, :], w0[:, 3, :])
            pe.wait_ge(*after("bvrep"))
            mm(bank[5][0:64, 128:256], bvrep[:], w0[:, 3, :], start=True, stop=False)
            pe.wait_ge(*after("ones"))
            mm(bank[5][0:64, 128:256], ones[0:1, 0:64], row("L0_xattn_bo"), start=False, stop=True).then_inc(
                step("fold0b"), 1)
            pe.wait_ge(sig("ident_loaded"), 16)
            pe.wait_ge(*after("xn1"))
            nc.tensor.transpose(bank[6][:, 0:64], xn[:], ident[0:64, 0:64]).then_inc(step("xnT1_ps"), 1)
            pe.wait_ge(*after("xnT1"))
            pe.wait_ge(*after("a0"))
            one(bank[7][:, 0:64], a0[:], xnT[:]).then_inc(step("qk1_ps"), 1)

            def transposes(c):
                n = CHUNK if c < CHUNKS else 1
                pe.wait_ge(sig(f"ctx_loaded{c % 4}"), 16 * (c // 4 + 1))
                if c >= 2:
                    pe.wait_ge(sig("chunkT_lo"), 2 * (c - 1))
                for j in range(n):
                    ins = nc.tensor.transpose(bank[2 * (c % 2) + j // 4][:, 128 * (j % 4):128 * (j % 4) + 128],
                                              chunk[c % 4][:, j, :], ident)
                    if j % 4 == 3 or n == 1:
                        ins.then_inc(sig("chunk_half_transposed"), 1)

            def scores1_hi(c):
                if c == 0:
                    pe.wait_ge(*after("qk1"))
                    pe.wait_ge(*after("b0"))
                    pe.wait_ge(*after("xb1"))
                if c >= 2:
                    pe.wait_ge(sig("max1_part"), c - 1)
                pe.wait_ge(sig("chunkT_hi"), 2 * c + (2 if c < CHUNKS else 1))
                b = bank[4 + c % 2]
                for half in range(2 if c < CHUNKS else 1):
                    t0 = CHUNK * c + 4 * half
                    n = 4 if c < CHUNKS else 1
                    ins = mm(b[64 * half:64 * half + 64, 0:128 * n], qk1_hi[:],
                             ctxT_hi[:, t0:t0 + n, :].rearrange("p t k -> p (t k)"), start=True, stop=True)
                ins.then_inc(sig("scores1_hi"), 1)

            transposes(0)
            for c in range(CHUNKS + 1):
                if c < CHUNKS:
                    transposes(c + 1)
                scores1_hi(c)
            pe.wait_ge(*after("max1"))
            one(bank[7][0:1, 0:128], m1[:], ident).then_inc(step("max1_row"), 1)
            pe.wait_ge(*after("shift1"))
            pe.wait_ge(*after("up16"))
            pe.wait_ge(sig("chunkT_lo"), 2 * CHUNKS + 1)

            def scores1(b):
                n = CHUNK if b < CHUNKS else 1
                whole = bank[b][:, 0:64 * n].rearrange("p (t q) -> p t q", q=64)
                mm(whole, up16[0:1, :], over(shift1[:], n), start=True, stop=False)
                for j in range(n):
                    o = bank[b][:, 64 * j:64 * j + 64]
                    tile = CHUNK * b + j
                    mm(o, ctxT_hi[:, tile, :], qk1_hi[:], start=False, stop=False)
                    mm(o, ctxT_hi[:, tile, :], qk1_lo[:], start=False, stop=False)
                    ins = mm(o, ctxT_lo[:, tile, :], qk1_hi[:], start=False, stop=(j == n - 1))
                ins.then_inc(sig("scores1"), 1)

            def weighted1(b):
                n = CHUNK if b < CHUNKS else 1
                pe.wait_ge(sig("prob1_hi"), b + 1)
                pe.wait_ge(sig("prob1_lo"), b + 1)
                for j in range(n):
                    tile = CHUNK * b + j
                    at = slice(64 * j, 64 * j + 64)
                    mm(bank[7][:, 0:64], ctx_hi[:, tile, :], P_hi[:, b, at], start=(tile == 0), stop=False)
                    mm(bank[7][:, 0:64], ctx_hi[:, tile, :], P_lo[:, b, at], start=False, stop=False)
                    ins = mm(bank[7][:, 0:64], ctx_lo[:, tile, :], P_hi[:, b, at], start=False,
                             stop=(tile == TILES - 1))
                return ins

            pe.wait_ge(sig("chunk_lo"), CHUNKS + 1)
            for b in range(CHUNKS + 3):
                if b <= CHUNKS:
                    scores1(b)
                if b >= 2:
                    ins = weighted1(b - 2)
            ins.then_inc(step("u1"), 1)
            pe.wait_ge(sig("acc1"), 1)
            for j in range(CHUNK):
                ins = mm(bank[1][0:64, 0:1], acc[:, 0, 64 * j:64 * j + 64], ones[:, 0:1], start=(j == 0),
                         stop=(j == CHUNK - 1))
            ins.then_inc(step("den1"), 1)
            pe.wait_ge(*after("UT"))
            one(bank[0][0:64, 0:128], UT[:], b0[:]).then_inc(step("y1"), 1)

            def fold4(*heads):
                for h in heads:
                    if h == 0:
                        pe.wait_ge(sig("w4_loaded"), 64)
                    if h >= 2:
                        pe.wait_ge(sig("fold4"), h - 1)
                    j, head = h // 2, slice(64 * (h % 2), 64 * (h % 2) + 64)
                    one(bank[6 + h % 2][:, 0:128], wq4t[head, j, :], wk4t[head, j, :])
                    one(bank[6 + h % 2][:, 128:256], wv4t[head, j, :], wp4t[head, j, :]).then_inc(
                        sig("fold4_ps"), 1)

            pe.wait_ge(sig("w2_loaded"), 32)
            pe.wait_ge(sig("wvg"), 2)
            mm(bank[3][:, 0:128], ones[0:1, :], bvg[:], start=True, stop=False)
            pe.wait_ge(*after("xn2"))
            nc.tensor.transpose(bank[0][:, 0:64], xn[:], ident[0:64, 0:64]).then_inc(step("xnT2_ps"), 1)
            fold4(0)
            pe.wait_ge(*after("xd2"))
            one(bank[2][:, 0:64], w2[:, 1, :], xd2[:, 0, :]).then_inc(step("k2_ps"), 1)
            one(bank[1][:, 0:64], w2[:, 0, :], xd2[:, 0, :]).then_inc(step("q2_ps"), 1)
            mm(bank[3][:, 0:128], xd2[:].rearrange("p i t -> p (i t)"), wvg[:], start=False, stop=True).then_inc(
                step("v2_ps"), 1)
            fold4(1)
            pe.wait_ge(*after("kb2"))
            pe.wait_ge(sig("q2"), 1)
            one(bank[4][:, 0:256], Q2[:].rearrange("p i t -> p (i t)"), Kb2[:].rearrange("p h t -> p (h t)")).then_inc(
                step("s2_ps"), 1)
            fold4(2, 3)
            pe.wait_ge(sig("e2"), 1)
            for c in range(2):
                ins = nc.tensor.transpose(bank[0][:, 128 * c:128 * c + 128], e2[:, 128 * c:128 * c + 128], ident)
            ins.then_inc(step("pt2_ps"), 1)
            fold4(4)
            pe.wait_ge(*after("pt2"))
            pe.wait_ge(*after("v2"))
            for f in range(2):
                for c in range(2):
                    h = 4 * f + 2 * c
                    ins = one(bank[1][0:64, 17 * h:17 * h + 34], PT2[:, c, 64 * f:64 * f + 64],
                              V2[:, h:h + 2, :].rearrange("p h g -> p (h g)"))
            ins.then_inc(step("att2_ps"), 1)
            fold4(5, 6, 7)
            pe.wait_ge(*after("turned"))
            for h in range(8):
                ins = mm(bank[2][0:64, 0:128], k("pick", 64)[:, 64 * h:64 * h + 64],
                         turned[:, h, :, :].rearrange("p b g -> p (b g)"), start=(h == 0), stop=(h == 7))
            ins.then_inc(step("o2_ps"), 1)
            fold4(8, 9)

            pe.wait_ge(sig("w3_loaded"), 80)
            mm(bank[4][:, 0:128], ones[0:1, :], row("in_bv"), start=True, stop=False)
            pe.wait_ge(*after("xf"))
            nc.tensor.transpose(bank[1][:, 0:64], xf[:], ident[0:64, 0:64]).then_inc(step("xfT_ps"), 1)
            fold4(10)
            pe.wait_ge(*after("qin"))
            nc.tensor.transpose(bank[0][:, 0:64], qin[:], ident[0:64, 0:64]).then_inc(step("qinT_ps"), 1)
            pe.wait_ge(sig("xfT"), 1)
            mm(bank[4][:, 0:128], xfT[:].rearrange("p i t -> p (i t)"), w3[:, 2, :], start=False, stop=True)
            pe.wait_ge(*after("qinT"))
            one(bank[3][:, 0:64], w3[:, 1, :], qinT[:]).then_inc(step("k3_ps"), 1)
            one(bank[2][:, 0:64], w3[:, 0, :], qinT[:]).then_inc(step("q3_ps"), 1)
            pe.wait_ge(*after("kb3"))
            pe.wait_ge(sig("q3"), 1)
            one(bank[5][:, :], Q3[:].rearrange("p i t -> p (i t)"), Kb3[:].rearrange("p h t -> p (h t)")).then_inc(
                step("s3_ps"), 1)
            fold4(11, 12, 13)
            pe.wait_ge(sig("e3"), 1)
            for c in range(4):
                ins = nc.tensor.transpose(bank[0][:, 128 * c:128 * c + 128], e3[:, 128 * c:128 * c + 128], ident)
            ins.then_inc(step("pt3_ps"), 1)
            fold4(14)
            pe.wait_ge(*after("pt3"))
            pe.wait_ge(*after("v3"))
            for f in range(2):
                for c in range(4):
                    h = 8 * f + 2 * c
                    ins = one(bank[1][0:64, 9 * h:9 * h + 18], PT3[:, c, 64 * f:64 * f + 64],
                              V3[:, h:h + 2, :].rearrange("p h g -> p (h g)"))
            ins.then_inc(step("att3_ps"), 1)
            pe.wait_ge(*after("att3"))
            nc.tensor.transpose(bank[2][:, 0:64], att3[:], ident[0:64, 0:64]).then_inc(step("att3T_ps"), 1)
            pe.wait_ge(*after("attT3"))
            one(bank[3][0:64, 0:128], attT3[:], w3[:, 3, :]).then_inc(step("proj3_ps"), 1)
            fold4(15)
            mm(bank[5][:, 0:8], ones[0:1, :], row("gate_b"), start=True, stop=False)
            mm(bank[0][:, :], k("halfrows", 2), eb3[:], start=True, stop=False)
            pe.wait_ge(*after("y3"))
            nc.tensor.transpose(bank[4][:, 0:64], y3[:], ident[0:64, 0:64]).then_inc(step("y3T_ps"), 1)
            pe.wait_ge(*after("y3T"))
            lower = y3T[:, 1:3, :].rearrange("p i t -> p (i t)")
            upper = y3T[:, 0:2, :].rearrange("p i t -> p (i t)")
            mm(bank[5][:, 0:8], lower, gate3[:], start=False, stop=False)
            mm(bank[5][:, 0:8], upper, gate3[:], start=False, stop=True).then_inc(step("lg3_ps"), 1)
            mm(bank[0][:, :], lower, ew3[:, 0:512], start=False, stop=False)
            mm(bank[0][:, :], upper, ew3[:, 512:1024], start=False, stop=True).then_inc(step("exp3_ps"), 1)
            mm(bank[1][0:64, 0:128], ident[0:64, 0:64], y3[:], start=True, stop=False)
            pe.wait_ge(*after("moe3"))
            for e in range(4):
                ins = mm(bank[1][0:64, 0:128], k("fold"), moe3[:, e, :], start=False, stop=(e == 3))
            ins.then_inc(step("z3b_ps"), 1)

            pe.wait_ge(*after("xn4"))
            nc.tensor.transpose(bank[2][:, 0:64], xn[:], ident[0:64, 0:64]).then_inc(step("xnT4_ps"), 1)
            pe.wait_ge(*after("xnT4"))
            pe.wait_ge(sig("fold4"), H4)

            def queries(g):
                for j in range(4):
                    ins = one(bank[g][:, 64 * j:64 * j + 64], a4[:, 4 * g + j, :], xnT4[:])
                ins.then_inc(sig("qk4_ps"), 1)

            queries(0)
            queries(1)

            ctxT = ctxT_hi[:].rearrange("p t k -> p (t k)")

            def edge_scores(g):
                for q in range(2):
                    a = GROUP * g + 128 * q
                    ins = mm(bank[6][:, 128 * q:128 * q + 128], qk_hi[:, a:a + 128], ctxT[:, CHUNKS * 1024:],
                             start=True, stop=True)
                ins.then_inc(sig("edge4_scores"), 1)

            def strip_scores(n, q, strip, g, b, free=None):
                if free is not None:
                    pe.wait_ge(sig("strip_max"), free)
                a = GROUP * g + 128 * q
                mm(bank[b][:, :], qk_hi[:, a:a + 128], ctxT[:, bass.ds(strip * 512, 512)], start=True,
                   stop=True).then_inc(sig("strip_scores"), 1)

            def turn_shifts(g):
                pe.wait_ge(sig("shiftcols"), g + 1)
                for q in range(2):
                    ins = mm(bank[7][:, 128 * q:128 * q + 128], shiftcols[:, q, :], ident16[:], start=True,
                             stop=True)
                ins.then_inc(sig("shift_ps"), 1)

            pe.wait_ge(sig("qk4_hi"), 1)
            pe.wait_ge(*after("ident16"))
            edge_scores(0)
            for half in range(2):
                strip_scores(half, 0, half, 0, 4 + half)
            queries(2)
            queries(3)
            pe.wait_ge(sig("edge4_max"), 1)
            for half in range(2):
                strip_scores(2 + half, 1, half, 0, 6 + half)
            with pe.Fori(1, CHUNKS) as i:
                for q in range(2):
                    for half in range(2):
                        n = i * 4 + (2 * q + half)
                        strip_scores(n, q, i * 2 + half, 0, 4 + 2 * q + half, free=n - 3)
            pe.wait_ge(sig("qk4_lo"), GROUPS)
            pe.wait_ge(sig("qk4_hi"), GROUPS)

            def scores4(s, tile, g, tiles=BLOCK, shift=True):
                hi, lo = (x[:, GROUP * g:GROUP * g + GROUP] for x in (qk_hi, qk_lo))
                for j in range(tiles):
                    o = bank[2 * s + j // 2][:, 256 * (j % 2):256 * (j % 2) + 256]
                    kh = ctxT_hi[:, bass.ds(tile + j, 1), :].rearrange("p t k -> p (t k)")
                    kl = ctxT_lo[:, bass.ds(tile + j, 1), :].rearrange("p t k -> p (t k)")
                    last = (j // 2 in vector_banks(g) and (g == LAST or tiles > 1)) and (j % 2 == 1 or tiles == 1)
                    mm(o, kh, hi, start=(j % 2 == 0), stop=False)
                    mm(o, kh, lo, start=False, stop=False)
                    ins = mm(o, kl, hi, start=False, stop=last)
                    if last:
                        ins.then_inc(sig(f"scores4_{j // 2}"), 1)
                if shift and g < LAST:
                    shift_by_row(s, tiles)

            def shift_by_row(s, tiles=BLOCK):
                w = min(2, tiles)
                mm(bank[2 * s][:, 0:256 * w].rearrange("p (t q) -> p t q", t=w), up16[0:1, :],
                   over(shiftrow[:], w), start=False, stop=True).then_inc(sig("scores4_0"), 1)

            def tiles4(x, tile, tiles):
                return [x[:, bass.ds(tile + j, 1), :].rearrange("p t k -> p (t k)") for j in range(tiles)]

            def weighted_hi(s, m, tile, g, tiles=BLOCK, first=False):
                pe.wait_ge(sig("prob4"), m)
                o = bank[4 + g % 2][:, 0:256]
                for j, (kh, kl) in enumerate(zip(tiles4(ctx_hi, tile, tiles), tiles4(ctx_lo, tile, tiles))):
                    at = slice(256 * j, 256 * j + 256)
                    mm(o, kh, ph4[:, s, at], start=(first and j == 0), stop=False)
                    ins = mm(o, kl, ph4[:, s, at], start=False, stop=False)
                ins.then_inc(sig("weighted_hi"), 1)

            def weighted_lo(s, n, tile, g, tiles=BLOCK, last=False):
                pe.wait_ge(sig("prob4_lo"), n + 1)
                for j, kh in enumerate(tiles4(ctx_hi, tile, tiles)):
                    ins = mm(bank[4 + g % 2][:, 0:256], kh, pl4[:, s, 256 * j:256 * j + 256], start=False,
                             stop=(last and j == tiles - 1))
                ins.then_inc(sig("weighted_lo"), 1)

            def finish4(g):
                pe.wait_ge(sig("acc4"), BLOCKS * (g + 1))
                for j in range(BLOCK):
                    ins = mm(bank[4 + g % 2][:, 256:512], ones[:], acc[:, g % 2, 256 * j:256 * j + 256],
                             start=(j == 0), stop=(j == BLOCK - 1))
                ins.then_inc(sig("den4"), 1)

            def output4(g):
                pe.wait_ge(sig("un4"), g + 1)
                for j in range(4):
                    h = 4 * g + j
                    ins = mm(bank[4 + g % 2][0:64, 0:128], un4[:, 64 * j:64 * j + 64], v4[:, h, :], start=(j == 0),
                             stop=(j == 3))
                ins.then_inc(sig("y4_part"), 1)

            for g in range(GROUPS):
                n0, m0 = BLOCKS * g, BANKS * g
                ahead = g + 1 < GROUPS
                even, odd = g % 2, (g + 1) % 2

                def strips(q, i):
                    for half in range(2 if ahead else 0):
                        n = i * 4 + (STRIPS * (g + 1) + 2 * q + half)
                        strip_scores(n, q, i * 2 + half, g + 1, 6 + half, free=n - 1)

                if g:
                    pe.wait_ge(sig("prob4"), m0 - 1)
                scores4(even, 0, g, shift=g > 0)
                if g == 0:
                    turn_shifts(0)
                    scores4(odd, 4, 0, shift=False)
                    pe.wait_ge(sig("shiftrow"), 1)
                    shift_by_row(even)
                    shift_by_row(odd)
                if ahead:
                    pe.wait_ge(sig("strip_max"), STRIPS * (g + 1))
                    edge_scores(g + 1)
                    pe.wait_ge(sig("edge4_max"), g + 2)
                    pe.wait_ge(sig("shift4"), g + 1)
                strips(0, 0)
                if g:
                    weighted_hi(odd, m0, TILES - 1, g - 1, 1)
                    weighted_lo(even, n0 - 2, TILES - 5, g - 1)
                    pe.wait_ge(sig("prob4"), m0)
                    scores4(odd, 4, g)
                strips(1, 0)
                if g >= 2:
                    pe.wait_ge(sig("x4_part"), g - 1)
                weighted_hi(even, m0 + 2, 0, g, first=True)
                if g:
                    weighted_lo(odd, n0 - 1, TILES - 1, g - 1, 1, last=True)
                    finish4(g - 1)

                def block4(s, i):
                    slot = (even, odd)[s]
                    n, m = i * 2 + (n0 + s), i * 4 + (m0 + 2 * s)
                    pe.wait_ge(sig("prob4"), m - 2)
                    scores4(slot, i * 8 + 4 * s, g)
                    strips(s, i)
                    weighted_hi(1 - slot, m, i * 8 + (4 * s - 4), g)
                    weighted_lo(slot, n - 2, i * 8 + (4 * s - 8), g)

                with pe.Fori(1, CHUNKS) as i:
                    for s in range(2):
                        block4(s, i)
                pe.wait_ge(sig("prob4"), m0 + BANKS - 3)
                scores4(even, TILES - 1, g, 1)
                if ahead:
                    turn_shifts(g + 1)
                if g:
                    output4(g - 1)
                weighted_hi(odd, m0 + BANKS - 1, TILES - 5, g)
                weighted_lo(even, n0 + BLOCKS - 3, TILES - 9, g)
                if g + 1 < LAST:
                    pe.wait_ge(sig("shiftrow"), g + 2)
            weighted_hi(LAST % 2, BANKS * GROUPS, TILES - 1, LAST, 1)
            weighted_lo(1 - LAST % 2, BLOCKS * GROUPS - 2, TILES - 5, LAST)
            weighted_lo(LAST % 2, BLOCKS * GROUPS - 1, TILES - 1, LAST, 1, last=True)
            finish4(LAST)
            output4(LAST)

            pe.wait_ge(sig("w6_loaded"), 16 * 9)
            for half in range(2):
                mm(bank[3 + half][:, :].rearrange("p (c t) -> p c t", t=64), b16[:],
                   each(ident[0:16, 8 * half:8 * half + 8], 64), start=True, stop=False)
            pe.wait_ge(sig("w5_loaded"), 16)
            mm(bank[2][0:64, 0:128], ones[0:1, 0:64], row("L1_attn_bk"), start=True, stop=False)
            pe.wait_ge(*after("xn5"))
            nc.tensor.transpose(bank[0][:, 0:64], xn[:], ident[0:64, 0:64]).then_inc(step("xnT5_ps"), 1)
            mm(bank[5][:, :], k("halfrows", 2), b26[:], start=True, stop=False)
            pe.wait_ge(*after("xnT5"))
            mm(bank[2][0:64, 0:128], xnT5[:], w5[:, 1, :], start=False, stop=True)
            mm(bank[2][0:64, 128:256], ones[0:1, 0:64], row("L1_attn_bv"), start=True, stop=False)
            mm(bank[2][0:64, 128:256], xnT5[:], w5[:, 2, :], start=False, stop=True).then_inc(step("kv5_ps"), 1)
            one(bank[1][:, 0:64], w5[:, 0, :], xnT5[:]).then_inc(step("q5_ps"), 1)
            pe.wait_ge(*after("k5"))
            pe.wait_ge(*after("vv5"))
            one(bank[6][:, 0:144], k5[:], vv5[:]).then_inc(step("kvsum5_ps"), 1)
            pe.wait_ge(*after("kv5"))
            pe.wait_ge(*after("q5"))
            one(bank[7][0:64, 0:144], q5[:], kv5[:]).then_inc(step("num5_ps"), 1)
            pe.wait_ge(*after("att5"))
            nc.tensor.transpose(bank[2][:, 0:64], att5[:], ident[0:64, 0:64]).then_inc(step("att5T_ps"), 1)
            pe.wait_ge(*after("attT5"))
            pe.wait_ge(*after("wo5"))
            one(bank[0][0:64, 0:128], attT5[:], wo5[:]).then_inc(step("o5_ps"), 1)

            pe.wait_ge(*after("xt6"))
            nc.tensor.transpose(bank[1][:, 0:64], xt6[:], ident[0:64, 0:64]).then_inc(step("xt6T_ps"), 1)
            pe.wait_ge(*after("xt6T"))
            lower = xt6T[:, 1:3, :].rearrange("p i t -> p (i t)")
            upper = xt6T[:, 0:2, :].rearrange("p i t -> p (i t)")
            for half in range(2):
                for c in range(8):
                    e, f = 4 * half + c // 2, c % 2
                    ins = mm(bank[3 + half][:, 64 * c:64 * c + 64], w16[:, e, 128 * f:128 * f + 128],
                             xt6T[:, 1, :], start=False, stop=(c == 7))
                ins.then_inc(sig("h6_ps"), 1)
            mm(bank[2][:, 0:8], lower, gate6[:], start=True, stop=False)
            mm(bank[2][:, 0:8], upper, gate6[:], start=False, stop=True).then_inc(step("lg6_ps"), 1)
            mm(bank[5][:, :].rearrange("p (e f) -> p e f", e=4), k("dup", 64), over(xt6[:], 4), start=False,
               stop=False)
            for half in range(2):
                pe.wait_ge(sig("hz6"), half + 1)
                for c in range(8):
                    e, f = c // 2, c % 2
                    ins = mm(bank[5][:, 128 * e:128 * e + 128], hz6[:, 8 * half + c, :],
                             w26[:, 4 * half + e, f, :], start=False, stop=(half == 1 and c == 7))
            ins.then_inc(step("o6_ps"), 1)
            pe.wait_ge(sig("wb6"), 1)
            for e in range(4):
                mm(bank[6][0:64, 0:128], k("fold"), wb6[:, e, :], start=(e == 0), stop=False)
            pe.wait_ge(*after("o6c"))
            for e in range(4):
                ins = mm(bank[6][0:64, 0:128], k("fold"), o6c[:, e, :], start=False, stop=(e == 3))
            ins.then_inc(step("out6_ps"), 1)


BLOCKS = (TILES + BLOCK - 1) // BLOCK
BANKS = (TILES + 1) // 2
STRIPS = 4 * CHUNKS
LAST = GROUPS - 1


def vector_banks(g):
    return (0, 1) if g == LAST else (1,)


def nth(g, i, s, j):
    return i * 2 + ((BLOCKS - j) * g + s + 1)


def nth_shifted(g, i, s, j):
    return nth(0 if j == 0 else g, i, s, j)


def kernel(debug=False, **inputs):
    import numpy as _np
    import concourse.bacc as _bacc
    from concourse import mybir as _mybir
    from concourse.bass_utils import run_bass_kernel_spmd as _run

    a = {n: _np.asarray(v) for n, v in inputs.items()}

    def stack(*xs):
        return _np.stack(xs, 1)

    def pairs(w):
        return w.reshape(8, 2, 128, 64).transpose(1, 3, 0, 2).reshape(128, 8, 128)

    wqkv = a["L0_ffn_in_proj_w"]
    bqkv = a["L0_ffn_in_proj_b"]
    vectors = dict(a, in_bq=bqkv[0:128], in_bk=bqkv[128:256], in_bv=bqkv[256:384], gate_b=a["L0_ffn_gate_b"],
                   stdp=_np.repeat(a["L1_attn_stdp"], 8))
    lay = {
        "x": a["x"][0], "ctx": a["ctx_1024"][0], "const": CONST,
        "cols": _np.stack([vectors[n] for n in COLS], 1),
        "rows": _np.concatenate([vectors[n] for n in ROWS])[None],
        "wide": _np.broadcast_to(_np.stack([vectors[n] for n in WIDE])[None], (64, len(WIDE), 128)),
        "w0": stack(a["L0_xattn_Wq"], a["L0_xattn_Wk"], a["L0_xattn_Wv"], a["L0_xattn_Wo"].T),
        "w2": stack(a["L0_attn_Wq"], a["L0_attn_Wk"]),
        "L0_attn_Wv": a["L0_attn_Wv"],
        "w3": stack(wqkv[0:128].T, wqkv[128:256].T, wqkv[256:384].T, a["L0_ffn_out_proj_w"].T),
        "gate3": a["L0_ffn_gate_w"].T,
        "ew3": a["L0_ffn_expert_w"].transpose(2, 0, 1).reshape(128, 1024),
        "eb3": a["L0_ffn_expert_b"].reshape(2, 512),
        "wq4t": pairs(a["L1_xattn_w_q"]), "wk4t": pairs(a["L1_xattn_w_k"]), "wv4t": pairs(a["L1_xattn_w_v"]),
        "wp4t": a["L1_xattn_proj_w"].reshape(128, 8, 128).transpose(2, 1, 0),
        "w5": stack(a["L1_attn_Wq"].T, a["L1_attn_Wk"].T, a["L1_attn_Wv"].T, a["L1_attn_Wo"].T),
        "L1_ffn_gate_w": a["L1_ffn_gate_w"],
        "w16": a["L1_ffn_w1"].transpose(1, 0, 2),
        "w26": a["L1_ffn_w2"].reshape(8, 2, 128, 128).transpose(2, 0, 1, 3),
        "b16": a["L1_ffn_b1"].reshape(16, 128), "b26": a["L1_ffn_b2"].reshape(2, 512),
        "lng6": a["L1_ffn_ln_g"].reshape(2, 512), "lnb6": a["L1_ffn_ln_b"].reshape(2, 512),
    }
    nc = _bacc.Bacc("TRN2", target_bir_lowering=False, num_devices=1)
    arrays, t = {}, {}
    for name, v in lay.items():
        v = _np.ascontiguousarray(v)
        arrays[f"in_{name}"] = v
        t[name] = nc.dram_tensor(f"in_{name}", v.shape, _mybir.dt.from_np(v.dtype), kind="ExternalInput").ap()
    out = nc.dram_tensor("out", (64, 128), _mybir.dt.float32, kind="ExternalOutput").ap()
    dbg = [nc.dram_tensor(f"dbg{i}", (64, 128), _mybir.dt.float32, kind="ExternalOutput").ap()
           for i in range(5)] if debug else None
    build(nc, t, out, dbg)
    r = _run(nc, [arrays], core_ids=[0])
    got = r.results[0]["out"].reshape(1, 64, 128)
    if debug:
        return (got,) + tuple(r.results[0][f"dbg{i}"].reshape(1, 64, 128) for i in range(5))
    return got
```

```python
import math
import numpy as np
import concourse.bass as bass
from concourse import mybir
from contextlib import ExitStack

Q = 64
D = 128
KEYS = 6272
TILES = KEYS // D
CHUNK = 8
CHUNKS = TILES // CHUNK
H4 = 16
GROUP = 256
GROUPS = H4 * Q // GROUP
BLOCK = 4
E = 8

STEPS = {
    "vector_step": [
        "halfpow", "ones", "up16", "mv0", "bvrep", "xn1", "ident16", "a0", "b0", "xb1", "xnT1", "qk1", "max1",
        "shift1", "UT", "mv1", "xn2", "xd2", "kb2", "v2", "s2", "pt2", "turned", "mv2", "xf", "qin", "qinT",
        "kb3", "v3", "s3", "pt3", "att3", "attT3", "mv3", "y3", "y3T", "neg3", "wf3", "mv4", "x3", "mv5",
        "xn4", "xnT4", "mv6", "wo5", "xn5", "xnT5", "kmin5", "qmin5", "vv5", "k5", "q5", "kv5", "att5",
        "attT5", "mv7", "xt6", "xt6T", "d6", "w4_6", "mv6e", "ve6", "o6b", "wf6", "x6",
    ],
    "tensor_step": [
        "fold0", "fold0b", "xnT1_ps", "qk1_ps", "max1_row", "u1", "den1", "y1", "xnT2_ps", "k2_ps", "q2_ps",
        "v2_ps", "s2_ps", "pt2_ps", "att2_ps", "o2_ps", "xfT_ps", "qinT_ps", "k3_ps", "q3_ps", "s3_ps",
        "pt3_ps", "att3_ps", "att3T_ps", "proj3_ps", "y3T_ps", "lg3_ps", "exp3_ps", "z3b_ps", "xnT4_ps",
        "xnT5_ps", "k5_ps", "q5_ps", "v5_ps", "kvsum5_ps", "num5_ps", "att5T_ps", "o5_ps", "xt6T_ps", "lg6_ps",
        "o6_ps", "out6_ps",
    ],
}

CTX_UP = 64.0
QK_UP = 16.0
UP = CTX_UP * QK_UP
HEADROOM = 5.0
ROOT = math.sqrt(float(D))


def constants():
    p = np.arange(128)
    parts = {}
    parts["ident"] = np.eye(128)
    parts["fold"] = (p[:, None] % 64 == np.arange(64)[None])
    parts["half"] = (p[:, None] // 64 == np.arange(2)[None])
    parts["head_k2"] = ((p[:, None] // 16) % 4 == np.arange(4)[None])
    parts["head_k3"] = ((p[:, None] // 8) % 8 == np.arange(8)[None])
    parts["pair2"] = (p[:, None] // 64 == np.arange(8)[None] % 2)
    parts["pair3"] = (p[:, None] // 64 == np.arange(16)[None] % 2)
    own = np.zeros((128, 144))
    own[:, :128] = p[:, None] // 8 == p[None] // 8
    own[:, 128:] = p[:, None] // 8 == np.arange(16)[None]
    parts["own_head"] = own
    t = np.arange(64)
    parts["causal"] = np.where(t[None] <= (p[:, None] % 64), 0.0, -1e30)
    parts["iota8"] = np.tile(np.arange(8), (128, 1))
    halfrows = np.zeros((128, 128))
    halfrows[0, :64] = 1
    halfrows[1, 64:] = 1
    parts["halfrows"] = halfrows
    dup = np.zeros((128, 128))
    dup[:64] = np.concatenate([np.eye(64), np.eye(64)], 1)
    parts["dup"] = dup
    inv = (1.0 / np.float32(10000.0) ** (np.arange(0, 8, 2, dtype=np.float32) / np.float32(8))).astype(np.float32)
    f = (t.astype(np.float32)[:, None] * inv[None]).astype(np.float32)
    cos, sin = np.zeros((128, 128)), np.zeros((128, 128))
    cos[:64] = np.tile(np.repeat(np.cos(f), 2, axis=1), (1, 16))
    sin[:64] = np.tile(np.stack([-np.sin(f), np.sin(f)], -1).reshape(64, 8), (1, 16))
    parts["cos"], parts["sin"] = cos, sin
    turn = np.zeros((128, 8))
    turn[:64] = t[:, None] % 8 == np.arange(8)[None]
    parts["turn"] = turn
    pick = np.zeros((128, 8, 64))
    for s in range(64):
        for h in range(8):
            pick[s, h, h * 8 + s // 8] = 1
    parts["pick"] = pick.reshape(128, 512)
    at, where = 0, {}
    for name, a in parts.items():
        where[name] = (at, at + a.shape[1])
        at += a.shape[1]
    return np.ascontiguousarray(np.concatenate(list(parts.values()), 1).astype(np.float32)), where


CONST, AT = constants()
EARLY = AT["half"][0]

COLS = ["L0_xattn_bq", "L0_xattn_bv", "L0_attn_gamma", "L0_attn_beta", "L0_attn_bq", "L0_attn_bk",
        "in_bq", "in_bk", "L1_attn_bq", "stdp"]
ROWS = {"L0_xattn_bo": 128, "L0_attn_bv": 1024, "in_bv": 128, "gate_b": 8, "L1_attn_bk": 128, "L1_attn_bv": 128}
WIDE = ["L0_ffn_out_proj_b", "L0_ffn_ln1_w", "L0_ffn_ln1_b", "L0_ffn_ln2_w", "L0_ffn_ln2_b",
        "L1_xattn_proj_b", "L1_attn_bo"]


def build(nc, t, out):
    f32, f16, u32 = mybir.dt.float32, mybir.dt.float16, mybir.dt.uint32
    ALU = mybir.AluOpType
    ACT = mybir.ActivationFunctionType
    AX = mybir.AxisListType.X

    with ExitStack() as ctx:
        def sb(name, shape, dt=f32):
            return ctx.enter_context(nc.sbuf_tensor(name, shape, dt))

        sems = {}

        def sig(name):
            if name not in sems:
                sems[name] = ctx.enter_context(nc.semaphore(name))
            return sems[name]

        made = {name: 0 for name in STEPS}

        def counter(name):
            return next(c for c, names in STEPS.items() if name in names)

        def step(name):
            c = counter(name)
            assert STEPS[c][made[c]] == name, (name, STEPS[c][made[c]])
            made[c] += 1
            return sig(c)

        def after(name):
            return sig(counter(name)), STEPS[counter(name)].index(name) + 1

        bank = [ctx.enter_context(nc.psum_tensor(f"bank{i}", [128, 512], f32)) for i in range(8)]

        const = sb("const", list(CONST.shape))

        def k(name, rows=128):
            a, b = AT[name]
            return const[0:rows, a:b]

        ident = k("ident")
        x0 = sb("x0", [64, D])
        cols = sb("cols", [128, len(COLS)])
        rows = sb("rows", [1, sum(ROWS.values())])
        wide = sb("wide", [64, len(WIDE), D])

        def col(name):
            return cols[:, COLS.index(name):COLS.index(name) + 1]

        def row(name):
            names = list(ROWS)
            a = sum(ROWS[n] for n in names[:names.index(name)])
            return rows[0:1, a:a + ROWS[name]]

        def spread(name):
            return wide[:, WIDE.index(name), :]

        w0 = sb("w0", [128, 4, D])
        w2 = sb("w2", [128, 2, D])
        wv2 = sb("wv2", [128, 1024])
        w3 = sb("w3", [128, 4, D])
        gate3 = sb("gate3", [128, E])
        ew3 = sb("ew3", [128, E * D])
        eb3 = sb("eb3", [2, 512])
        w4 = sb("w4", [128, 4, 8, D])
        wq4t, wk4t, wv4t, wp4t = (w4[:, i] for i in range(4))
        w5 = sb("w5", [128, 4, D])
        gate6 = sb("gate6", [128, E])
        w16 = sb("w16", [128, E, 256])
        w26 = sb("w26", [128, E, 2, D])
        b16 = sb("b16", [16, D])
        b26 = sb("b26", [2, 512])
        lng6 = sb("lng6", [128, 512])
        lnb6 = sb("lnb6", [128, 512])

        ctx32 = sb("ctx32", [128, 2, CHUNK, D])
        late = w26[:].rearrange("p (c e) f d -> p c (e f) d", c=2)
        chunk = [ctx32[:, 0], ctx32[:, 1], late[:, 0], late[:, 1]]
        ctx_hi = sb("ctx_hi", [128, TILES, D], f16)
        ctx_lo = sb("ctx_lo", [128, TILES, D], f16)
        ctxT_hi = sb("ctxT_hi", [128, TILES, D], f16)
        ctxT_lo = sb("ctxT_lo", [128, TILES, D], f16)
        ones = sb("ones", [128, 128])
        up16 = sb("up16", [128, 128], f16)
        halfpow = sb("halfpow", [128, 4])

        block = ctx.enter_context(nc.Block())

        xn = sb("xn", [64, D])
        stat = sb("stat", [64, 8, 6])
        mv = sb("mv", [64, 8, 2])
        tiny = sb("tiny", [64, 16])
        xb1 = sb("xb1", [64, D])
        a0 = sb("a0", [128, D])
        c0 = sb("c0", [128, 1])
        b0 = sb("b0", [128, D])
        bvrep = sb("bvrep", [128, 64])
        xnT = sb("xnT", [128, 64])
        qkf = sb("qkf", [128, 64])
        qk1_hi = sb("qk1_hi", [128, 64], f16)
        qk1_lo = sb("qk1_lo", [128, 64], f16)
        cm1 = sb("cm1", [128, 8])
        m1 = sb("m1", [128, 1])
        mrow1 = sb("mrow1", [1, 64])
        shift1 = sb("shift1", [1, 64], f16)
        prob = sb("prob", [128, 8192], f16)
        P_hi = prob[:, 0:3584].rearrange("p (b n) -> p b n", b=7)
        P_lo = prob[:, 3584:7168].rearrange("p (b n) -> p b n", b=7)
        ph4 = prob[:, 0:2048].rearrange("p (s n) -> p s n", s=2)
        pl4 = prob[:, 2048:4096].rearrange("p (s n) -> p s n", s=2)
        P = prob[:, 4096:8192].bitcast(f32).rearrange("p (s n) -> p s n", s=2)
        big = sb("big", [128, 2 * H4 * D])
        p1 = big[:, 0:3584].rearrange("p (b n) -> p b n", b=7)
        a4 = big[:, 0:2048].rearrange("p (h d) -> p h d", h=H4)
        v4 = big[:, 2048:4096].rearrange("p (h d) -> p h d", h=H4)
        acc = sb("acc", [128, 2, 1024])
        UT = sb("UT", [128, 64])
        rden1 = sb("rden1", [64, 1])
        x1 = sb("x1", [64, D])
        wvg = sb("wvg", [128, D])
        bvg = sb("bvg", [1, D])
        xd2 = sb("xd2", [128, 2, 64])
        bqh = sb("bqh", [128, 4])
        Q2 = sb("Q2", [128, 2, 64])
        KT2 = sb("KT2", [128, 64])
        Kb2 = P[:, 0, 0:256].rearrange("p (h t) -> p h t", h=4)
        V2 = sb("V2", [128, 8, 17])
        mx2 = sb("mx2", [128, 8])
        s2, s3, e2, e3 = (ctx32[:, i // 2, 4 * (i % 2):4 * (i % 2) + 4, :].rearrange("p t d -> p (t d)")
                          for i in range(4))
        PT2, PT3 = (acc[:, 1, 512 * i:512 * i + 512].rearrange("p (c q) -> p c q", c=4) for i in range(2))
        rd2 = sb("rd2", [64, 16])
        att2 = sb("att2", [64, D])
        turned = acc[0:64, 0, :].rearrange("p (h b g) -> p h b g", h=8, b=8)
        x2 = sb("x2", [64, D])
        xf = sb("xf", [64, D])
        rope_a = sb("rope_a", [64, D])
        rope_b = sb("rope_b", [64, D])
        qin = sb("qin", [64, D])
        qinT = sb("qinT", [128, 64])
        xfT = sb("xfT", [128, 2, 64])
        Q3 = sb("Q3", [128, 2, 64])
        KT3 = sb("KT3", [128, 64])
        Kb3 = P[:, 0, 512:1024].rearrange("p (h t) -> p h t", h=8)
        V3 = sb("V3", [128, 16, 9])
        mx3 = sb("mx3", [128, 8])
        rd3 = sb("rd3", [64, 16])
        att3 = sb("att3", [64, D])
        attT3 = sb("attT3", [128, 64])
        xfb = sb("xfb", [64, D])
        z3 = sb("z3", [64, D])
        za3 = sb("za3", [64, D])
        y3 = sb("y3", [64, D])
        y3T = sb("y3T", [128, 3, 64])
        lg3 = sb("lg3", [128, 8])
        top3 = sb("top3", [128, 8])
        idx3 = sb("idx3", [128, 8], u32)
        idf3 = sb("idf3", [128, 2])
        neg3 = sb("neg3", [128, 1])
        eg3 = sb("eg3", [128, 8])
        sum3 = sb("sum3", [128, 2])
        hot3 = sb("hot3", [128, 3, 8])
        w4_3 = sb("w4_3", [128, 2, 4])
        exp3 = P[:, 1, 0:512].rearrange("p (e f) -> p e f", e=4)
        wf3 = P[:, 1, 512:768].rearrange("p (e t) -> p e t", e=4)
        zb3 = sb("zb3", [64, D])
        x2b = sb("x2b", [64, D])
        x3 = sb("x3", [64, D])
        xnT4 = sb("xnT4", [128, 64])
        qk_hi = sb("qk_hi", [128, H4 * Q], f16)
        qk_lo = sb("qk_lo", [128, H4 * Q], f16)
        qk32 = acc[:, 0, :]
        pair = ctx32[:, 0].bitcast(f16).rearrange("p t d -> p (t d)").rearrange("p (s k) -> p s k", s=2)
        best = ctx32[:, 1, 0:4].bitcast(f16).rearrange("p t d -> p (t d)")
        cm = sb("cm", [128, 2, 2 * CHUNKS + 1])
        m4 = sb("m4", [128, 2])
        shiftcols = sb("shiftcols", [128, 2, 128], f16)
        shiftrow = sb("shiftrow", [1, GROUP], f16)
        shift4 = sb("shift4", [128, GROUP])
        rden4 = sb("rden4", [64, 4])
        u4 = sb("u4", [128, GROUP])
        ident16 = sb("ident16", [128, 128], f16)
        x3b = sb("x3b", [64, D])
        x4 = sb("x4", [64, D])
        wo5 = sb("wo5", [128, D])
        gate5 = sb("gate5", [128, 4])
        tq5 = sb("tq5", [128, 3, 64])
        q5 = sb("q5", [128, 64])
        tk5 = sb("tk5", [64, 2, D])
        k5 = sb("k5", [64, D])
        vv5 = sb("vv5", [64, 144])
        kv5 = sb("kv5", [128, 144])
        dn5 = sb("dn5", [64, 2, 16])
        att5 = sb("att5", [64, D])
        attT5 = sb("attT5", [128, 64])
        xnT5 = sb("xnT5", [128, 64])
        x4b = sb("x4b", [64, D])
        x5 = sb("x5", [64, D])
        xt6 = sb("xt6", [64, D])
        xt6T = sb("xt6T", [128, 3, 64])
        hz6 = w4[:, 0:2].rearrange("p i h d -> p (i h) d")
        o6 = w4[:, 2:4].rearrange("p i (j h) d -> p (i j) h d", j=2)
        lg6 = sb("lg6", [128, 8])
        top6 = sb("top6", [128, 8])
        idx6 = sb("idx6", [128, 8], u32)
        idf6 = sb("idf6", [128, 2])
        d6 = sb("d6", [128, 5])
        hot6 = sb("hot6", [128, 3, 8])
        w4_6 = sb("w4_6", [128, 3, 4])
        st6 = sb("st6", [128, 4, 6])
        mv6 = sb("mv6", [128, 4, 2])
        ve6 = sb("ve6", [128, 2, 4])
        o6b, wb6 = o6[:, 0], o6[:, 1]
        wf6 = o6[:, 2, 0:2].rearrange("p h (i t) -> p (h i) t", t=64)
        x6 = sb("x6", [64, D])

        def over(ap, n):
            return ap.unsqueeze(1).broadcast_to([ap.shape[0], n, ap.shape[1]])

        def each(ap, n):
            return ap.unsqueeze(2).broadcast_to([ap.shape[0], ap.shape[1], n])

        def sums_place(g):
            return bank[4 + g % 2][0:64, 256:260] if g < LAST else bank[0][0:64, 0:4]

        @block.sync
        def _(sp):
            def load(dst, name, ready):
                sp.dma_start(dst, t[name]).then_inc(sig(ready), 16)

            sp.dma_start(x0[:], t["x"]).then_inc(sig("x_loaded"), 16)
            sp.dma_start(const[:, 0:EARLY], t["const"][:, 0:EARLY]).then_inc(sig("ident_loaded"), 16)
            load(cols[:], "cols", "w0_loaded")
            load(w0[:], "w0", "w0_loaded")
            load(rows[:], "rows", "w0_loaded")
            view = t["ctx"].rearrange("(p t) d -> p t d", t=TILES)
            for c in range(CHUNKS + 1):
                n = CHUNK if c < CHUNKS else TILES - CHUNK * CHUNKS
                if c >= 4:
                    sp.wait_ge(sig("chunk_half_transposed"), 2 * (c - 3))
                    sp.wait_ge(sig("chunk_lo"), c - 3)
                sp.dma_start(chunk[c % 4][:, 0:n, :], view[:, CHUNK * c:CHUNK * c + n, :]).then_inc(
                    sig(f"ctx_loaded{c % 4}"), 16)
            sp.dma_start(const[:, EARLY:], t["const"][:, EARLY:]).then_inc(sig("const_loaded"), 16)
            load(w2[:], "w2", "w2_loaded")
            load(wv2[:], "L0_attn_Wv", "w2_loaded")
            load(wide[:], "wide", "w3_loaded")
            load(w3[:], "w3", "w3_loaded")
            load(gate3[:], "gate3", "w3_loaded")
            load(ew3[:], "ew3", "w3_loaded")
            load(eb3[:], "eb3", "w3_loaded")
            load(wq4t[:], "wq4t", "w4_loaded")
            load(wk4t[:], "wk4t", "w4_loaded")
            load(wv4t[:], "wv4t", "w4_loaded")
            load(wp4t[:], "wp4t", "w4_loaded")
            load(w5[:], "w5", "w5_loaded")
            load(gate6[:], "L1_ffn_gate_w", "w6_loaded")
            load(w16[:], "w16", "w6_loaded")
            sp.wait_ge(sig("chunk_half_transposed"), 2 * CHUNKS + 1)
            sp.wait_ge(sig("chunk_lo"), CHUNKS + 1)
            load(w26[:], "w26", "w6_loaded")
            load(b16[:], "b16", "w6_loaded")
            load(b26[:], "b26", "w6_loaded")
            for half in range(2):
                for dst, name in ((lng6, "lng6"), (lnb6, "lnb6")):
                    sp.dma_start(dst[64 * half:64 * half + 64, :],
                                 t[name][half:half + 1, :].broadcast_to([64, 512])).then_inc(sig("w6_loaded"), 16)
            sp.wait_ge(*after("x6"))
            sp.dma_start(out, x6[:]).then_inc(sig("stored"), 16)
            sp.wait_ge(sig("stored"), 16)

        @block.vector
        def _(dve):
            v = nc.vector
            count = [0]

            def own(ins):
                count[0] += 1
                ins.then_inc(sig("dve_own"), 1)
                dve.wait_ge(sig("dve_own"), count[0])

            def moments(src, s, name):
                own(v.bn_stats(stat[:, s, :], src))
                v.bn_aggr(mv[:, s, :], stat[:, s, :]).then_inc(step(name), 1)

            def normed(dst, src, s, scale, name):
                v.tensor_scalar(dst, src, mv[:, s, 0:1], scale, ALU.subtract, ALU.mult).then_inc(step(name), 1)

            v.memset(halfpow[:], -0.5).then_inc(step("halfpow"), 1)
            v.memset(ones[:], 1.0).then_inc(step("ones"), 1)
            v.memset(up16[:], UP).then_inc(step("up16"), 1)
            own(v.memset(cm1[:], -3.0e38))
            v.memset(y3T[:], 0.0).then_inc(sig("zeros"), 1)
            v.memset(xt6T[:], 0.0).then_inc(sig("zeros"), 1)
            own(v.memset(vv5[:], 1.0))

            dve.wait_ge(sig("x_loaded"), 16)
            moments(x0[:], 0, "mv0")
            dve.wait_ge(sig("w0_loaded"), 48)
            v.reduce_sum(bvg[:], row("L0_attn_bv").rearrange("p (e j) -> p e j", j=8), AX).then_inc(sig("wvg"), 1)
            v.tensor_copy(bvrep[:], col("L0_xattn_bv").broadcast_to([128, 64])).then_inc(step("bvrep"), 1)
            dve.wait_ge(sig("rstd0"), 1)
            normed(xn[:], x0[:], 0, tiny[:, 0:1], "xn1")
            dve.wait_ge(sig("ident_loaded"), 16)
            v.tensor_copy(ident16[:], ident).then_inc(step("ident16"), 1)
            dve.wait_ge(*after("fold0"))
            v.tensor_copy(a0[:], bank[4][:, 0:128])
            v.tensor_copy(c0[:], bank[4][:, 128:129]).then_inc(step("a0"), 1)
            dve.wait_ge(*after("a0"))
            dve.wait_ge(*after("fold0b"))
            v.tensor_copy(b0[:], bank[5][:, 0:128]).then_inc(step("b0"), 1)
            v.tensor_tensor(xb1[:], x0[:], bank[5][0:64, 128:256], ALU.add).then_inc(step("xb1"), 1)
            dve.wait_ge(*after("xnT1_ps"))
            v.tensor_copy(xnT[:], bank[6][:, 0:64]).then_inc(step("xnT1"), 1)
            dve.wait_ge(*after("qk1_ps"))
            own(v.tensor_scalar(qkf[:], bank[7][:, 0:64], c0[:, 0:1], QK_UP, ALU.add, ALU.mult))
            own(v.tensor_copy(qk1_hi[:], qkf[:]))
            v.tensor_tensor(qk1_lo[:], qkf[:], qk1_hi[:], ALU.subtract).then_inc(step("qk1"), 1)

            def split_lo(c, n):
                for j in range(0, n, 4):
                    m = min(4, n - j)
                    b = bank[2 * (c % 2) + j // 4]
                    dve.wait_ge(sig("chunkT_hi"), 2 * c + j // 4 + 1)
                    v.scalar_tensor_tensor(
                        ctxT_lo[:, CHUNK * c + j:CHUNK * c + j + m, :].rearrange("p t k -> p (t k)"),
                        b[:, 0:128 * m], CTX_UP,
                        ctxT_hi[:, CHUNK * c + j:CHUNK * c + j + m, :].rearrange("p t k -> p (t k)"),
                        ALU.mult, ALU.subtract).then_inc(sig("chunkT_lo"), 1)

            for c in range(CHUNKS + 1):
                split_lo(c, CHUNK if c < CHUNKS else 1)
                dve.wait_ge(sig("scores1_hi"), c + 1)
                if c < CHUNKS:
                    ins = v.reduce_max(cm1[:, c:c + 1], bank[4 + c % 2][:], AX)
                else:
                    ins = v.reduce_max(cm1[0:64, c:c + 1], bank[4 + c % 2][0:64, 0:128], AX)
                ins.then_inc(sig("max1_part"), 1)
            dve.wait_ge(sig("max1_part"), CHUNKS + 1)
            v.reduce_max(m1[:], cm1[:], AX).then_inc(step("max1"), 1)
            dve.wait_ge(*after("max1_row"))
            own(v.reduce_max(mrow1[:], bank[7][0:1, 0:128].rearrange("p (h q) -> p q h", h=2), AX))
            v.tensor_scalar(shift1[:], mrow1[:], -1.0 / UP, HEADROOM * ROOT, ALU.mult, ALU.add).then_inc(
                step("shift1"), 1)
            dve.wait_ge(sig("w2_loaded"), 32)
            v.reduce_sum(wvg[:], wv2[:].rearrange("p (e j) -> p e j", j=8), AX).then_inc(sig("wvg"), 1)
            for b in range(CHUNKS + 1):
                n = 512 if b < CHUNKS else 64
                dve.wait_ge(sig("prob1"), b + 1)
                v.tensor_tensor(P_lo[:, b, 0:n], p1[:, b, 0:n], P_hi[:, b, 0:n], ALU.subtract).then_inc(
                    sig("prob1_lo"), 1)
            dve.wait_ge(*after("u1"))
            v.tensor_copy(UT[:], bank[7][:, 0:64]).then_inc(step("UT"), 1)
            dve.wait_ge(*after("den1"))
            own(v.reciprocal(rden1[:], bank[1][0:64, 0:1]))
            dve.wait_ge(*after("y1"))
            own(v.scalar_tensor_tensor(x1[:], bank[0][0:64, 0:128], rden1[:, 0:1], xb1[:], ALU.mult, ALU.add))

            moments(x1[:], 1, "mv1")
            dve.wait_ge(sig("const_loaded"), 16)
            v.tensor_scalar(bqh[:, 0:2], k("half"), col("L0_attn_bq"), None, ALU.mult).then_inc(sig("bqh"), 1)
            v.tensor_scalar(bqh[:, 2:4], k("half"), col("in_bq"), None, ALU.mult).then_inc(sig("bqh"), 1)
            own(v.tensor_copy(V2[:, :, 16], k("pair2")))
            own(v.tensor_copy(V3[:, :, 8], k("pair3")))
            dve.wait_ge(sig("rstd1"), 1)
            normed(xn[:], x1[:], 1, tiny[:, 7:8], "xn2")
            dve.wait_ge(*after("xnT2_ps"))
            v.tensor_scalar(xd2[:], over(bank[0][:, 0:64], 2), col("L0_attn_gamma"), col("L0_attn_beta"),
                            ALU.mult, ALU.add).then_inc(step("xd2"), 1)
            dve.wait_ge(*after("k2_ps"))
            own(v.tensor_scalar(KT2[:], bank[2][:, 0:64], col("L0_attn_bk"), None, ALU.add))
            v.tensor_tensor(Kb2[:], over(KT2[:], 4), each(k("head_k2"), 64), ALU.mult).then_inc(step("kb2"), 1)
            dve.wait_ge(*after("v2_ps"))
            v.tensor_tensor(V2[:, :, 0:16], bank[3][:, 0:128].rearrange("p (h g) -> p h g", g=16),
                            each(k("pair2"), 16), ALU.mult).then_inc(step("v2"), 1)
            dve.wait_ge(*after("s2_ps"))
            sview = bank[4][:, 0:256].rearrange("p (h t) -> p h t", t=64)
            own(v.reduce_max(mx2[:, 0:4], sview, AX))
            v.tensor_tensor(s2[:, 0:256].rearrange("p (h t) -> p h t", t=64), sview, each(mx2[:, 0:4], 64),
                            ALU.subtract).then_inc(step("s2"), 1)
            dve.wait_ge(*after("pt2_ps"))
            v.tensor_copy(PT2[:, 0:2, :].rearrange("p c q -> p (c q)"), bank[0][:, 0:256]).then_inc(step("pt2"), 1)
            dve.wait_ge(*after("att2_ps"))
            attv = bank[1][0:64, 0:136].rearrange("p (h g) -> p h g", g=17)
            own(v.reciprocal(rd2[:, 0:8], attv[:, :, 16]))
            own(v.tensor_tensor(att2[:].rearrange("p (h g) -> p h g", g=16), attv[:, :, 0:16],
                                each(rd2[:, 0:8], 16), ALU.mult))
            v.tensor_tensor(turned, att2[:].rearrange("p (h g) -> p h g", g=16).unsqueeze(2).broadcast_to([64, 8, 8, 16]),
                            k("turn", 64).unsqueeze(1).unsqueeze(3).broadcast_to([64, 8, 8, 16]),
                            ALU.mult).then_inc(step("turned"), 1)
            dve.wait_ge(*after("o2_ps"))
            own(v.tensor_tensor(x2[:], x1[:], bank[2][0:64, 0:128], ALU.add))

            moments(x2[:], 2, "mv2")
            dve.wait_ge(sig("w3_loaded"), 80)
            dve.wait_ge(sig("rstd2"), 1)
            normed(xf[:], x2[:], 2, tiny[:, 9:10], "xf")
            dve.wait_ge(*after("xf"))
            pairs = xf[:].rearrange("p (i two) -> p i two", two=2)
            sin = k("sin", 64).rearrange("p (i two) -> p i two", two=2)
            rb = rope_b[:].rearrange("p (i two) -> p i two", two=2)
            v.tensor_tensor(rb[:, :, 0], pairs[:, :, 1], sin[:, :, 0], ALU.mult)
            own(v.tensor_tensor(rb[:, :, 1], pairs[:, :, 0], sin[:, :, 1], ALU.mult))
            own(v.tensor_tensor(rope_a[:], xf[:], k("cos", 64), ALU.mult))
            v.tensor_tensor(qin[:], rope_a[:], rope_b[:], ALU.add).then_inc(step("qin"), 1)
            dve.wait_ge(*after("qinT_ps"))
            v.tensor_copy(qinT[:], bank[0][:, 0:64]).then_inc(step("qinT"), 1)
            dve.wait_ge(*after("k3_ps"))
            own(v.tensor_scalar(KT3[:], bank[3][:, 0:64], col("in_bk"), None, ALU.add))
            v.tensor_tensor(Kb3[:], over(KT3[:], 8), each(k("head_k3"), 64), ALU.mult).then_inc(step("kb3"), 1)
            v.tensor_tensor(V3[:, :, 0:8], bank[4][:, 0:128].rearrange("p (h g) -> p h g", g=8),
                            each(k("pair3"), 8), ALU.mult).then_inc(step("v3"), 1)
            dve.wait_ge(*after("s3_ps"))
            sview = bank[5][:, :].rearrange("p (h t) -> p h t", t=64)
            s2v = s2[:].rearrange("p (h t) -> p h t", t=64)
            s3v = s3[:].rearrange("p (h t) -> p h t", t=64)
            own(v.tensor_tensor(s2v, sview, over(k("causal"), 8), ALU.add))
            own(v.reduce_max(mx3[:], s2v, AX))
            v.tensor_tensor(s3v, s2v, each(mx3[:], 64), ALU.subtract).then_inc(step("s3"), 1)
            dve.wait_ge(*after("pt3_ps"))
            v.tensor_copy(PT3[:].rearrange("p c q -> p (c q)"), bank[0][:, :]).then_inc(step("pt3"), 1)
            dve.wait_ge(*after("att3_ps"))
            attv = bank[1][0:64, 0:144].rearrange("p (h g) -> p h g", g=9)
            own(v.reciprocal(rd3[:], attv[:, :, 8]))
            v.tensor_tensor(att3[:].rearrange("p (h g) -> p h g", g=8), attv[:, :, 0:8],
                            each(rd3[:], 8), ALU.mult).then_inc(step("att3"), 1)
            dve.wait_ge(*after("att3T_ps"))
            v.tensor_copy(attT3[:], bank[2][:, 0:64]).then_inc(step("attT3"), 1)
            dve.wait_ge(*after("proj3_ps"))
            dve.wait_ge(sig("xfb"), 1)
            own(v.tensor_tensor(z3[:], bank[3][0:64, 0:128], xfb[:], ALU.add))
            moments(z3[:], 3, "mv3")
            dve.wait_ge(*after("mv3"))
            own(v.scalar_tensor_tensor(za3[:], z3[:], mv[:, 3, 0:1], spread("L0_ffn_ln1_w"),
                                       ALU.subtract, ALU.mult))
            dve.wait_ge(sig("rstd3"), 1)
            v.scalar_tensor_tensor(y3[:], za3[:], tiny[:, 11:12], spread("L0_ffn_ln1_b"),
                                   ALU.mult, ALU.add).then_inc(step("y3"), 1)
            dve.wait_ge(*after("y3T_ps"))
            v.tensor_copy(y3T[:, 1, :], bank[4][:, 0:64]).then_inc(step("y3T"), 1)

            def top_two(lg, top, idx, idf, hot):
                own(v.max_index(idx, top, lg))
                own(v.tensor_copy(idf, idx[:, 0:2]))
                v.tensor_scalar(hot[:, 0, :], k("iota8"), idf[:, 0:1], None, ALU.is_equal)
                own(v.tensor_scalar(hot[:, 1, :], k("iota8"), idf[:, 1:2], None, ALU.is_equal))

            dve.wait_ge(*after("lg3_ps"))
            own(v.tensor_copy(lg3[:], bank[5][:, 0:8]))
            own(v.max(top3[:], lg3[:]))
            v.tensor_scalar(neg3[:], top3[:, 0:1], -1.0, None, ALU.mult).then_inc(step("neg3"), 1)
            top_two(lg3[:], top3[:], idx3[:], idf3[:], hot3)
            own(v.tensor_tensor(hot3[:, 2, :], hot3[:, 0, :], hot3[:, 1, :], ALU.add))
            dve.wait_ge(sig("eg3"), 1)
            own(v.reciprocal(sum3[:, 1:2], sum3[:, 0:1]))
            own(v.scalar_tensor_tensor(hot3[:, 0, :], eg3[:], sum3[:, 1:2], hot3[:, 2, :], ALU.mult, ALU.mult))
            own(v.tensor_scalar(w4_3[:, 0, :], hot3[:, 0, 0:4], k("half")[:, 0:1], None, ALU.mult))
            own(v.scalar_tensor_tensor(w4_3[:, 1, :], hot3[:, 0, 4:8], k("half")[:, 1:2], w4_3[:, 0, :],
                                       ALU.mult, ALU.add))
            v.tensor_tensor(wf3, over(k("fold"), 4), each(w4_3[:, 1, :], 64), ALU.mult).then_inc(step("wf3"), 1)
            dve.wait_ge(*after("z3b_ps"))
            moments(bank[1][0:64, 0:128], 4, "mv4")
            dve.wait_ge(*after("mv4"))
            own(v.scalar_tensor_tensor(zb3[:], bank[1][0:64, 0:128], mv[:, 4, 0:1], spread("L0_ffn_ln2_w"),
                                       ALU.subtract, ALU.mult))
            dve.wait_ge(sig("rstd4"), 1)
            dve.wait_ge(sig("x2b"), 1)
            v.scalar_tensor_tensor(x3[:], zb3[:], tiny[:, 13:14], x2b[:], ALU.mult, ALU.add).then_inc(step("x3"), 1)
            dve.wait_ge(*after("x3"))

            moments(x3[:], 5, "mv5")
            dve.wait_ge(sig("rstd5"), 1)
            normed(xn[:], x3[:], 5, tiny[:, 15:16], "xn4")
            dve.wait_ge(*after("xnT4_ps"))
            v.tensor_copy(xnT4[:], bank[2][:, 0:64]).then_inc(step("xnT4"), 1)

            def edge_max(g, b=6):
                dve.wait_ge(sig("edge4_scores"), g + 1)
                v.reduce_max(cm[:, :, 2 * CHUNKS], bank[b][:, 0:256].rearrange("p (q k) -> p q k", q=2), AX).then_inc(
                    sig("edge4_max"), 1)

            def strip_max(n, dst, b):
                dve.wait_ge(sig("strip_scores"), n + 1)
                v.reduce_max(dst, bank[b][:, :], AX).then_inc(sig("strip_max"), 1)

            def shift_columns(g):
                dve.wait_ge(sig("strip_max"), STRIPS * g + FIRST)
                dve.wait_ge(sig("edge4_max"), g + 1)
                if g:
                    own(v.reduce_max(m4[:], cm[:], AX))
                else:
                    own(v.tensor_tensor(best[:, 0:512], best[:, 0:512], best[:, 512:1024], ALU.max))
                    own(v.reduce_max(cm[:, 0, 0:1], best[:, 0:512], AX))
                    v.scalar_tensor_tensor(m4[:, 0:1], cm[:, 0, 0:1], UP, cm[:, 0, 2 * CHUNKS:], ALU.mult, ALU.max)
                    own(v.reduce_max(m4[:, 1:2], cm[:, 1, :], AX))
                if g:
                    dve.wait_ge(sig("shift_ps"), g)
                v.tensor_scalar(shiftcols[:], each(m4[:], 128), -1.0 / UP, HEADROOM * ROOT,
                                ALU.mult, ALU.add).then_inc(sig("shiftcols"), 1)

            def shift_rows(g):
                dve.wait_ge(sig("shift_ps"), g + 1)
                if g < LAST:
                    if g:
                        dve.wait_ge(sig("scores4_0"), BLOCKS * g)
                    v.tensor_copy(shiftrow[:], bank[7][0:1, 0:GROUP]).then_inc(sig("shiftrow"), 1)
                v.tensor_scalar(shift4[:], bank[7][:, 0:GROUP], UP, None, ALU.mult).then_inc(sig("shift4"), 1)
                dve.wait_ge(sig("shift4"), g + 1)

            def shifted(g, i, s, j, tiles=2):
                dve.wait_ge(sig(f"scores4_{j}"), nth(g, i, s, j))
                o = bank[2 * ((g + s) % 2) + j][:, 0:256 * tiles].rearrange("p (t q) -> p t q", t=tiles)
                v.tensor_tensor(o, o, over(shift4[:], tiles), ALU.add).then_inc(sig(f"shifted4_{j}"), 1)

            def low(m, s, width=1024, before=None):
                dve.wait_ge(sig("prob4"), m + 1)
                if before is not None:
                    dve.wait_ge(sig("weighted_lo"), before)
                v.tensor_tensor(pl4[:, s, 0:width], P[:, s, 0:width], ph4[:, s, 0:width], ALU.subtract).then_inc(
                    sig("prob4_lo"), 1)

            def denominators(g):
                dve.wait_ge(sig("den4"), g + 1)
                if g:
                    dve.wait_ge(sig("x4_part"), 4 * g)
                v.reciprocal(rden4[:], sums_place(g)).then_inc(sig("rden4"), 1)

            def add_output(g, heads=range(4)):
                dve.wait_ge(sig("y4_part"), g + 1)
                dve.wait_ge(sig("rden4"), g + 1)
                if g == 0:
                    dve.wait_ge(sig("x3b"), 1)
                for j in heads:
                    if g or j:
                        dve.wait_ge(sig("x4_part"), 4 * g + j)
                    v.scalar_tensor_tensor(x4[:], bank[4 + g % 2][0:64, 128 * j:128 * j + 128], rden4[:, j:j + 1],
                                           x4[:] if g or j else x3b[:], ALU.mult, ALU.add).then_inc(
                        sig("x4_part"), 1)

            edge_max(0, 3)
            for half in range(2):
                strip_max(half, cm[:, 1, half:half + 1], 6 + half)
            for i in range(1, CHUNKS):
                for half in range(2):
                    strip_max(i * 2 + half, cm[:, 1, 2 * i + half:2 * i + half + 1], 6 + half)
                dve.wait_ge(sig("first_copied"), i * 2 + 2)
                if i > 1:
                    dve.wait_ge(sig("compared"), i - 1)
                v.tensor_tensor(best[:], best[:], pair[:, i % 2], ALU.max).then_inc(sig("compared"), 1)
            dve.wait_ge(sig("compared"), CHUNKS - 1)
            shift_columns(0)
            shift_rows(0)

            def block4(g, s, i, low_width=1024):
                slot = (g + s) % 2
                m = i * 4 + (BANKS * g + 2 * s)
                strip = i * 4 + (STRIPS * g + FIRST + 2 * s)
                for j in vector_banks(g):
                    shifted(g, i, s, j)
                if g < LAST:
                    strip_max(strip, cm[:, s, bass.ds(i * 2, 1)], 6)
                    strip_max(strip + 1, cm[:, s, bass.ds(i * 2 + 1, 1)], 7)
                n = i * 2 + (BLOCKS * g + s)
                if low_width:
                    low(m - 1, 1 - slot, low_width, before=n - 2 if g or not isinstance(i, int) else None)

            for g in range(GROUPS):
                m0 = BANKS * g
                ahead = g + 1 < GROUPS
                block4(g, 0, 0, GROUP if g else 0)
                block4(g, 1, 0)
                if ahead:
                    edge_max(g + 1)
                if g:
                    denominators(g - 1)
                block4(g, 0, 1)
                block4(g, 1, 1)
                if g:
                    add_output(g - 1, range(2 if g == LAST else 4))
                with dve.Fori(2, CHUNKS) as i:
                    for s in range(2):
                        block4(g, s, i)
                if g == LAST:
                    add_output(g - 1, range(2, 4))
                if ahead:
                    shift_columns(g + 1)
                if g == LAST:
                    shifted(g, CHUNKS, 0, 0, 1)
                if ahead:
                    shift_rows(g + 1)
                low(m0 + BANKS - 2, (g + 1) % 2, before=BLOCKS * (g + 1) - 3)
            low(GROUPS * BANKS - 1, LAST % 2, GROUP, before=GROUPS * BLOCKS - 2)
            dve.wait_ge(sig("acc4"), BLOCKS * GROUPS)
            a = acc[:, LAST % 2, :]
            own(v.tensor_tensor(a[:, 0:512], a[:, 0:512], a[:, 512:1024], ALU.add))
            v.tensor_tensor(a[:, 0:256], a[:, 0:256], a[:, 256:512], ALU.add).then_inc(sig("sums4"), 1)
            denominators(LAST)
            add_output(LAST)

            dve.wait_ge(sig("x4_part"), 4 * GROUPS)
            moments(x4[:], 6, "mv6")
            dve.wait_ge(sig("w5_loaded"), 16)
            own(v.tensor_scalar(gate5[:, 1:2], gate5[:, 0:1], 1.0, None, ALU.add))
            own(v.reciprocal(gate5[:, 2:3], gate5[:, 1:2]))
            v.tensor_scalar(wo5[:], w5[:, 3, :], gate5[:, 2:3], None, ALU.mult).then_inc(step("wo5"), 1)
            dve.wait_ge(sig("rstd6"), 1)
            normed(xn[:], x4[:], 6, tiny[:, 3:4], "xn5")
            dve.wait_ge(*after("xnT5_ps"))
            v.tensor_copy(xnT5[:], bank[0][:, 0:64]).then_inc(step("xnT5"), 1)
            dve.wait_ge(*after("k5_ps"))
            v.tensor_scalar(tk5[:, 0, :], bank[2][0:64, 0:128], 0.0, None, ALU.min).then_inc(step("kmin5"), 1)
            dve.wait_ge(*after("q5_ps"))
            v.tensor_scalar(tq5[:, 0, :], bank[1][:, 0:64], col("L1_attn_bq"), 0.0, ALU.add, ALU.min).then_inc(
                step("qmin5"), 1)
            own(v.tensor_scalar(tq5[:, 1, :], bank[1][:, 0:64], col("L1_attn_bq"), 0.0, ALU.add, ALU.max))
            dve.wait_ge(*after("v5_ps"))
            v.tensor_copy(vv5[:, 0:128], bank[6][0:64, 0:128]).then_inc(step("vv5"), 1)
            dve.wait_ge(sig("kexp5"), 1)
            v.scalar_tensor_tensor(k5[:], bank[2][0:64, 0:128], 0.0, tk5[:, 1, :], ALU.max, ALU.add).then_inc(
                step("k5"), 1)
            dve.wait_ge(sig("qexp5"), 1)
            v.tensor_tensor(q5[:], tq5[:, 1, :], tq5[:, 2, :], ALU.add).then_inc(step("q5"), 1)
            dve.wait_ge(*after("kvsum5_ps"))
            v.tensor_tensor(kv5[:], bank[7][:, 0:144], k("own_head"), ALU.mult).then_inc(step("kv5"), 1)
            dve.wait_ge(*after("num5_ps"))
            own(v.tensor_scalar(dn5[:, 0, :], bank[0][0:64, 128:144], 1e-6, None, ALU.add))
            own(v.reciprocal(dn5[:, 1, :], dn5[:, 0, :]))
            v.tensor_tensor(att5[:].rearrange("p (h g) -> p h g", g=8),
                            bank[0][0:64, 0:128].rearrange("p (h g) -> p h g", g=8),
                            each(dn5[:, 1, :], 8), ALU.mult).then_inc(step("att5"), 1)
            dve.wait_ge(*after("att5T_ps"))
            v.tensor_copy(attT5[:], bank[2][:, 0:64]).then_inc(step("attT5"), 1)
            dve.wait_ge(*after("o5_ps"))
            dve.wait_ge(sig("x4b"), 1)
            own(v.tensor_tensor(x5[:], bank[1][0:64, 0:128], x4b[:], ALU.add))

            moments(x5[:], 7, "mv7")
            dve.wait_ge(sig("rstd7"), 1)
            normed(xt6[:], x5[:], 7, tiny[:, 5:6], "xt6")
            dve.wait_ge(*after("xt6T_ps"))
            v.tensor_copy(xt6T[:, 1, :], bank[1][:, 0:64]).then_inc(step("xt6T"), 1)
            dve.wait_ge(*after("lg6_ps"))
            own(v.tensor_copy(lg6[:], bank[2][:, 0:8]))
            own(v.max(top6[:], lg6[:]))
            v.tensor_tensor(d6[:, 0:1], top6[:, 1:2], top6[:, 0:1], ALU.subtract).then_inc(step("d6"), 1)
            top_two(lg6[:], top6[:], idx6[:], idf6[:], hot6)
            dve.wait_ge(sig("e6"), 1)
            own(v.tensor_scalar(d6[:, 2:3], d6[:, 1:2], 1.0, None, ALU.add))
            own(v.reciprocal(d6[:, 3:4], d6[:, 2:3]))
            own(v.tensor_tensor(d6[:, 4:5], d6[:, 1:2], d6[:, 3:4], ALU.mult))
            own(v.tensor_scalar(hot6[:, 2, :], hot6[:, 0, :], d6[:, 3:4], None, ALU.mult))
            own(v.scalar_tensor_tensor(hot6[:, 0, :], hot6[:, 1, :], d6[:, 4:5], hot6[:, 2, :], ALU.mult, ALU.add))
            own(v.tensor_scalar(w4_6[:, 0, :], hot6[:, 0, 0:4], k("half")[:, 0:1], None, ALU.mult))
            v.scalar_tensor_tensor(w4_6[:, 1, :], hot6[:, 0, 4:8], k("half")[:, 1:2], w4_6[:, 0, :],
                                   ALU.mult, ALU.add).then_inc(step("w4_6"), 1)
            dve.wait_ge(*after("o6_ps"))
            zv = bank[5][:, :].rearrange("p (e f) -> p e f", e=4)
            for e in range(4):
                ins = v.bn_stats(st6[:, e, :], zv[:, e, :])
            own(ins)
            for e in range(4):
                ins = v.bn_aggr(mv6[:, e, :], st6[:, e, :])
            ins.then_inc(step("mv6e"), 1)
            dve.wait_ge(*after("mv6e"))
            v.tensor_scalar(ve6[:, 0, :], mv6[:, :, 1], 1e-6, None, ALU.add).then_inc(step("ve6"), 1)
            for e in range(4):
                ins = v.scalar_tensor_tensor(o6b[:, e, :], zv[:, e, :], mv6[:, e, 0:1],
                                             lng6[:, 128 * e:128 * e + 128], ALU.subtract, ALU.mult)
            ins.then_inc(step("o6b"), 1)
            dve.wait_ge(sig("rstd6e"), 1)
            own(v.tensor_tensor(w4_6[:, 2, :], ve6[:, 1, :], w4_6[:, 1, :], ALU.mult))
            v.tensor_tensor(wf6, over(k("fold"), 4), each(w4_6[:, 2, :], 64), ALU.mult).then_inc(step("wf6"), 1)
            dve.wait_ge(*after("out6_ps"))
            v.tensor_tensor(x6[:], bank[6][0:64, 0:128], x5[:], ALU.add).then_inc(step("x6"), 1)

        @block.gpsimd
        def _(pool):
            g = nc.gpsimd
            count = [0]

            def own(ins):
                count[0] += 1
                ins.then_inc(sig("pool_own"), 1)
                pool.wait_ge(sig("pool_own"), count[0])

            def inverse_root(dst, tmp, var, eps, name):
                own(g.tensor_scalar(tmp, var, eps, None, ALU.add))
                g.tensor_tensor(dst, tmp, halfpow[0:64, 0:1], ALU.pow).then_inc(sig(name), 1)

            pool.wait_ge(*after("halfpow"))
            pool.wait_ge(*after("mv0"))
            inverse_root(tiny[:, 0:1], tiny[:, 1:2], mv[:, 0, 1:2], 1e-5, "rstd0")
            for c in range(CHUNKS + 1):
                n = CHUNK if c < CHUNKS else 1
                pool.wait_ge(sig("chunk_hi"), c + 1)
                g.tensor_tensor(ctx_lo[:, CHUNK * c:CHUNK * c + n, :], chunk[c % 4][:, 0:n, :],
                                ctx_hi[:, CHUNK * c:CHUNK * c + n, :], ALU.subtract).then_inc(sig("chunk_lo"), 1)
            for b in range(CHUNKS + 1):
                pool.wait_ge(sig("prob1"), b + 1)
                if b == 0:
                    own(g.tensor_copy(acc[:, 0, 0:512], p1[:, 0, :]))
                elif b < CHUNKS:
                    own(g.tensor_tensor(acc[:, 0, 0:512], acc[:, 0, 0:512], p1[:, b, :], ALU.add))
                else:
                    g.tensor_tensor(acc[:, 0, 0:64], acc[:, 0, 0:64], p1[:, b, 0:64], ALU.add).then_inc(
                        sig("acc1"), 1)
            pool.wait_ge(*after("mv1"))
            own(g.tensor_scalar(tiny[:, 1:2], mv[:, 1, 1:2], 1.0 + 1e-5, 1e-10, ALU.mult, ALU.add))
            g.tensor_tensor(tiny[:, 7:8], tiny[:, 1:2], halfpow[0:64, 0:1], ALU.pow).then_inc(sig("rstd1"), 1)
            pool.wait_ge(*after("mv2"))
            inverse_root(tiny[:, 9:10], tiny[:, 8:9], mv[:, 2, 1:2], 1e-5, "rstd2")
            pool.wait_ge(sig("w3_loaded"), 80)
            pool.wait_ge(*after("xf"))
            g.tensor_tensor(xfb[:], xf[:], spread("L0_ffn_out_proj_b"), ALU.add).then_inc(sig("xfb"), 1)
            g.tensor_tensor(x2b[:], x2[:], spread("L0_ffn_ln2_b"), ALU.add).then_inc(sig("x2b"), 1)
            pool.wait_ge(*after("mv3"))
            inverse_root(tiny[:, 11:12], tiny[:, 10:11], mv[:, 3, 1:2], 1e-5, "rstd3")
            pool.wait_ge(sig("fold4_ps"), H4)
            g.memset(hz6[:], 0.0).then_inc(sig("hz6_zero"), 1)
            pool.wait_ge(*after("mv4"))
            inverse_root(tiny[:, 13:14], tiny[:, 12:13], mv[:, 4, 1:2], 1e-5, "rstd4")
            pool.wait_ge(*after("mv5"))
            inverse_root(tiny[:, 15:16], tiny[:, 14:15], mv[:, 5, 1:2], 1e-5, "rstd5")
            g.tensor_tensor(x3b[:], x3[:], spread("L1_xattn_proj_b"), ALU.add).then_inc(sig("x3b"), 1)

            def low_queries(grp):
                pool.wait_ge(sig("qk4_32"), grp + 1)
                at = slice(GROUP * grp, GROUP * grp + GROUP)
                g.tensor_tensor(qk_lo[:, at], qk32[:, at], qk_hi[:, at], ALU.subtract).then_inc(sig("qk4_lo"), 1)

            for grp in range(GROUPS):
                low_queries(grp)
            pool.wait_ge(sig("qk4_lo"), GROUPS)

            def add_block(n, s, m, first=False, width=1024, to=0):
                pool.wait_ge(sig("prob4"), m + 1)
                a = acc[:, to, 0:width]
                if first:
                    g.tensor_copy(a, P[:, s, 0:width]).then_inc(sig("acc4"), 1)
                else:
                    pool.wait_ge(sig("acc4"), n)
                    g.tensor_tensor(a, a, P[:, s, 0:width], ALU.add).then_inc(sig("acc4"), 1)

            for grp in range(GROUPS):
                if grp >= 2:
                    pool.wait_ge(sig("den4"), grp - 1)
                n0, m0 = BLOCKS * grp, BANKS * grp
                add_block(n0, grp % 2, m0 + 1, first=True, to=grp % 2)
                add_block(n0 + 1, (grp + 1) % 2, m0 + 3, to=grp % 2)
                with pool.Fori(1, CHUNKS) as i:
                    for s in range(2):
                        add_block(i * 2 + (n0 + s), (grp + s) % 2, i * 4 + (m0 + 2 * s + 1), to=grp % 2)
                add_block(n0 + BLOCKS - 1, grp % 2, m0 + BANKS - 1, width=GROUP, to=grp % 2)
                if grp < LAST:
                    pool.wait_ge(sig("acc4"), n0 + BLOCKS)
                    a = acc[:, grp % 2, :]
                    own(g.tensor_tensor(a[:, 0:512], a[:, 0:512], a[:, 512:1024], ALU.add))
                    g.tensor_tensor(a[:, 0:256], a[:, 0:256], a[:, 256:512], ALU.add).then_inc(sig("sums4"), 1)
            pool.wait_ge(*after("mv6"))
            inverse_root(tiny[:, 3:4], tiny[:, 2:3], mv[:, 6, 1:2], 1e-5, "rstd6")
            g.tensor_tensor(x4b[:], x4[:], spread("L1_attn_bo"), ALU.add).then_inc(sig("x4b"), 1)
            pool.wait_ge(*after("mv7"))
            inverse_root(tiny[:, 5:6], tiny[:, 4:5], mv[:, 7, 1:2], 1e-5, "rstd7")
            pool.wait_ge(sig("w6_loaded"), 16 * 9)
            pool.wait_ge(*after("w4_6"))
            g.tensor_tensor(wb6[:], lnb6[:].rearrange("p (e f) -> p e f", e=4), each(w4_6[:, 1, :], 128),
                            ALU.mult).then_inc(sig("wb6"), 1)
            pool.wait_ge(*after("ve6"))
            g.tensor_tensor(ve6[:, 1, :], ve6[:, 0, :], halfpow[:, 0:4], ALU.pow).then_inc(sig("rstd6e"), 1)

        @block.scalar
        def _(act):
            a = nc.scalar

            for c in range(CHUNKS + 1):
                n = CHUNK if c < CHUNKS else 1
                act.wait_ge(sig(f"ctx_loaded{c % 4}"), 16 * (c // 4 + 1))
                a.activation(ctx_hi[:, CHUNK * c:CHUNK * c + n, :], chunk[c % 4][:, 0:n, :], ACT.Copy).then_inc(
                    sig("chunk_hi"), 1)
                for j in range(0, n, 4):
                    m = min(4, n - j)
                    act.wait_ge(sig("chunk_half_transposed"), 2 * c + j // 4 + 1)
                    a.activation(ctxT_hi[:, CHUNK * c + j:CHUNK * c + j + m, :].rearrange("p t k -> p (t k)"),
                                 bank[2 * (c % 2) + j // 4][:, 0:128 * m], ACT.Copy, scale=CTX_UP).then_inc(
                        sig("chunkT_hi"), 1)
            SOFT = 1.0 / (ROOT * UP)
            for b in range(CHUNKS + 1):
                n = 512 if b < CHUNKS else 64
                act.wait_ge(sig("scores1"), b + 1)
                a.activation(P_hi[:, b, 0:n], bank[b][:, 0:n], ACT.Exp, scale=SOFT).then_inc(sig("prob1_hi"), 1)
                a.activation(p1[:, b, 0:n], bank[b][:, 0:n], ACT.Exp, scale=SOFT).then_inc(sig("prob1"), 1)
            a.activation(gate5[:, 0:1], col("stdp"), ACT.Exp, scale=-1.0).then_inc(sig("gate5"), 1)

            def fold_copy(*heads):
                both = big[:].rearrange("p (w h d) -> p h w d", w=2, h=H4)
                for h in heads:
                    act.wait_ge(sig("fold4_ps"), h + 1)
                    a.activation(both[:, h], bank[6 + h % 2][:, 0:256].rearrange("p (w d) -> p w d", w=2),
                                 ACT.Copy).then_inc(sig("fold4"), 1)

            fold_copy(0)
            act.wait_ge(sig("bqh"), 2)
            act.wait_ge(*after("q2_ps"))
            for f in range(2):
                ins = a.activation(Q2[:, f, :], bank[1][:, 0:64], ACT.Identity, bias=bqh[:, f:f + 1],
                                   scale=k("half")[:, f:f + 1])
            ins.then_inc(sig("q2"), 1)
            fold_copy(1, 2)
            act.wait_ge(*after("s2"))
            a.activation(e2[:, 0:256], s2[:, 0:256], ACT.Exp, scale=0.25).then_inc(sig("e2"), 1)
            fold_copy(3, 4, 5, 6, 7, 8, 9)

            act.wait_ge(*after("xfT_ps"))
            a.activation(xfT[:], over(bank[1][:, 0:64], 2), ACT.Copy).then_inc(sig("xfT"), 1)
            fold_copy(10)
            act.wait_ge(*after("q3_ps"))
            for f in range(2):
                ins = a.activation(Q3[:, f, :], bank[2][:, 0:64], ACT.Identity, bias=bqh[:, 2 + f:3 + f],
                                   scale=k("half")[:, f:f + 1])
            ins.then_inc(sig("q3"), 1)
            fold_copy(11, 12)
            act.wait_ge(*after("s3"))
            a.activation(e3[:], s3[:], ACT.Exp, scale=1.0 / math.sqrt(8.0)).then_inc(sig("e3"), 1)
            fold_copy(13, 14, 15)
            act.wait_ge(*after("neg3"))
            a.activation(eg3[:], lg3[:], ACT.Exp, bias=neg3[:, 0:1], accum_out=sum3[:, 0:1]).then_inc(sig("eg3"), 1)
            act.wait_ge(*after("exp3_ps"))
            a.activation(exp3, bank[0][:, :].rearrange("p (e f) -> p e f", e=4), ACT.Copy).then_inc(sig("exp3"), 1)

            def queries4(grp):
                act.wait_ge(sig("qk4_ps"), grp + 1)
                at = slice(GROUP * grp, GROUP * grp + GROUP)
                a.activation(qk_hi[:, at], bank[grp][:, 0:GROUP], ACT.Copy, scale=QK_UP).then_inc(sig("qk4_hi"), 1)
                a.activation(qk32[:, at], bank[grp][:, 0:GROUP], ACT.Copy, scale=QK_UP).then_inc(sig("qk4_32"), 1)

            def exponentials(group, i, block, j, width=512):
                s = (group + block) % 2
                if j in vector_banks(group) and (group == LAST or width == 512):
                    act.wait_ge(sig(f"shifted4_{j}"), nth_shifted(group, i, block, j))
                else:
                    act.wait_ge(sig(f"scores4_{j}"), nth(group, i, block, j))
                at = slice(512 * j, 512 * j + width)
                a.activation(ph4[:, s, at], bank[2 * s + j][:, 0:width], ACT.Exp, scale=SOFT)
                a.activation(P[:, s, at], bank[2 * s + j][:, 0:width], ACT.Exp, scale=SOFT).then_inc(
                    sig("prob4"), 1)

            def sums_copy(grp):
                if grp < LAST:
                    act.wait_ge(sig("rden4"), grp + 1)
                else:
                    act.wait_ge(sig("weighted_lo"), BLOCKS * GROUPS)
                if grp:
                    act.wait_ge(sig("y4_part"), grp)
                a.activation(u4[:], bank[4 + grp % 2][:, 0:GROUP], ACT.Copy).then_inc(sig("u4"), 1)

            def used(n):
                act.wait_ge(sig("weighted_hi"), n - 1)
                act.wait_ge(sig("acc4"), n - 1)
                act.wait_ge(sig("prob4_lo"), n - 1)

            queries4(0)
            for i in range(CHUNKS):
                if i >= 3:
                    act.wait_ge(sig("compared"), i - 2)
                for half in range(2):
                    act.wait_ge(sig("first_scores"), 2 * i + half + 1)
                    at = slice(512 * half, 512 * half + 512)
                    a.activation(pair[:, i % 2, at] if i else best[:, at], bank[4 + half][:, :], ACT.Copy,
                                 scale=1.0 / UP).then_inc(sig("first_copied"), 1)
                if i + 1 < GROUPS:
                    queries4(i + 1)

            for grp in range(GROUPS):
                n0 = BLOCKS * grp
                for s in range(2):
                    if n0 + s >= 2:
                        used(n0 + s)
                    for j in range(2):
                        exponentials(grp, 0, s, j)
                if grp:
                    sums_copy(grp - 1)
                with act.Fori(1, CHUNKS) as i:
                    for s in range(2):
                        used(i * 2 + (n0 + s))
                        for j in range(2):
                            exponentials(grp, i, s, j)
                used(n0 + BLOCKS - 1)
                exponentials(grp, CHUNKS, 0, 0, GROUP)

            sums_copy(GROUPS - 1)
            act.wait_ge(*after("kmin5"))
            a.activation(tk5[:, 1, :], tk5[:, 0, :], ACT.Exp).then_inc(sig("kexp5"), 1)
            act.wait_ge(*after("qmin5"))
            a.activation(tq5[:, 2, :], tq5[:, 0, :], ACT.Exp).then_inc(sig("qexp5"), 1)
            a.preload_act_table(ACT.Gelu)
            act.wait_ge(sig("hz6_zero"), 1)
            for half in range(2):
                act.wait_ge(sig("h6_ps"), half + 1)
                a.activation(hz6[:, 8 * half:8 * half + 8, 64 * half:64 * half + 64],
                             bank[3 + half][:, :].rearrange("p (c t) -> p c t", t=64), ACT.Gelu).then_inc(
                    sig("hz6"), 1)
            act.wait_ge(*after("d6"))
            a.activation(d6[:, 1:2], d6[:, 0:1], ACT.Exp).then_inc(sig("e6"), 1)

        @block.tensor
        def _(pe):
            mm = nc.tensor.matmul

            def one(o, lhsT, rhs):
                return mm(o, lhsT, rhs, start=True, stop=True)

            def busy(n, b):
                for _ in range(n):
                    one(bank[b][:, :], ident16[:], ctxT_hi[:, 0:4, :].rearrange("p t k -> p (t k)"))

            pe.wait_ge(sig("w0_loaded"), 48)
            one(bank[4][:, 0:128], w0[:, 0, :], w0[:, 1, :])
            one(bank[4][:, 128:129], w0[:, 1, :], col("L0_xattn_bq")).then_inc(step("fold0"), 1)
            one(bank[5][:, 0:128], w0[:, 2, :], w0[:, 3, :])
            pe.wait_ge(*after("bvrep"))
            mm(bank[5][0:64, 128:256], bvrep[:], w0[:, 3, :], start=True, stop=False)
            pe.wait_ge(*after("ones"))
            mm(bank[5][0:64, 128:256], ones[0:1, 0:64], row("L0_xattn_bo"), start=False, stop=True).then_inc(
                step("fold0b"), 1)
            pe.wait_ge(sig("ident_loaded"), 16)
            pe.wait_ge(*after("xn1"))
            nc.tensor.transpose(bank[6][:, 0:64], xn[:], ident[0:64, 0:64]).then_inc(step("xnT1_ps"), 1)
            pe.wait_ge(*after("xnT1"))
            pe.wait_ge(*after("a0"))
            one(bank[7][:, 0:64], a0[:], xnT[:]).then_inc(step("qk1_ps"), 1)

            def transposes(c):
                n = CHUNK if c < CHUNKS else 1
                pe.wait_ge(sig(f"ctx_loaded{c % 4}"), 16 * (c // 4 + 1))
                if c >= 2:
                    pe.wait_ge(sig("chunkT_lo"), 2 * (c - 1))
                for j in range(n):
                    ins = nc.tensor.transpose(bank[2 * (c % 2) + j // 4][:, 128 * (j % 4):128 * (j % 4) + 128],
                                              chunk[c % 4][:, j, :], ident)
                    if j % 4 == 3 or n == 1:
                        ins.then_inc(sig("chunk_half_transposed"), 1)

            def scores1_hi(c):
                if c == 0:
                    pe.wait_ge(*after("qk1"))
                    pe.wait_ge(*after("b0"))
                    pe.wait_ge(*after("xb1"))
                if c >= 2:
                    pe.wait_ge(sig("max1_part"), c - 1)
                pe.wait_ge(sig("chunkT_hi"), 2 * c + (2 if c < CHUNKS else 1))
                b = bank[4 + c % 2]
                for half in range(2 if c < CHUNKS else 1):
                    t0 = CHUNK * c + 4 * half
                    n = 4 if c < CHUNKS else 1
                    ins = mm(b[64 * half:64 * half + 64, 0:128 * n], qk1_hi[:],
                             ctxT_hi[:, t0:t0 + n, :].rearrange("p t k -> p (t k)"), start=True, stop=True)
                ins.then_inc(sig("scores1_hi"), 1)

            transposes(0)
            for c in range(CHUNKS + 1):
                if c < CHUNKS:
                    transposes(c + 1)
                if c == 0:
                    pe.wait_ge(*after("ident16"))
                scores1_hi(c)
                busy(1, 6)
            busy(5, 6)
            pe.wait_ge(*after("max1"))
            one(bank[7][0:1, 0:128], m1[:], ident).then_inc(step("max1_row"), 1)
            busy(3, 6)
            pe.wait_ge(*after("shift1"))
            pe.wait_ge(*after("up16"))
            pe.wait_ge(sig("chunkT_lo"), 2 * CHUNKS + 1)

            def scores1(b):
                n = CHUNK if b < CHUNKS else 1
                whole = bank[b][:, 0:64 * n].rearrange("p (t q) -> p t q", q=64)
                mm(whole, up16[0:1, :], over(shift1[:], n), start=True, stop=False)
                for j in range(n):
                    o = bank[b][:, 64 * j:64 * j + 64]
                    tile = CHUNK * b + j
                    mm(o, ctxT_hi[:, tile, :], qk1_hi[:], start=False, stop=False)
                    mm(o, ctxT_hi[:, tile, :], qk1_lo[:], start=False, stop=False)
                    ins = mm(o, ctxT_lo[:, tile, :], qk1_hi[:], start=False, stop=(j == n - 1))
                ins.then_inc(sig("scores1"), 1)

            def weighted1(b):
                n = CHUNK if b < CHUNKS else 1
                pe.wait_ge(sig("prob1_hi"), b + 1)
                pe.wait_ge(sig("prob1_lo"), b + 1)
                for j in range(n):
                    tile = CHUNK * b + j
                    at = slice(64 * j, 64 * j + 64)
                    mm(bank[7][:, 0:64], ctx_hi[:, tile, :], P_hi[:, b, at], start=(tile == 0), stop=False)
                    mm(bank[7][:, 0:64], ctx_hi[:, tile, :], P_lo[:, b, at], start=False, stop=False)
                    ins = mm(bank[7][:, 0:64], ctx_lo[:, tile, :], P_hi[:, b, at], start=False,
                             stop=(tile == TILES - 1))
                return ins

            pe.wait_ge(sig("chunk_lo"), CHUNKS + 1)
            for b in range(CHUNKS + 3):
                if b <= CHUNKS:
                    scores1(b)
                if b >= 2:
                    ins = weighted1(b - 2)
            ins.then_inc(step("u1"), 1)
            pe.wait_ge(sig("acc1"), 1)
            for j in range(CHUNK):
                ins = mm(bank[1][0:64, 0:1], acc[:, 0, 64 * j:64 * j + 64], ones[:, 0:1], start=(j == 0),
                         stop=(j == CHUNK - 1))
            ins.then_inc(step("den1"), 1)
            pe.wait_ge(*after("UT"))
            one(bank[0][0:64, 0:128], UT[:], b0[:]).then_inc(step("y1"), 1)

            def fold4(*heads):
                for h in heads:
                    if h == 0:
                        pe.wait_ge(sig("w4_loaded"), 64)
                    if h >= 2:
                        pe.wait_ge(sig("fold4"), h - 1)
                    j, head = h // 2, slice(64 * (h % 2), 64 * (h % 2) + 64)
                    one(bank[6 + h % 2][:, 0:128], wq4t[head, j, :], wk4t[head, j, :])
                    one(bank[6 + h % 2][:, 128:256], wv4t[head, j, :], wp4t[head, j, :]).then_inc(
                        sig("fold4_ps"), 1)

            pe.wait_ge(sig("w2_loaded"), 32)
            pe.wait_ge(sig("wvg"), 2)
            mm(bank[3][:, 0:128], ones[0:1, :], bvg[:], start=True, stop=False)
            busy(8, 5)
            pe.wait_ge(*after("xn2"))
            nc.tensor.transpose(bank[0][:, 0:64], xn[:], ident[0:64, 0:64]).then_inc(step("xnT2_ps"), 1)
            fold4(0)
            busy(2, 5)
            pe.wait_ge(*after("xd2"))
            one(bank[2][:, 0:64], w2[:, 1, :], xd2[:, 0, :]).then_inc(step("k2_ps"), 1)
            one(bank[1][:, 0:64], w2[:, 0, :], xd2[:, 0, :]).then_inc(step("q2_ps"), 1)
            mm(bank[3][:, 0:128], xd2[:].rearrange("p i t -> p (i t)"), wvg[:], start=False, stop=True).then_inc(
                step("v2_ps"), 1)
            fold4(1)
            busy(2, 5)
            pe.wait_ge(*after("kb2"))
            pe.wait_ge(sig("q2"), 1)
            one(bank[4][:, 0:256], Q2[:].rearrange("p i t -> p (i t)"), Kb2[:].rearrange("p h t -> p (h t)")).then_inc(
                step("s2_ps"), 1)
            fold4(2, 3)
            busy(3, 5)
            pe.wait_ge(sig("e2"), 1)
            for c in range(2):
                ins = nc.tensor.transpose(bank[0][:, 128 * c:128 * c + 128], e2[:, 128 * c:128 * c + 128], ident)
            ins.then_inc(step("pt2_ps"), 1)
            fold4(4)
            busy(1, 5)
            pe.wait_ge(*after("pt2"))
            pe.wait_ge(*after("v2"))
            for f in range(2):
                for c in range(2):
                    h = 4 * f + 2 * c
                    ins = one(bank[1][0:64, 17 * h:17 * h + 34], PT2[:, c, 64 * f:64 * f + 64],
                              V2[:, h:h + 2, :].rearrange("p h g -> p (h g)"))
            ins.then_inc(step("att2_ps"), 1)
            fold4(5, 6, 7)
            busy(2, 5)
            pe.wait_ge(*after("turned"))
            for h in range(8):
                ins = mm(bank[2][0:64, 0:128], k("pick", 64)[:, 64 * h:64 * h + 64],
                         turned[:, h, :, :].rearrange("p b g -> p (b g)"), start=(h == 0), stop=(h == 7))
            ins.then_inc(step("o2_ps"), 1)
            fold4(8, 9)

            pe.wait_ge(sig("w3_loaded"), 80)
            mm(bank[4][:, 0:128], ones[0:1, :], row("in_bv"), start=True, stop=False)
            busy(5, 5)
            pe.wait_ge(*after("xf"))
            nc.tensor.transpose(bank[1][:, 0:64], xf[:], ident[0:64, 0:64]).then_inc(step("xfT_ps"), 1)
            fold4(10)
            busy(2, 5)
            pe.wait_ge(*after("qin"))
            nc.tensor.transpose(bank[0][:, 0:64], qin[:], ident[0:64, 0:64]).then_inc(step("qinT_ps"), 1)
            pe.wait_ge(sig("xfT"), 1)
            mm(bank[4][:, 0:128], xfT[:].rearrange("p i t -> p (i t)"), w3[:, 2, :], start=False, stop=True)
            pe.wait_ge(*after("qinT"))
            one(bank[3][:, 0:64], w3[:, 1, :], qinT[:]).then_inc(step("k3_ps"), 1)
            one(bank[2][:, 0:64], w3[:, 0, :], qinT[:]).then_inc(step("q3_ps"), 1)
            busy(4, 5)
            pe.wait_ge(*after("kb3"))
            pe.wait_ge(sig("q3"), 1)
            one(bank[5][:, :], Q3[:].rearrange("p i t -> p (i t)"), Kb3[:].rearrange("p h t -> p (h t)")).then_inc(
                step("s3_ps"), 1)
            fold4(11, 12, 13)
            busy(3, 0)
            pe.wait_ge(sig("e3"), 1)
            for c in range(4):
                ins = nc.tensor.transpose(bank[0][:, 128 * c:128 * c + 128], e3[:, 128 * c:128 * c + 128], ident)
            ins.then_inc(step("pt3_ps"), 1)
            fold4(14)
            busy(2, 1)
            pe.wait_ge(*after("pt3"))
            pe.wait_ge(*after("v3"))
            for f in range(2):
                for c in range(4):
                    h = 8 * f + 2 * c
                    ins = one(bank[1][0:64, 9 * h:9 * h + 18], PT3[:, c, 64 * f:64 * f + 64],
                              V3[:, h:h + 2, :].rearrange("p h g -> p (h g)"))
            ins.then_inc(step("att3_ps"), 1)
            busy(4, 5)
            pe.wait_ge(*after("att3"))
            nc.tensor.transpose(bank[2][:, 0:64], att3[:], ident[0:64, 0:64]).then_inc(step("att3T_ps"), 1)
            busy(2, 5)
            pe.wait_ge(*after("attT3"))
            one(bank[3][0:64, 0:128], attT3[:], w3[:, 3, :]).then_inc(step("proj3_ps"), 1)
            fold4(15)
            mm(bank[5][:, 0:8], ones[0:1, :], row("gate_b"), start=True, stop=False)
            mm(bank[0][:, :], k("halfrows", 2), eb3[:], start=True, stop=False)
            busy(5, 4)
            pe.wait_ge(*after("y3"))
            nc.tensor.transpose(bank[4][:, 0:64], y3[:], ident[0:64, 0:64]).then_inc(step("y3T_ps"), 1)
            busy(2, 2)
            pe.wait_ge(*after("y3T"))
            lower = y3T[:, 1:3, :].rearrange("p i t -> p (i t)")
            upper = y3T[:, 0:2, :].rearrange("p i t -> p (i t)")
            mm(bank[5][:, 0:8], lower, gate3[:], start=False, stop=False)
            mm(bank[5][:, 0:8], upper, gate3[:], start=False, stop=True).then_inc(step("lg3_ps"), 1)
            mm(bank[0][:, :], lower, ew3[:, 0:512], start=False, stop=False)
            mm(bank[0][:, :], upper, ew3[:, 512:1024], start=False, stop=True).then_inc(step("exp3_ps"), 1)
            mm(bank[1][0:64, 0:128], ident[0:64, 0:64], y3[:], start=True, stop=False)
            busy(3, 2)
            pe.wait_ge(sig("exp3"), 1)
            pe.wait_ge(*after("wf3"))
            for e in range(4):
                ins = mm(bank[1][0:64, 0:128], wf3[:, e, :], exp3[:, e, :], start=False, stop=(e == 3))
            ins.then_inc(step("z3b_ps"), 1)

            busy(18, 3)
            pe.wait_ge(*after("xn4"))
            nc.tensor.transpose(bank[2][:, 0:64], xn[:], ident[0:64, 0:64]).then_inc(step("xnT4_ps"), 1)
            busy(2, 3)
            pe.wait_ge(*after("xnT4"))
            pe.wait_ge(sig("fold4"), H4)

            def queries(g):
                for j in range(4):
                    ins = one(bank[g][:, 64 * j:64 * j + 64], a4[:, 4 * g + j, :], xnT4[:])
                ins.then_inc(sig("qk4_ps"), 1)

            queries(0)

            ctxT = ctxT_hi[:].rearrange("p t k -> p (t k)")

            def edge_scores(g, b=6):
                for q in range(2):
                    a = GROUP * g + 128 * q
                    ins = mm(bank[b][:, 128 * q:128 * q + 128], qk_hi[:, a:a + 128], ctxT[:, CHUNKS * 1024:],
                             start=True, stop=True)
                ins.then_inc(sig("edge4_scores"), 1)

            def strip_scores(q, strip, g, b, free=None, ready="strip_scores"):
                if free is not None:
                    pe.wait_ge(sig("strip_max"), free)
                a = GROUP * g + 128 * q
                mm(bank[b][:, :], qk_hi[:, a:a + 128], ctxT[:, bass.ds(strip * 512, 512)], start=True,
                   stop=True).then_inc(sig(ready), 1)

            def turn_shifts(g):
                pe.wait_ge(sig("shiftcols"), g + 1)
                for q in range(2):
                    ins = mm(bank[7][:, 128 * q:128 * q + 128], shiftcols[:, q, :], ident16[:], start=True,
                             stop=True)
                ins.then_inc(sig("shift_ps"), 1)

            pe.wait_ge(sig("qk4_hi"), 1)
            pe.wait_ge(*after("ident16"))
            edge_scores(0, 3)

            def first_strips(i):
                for q in range(2):
                    for half in range(2):
                        n, b = 2 * i + half, 4 + 2 * q + half
                        if i:
                            pe.wait_ge(sig(("first_copied", "strip_max")[q]), n - 1)
                        strip_scores(q, i * 2 + half, 0, b, ready=("first_scores", "strip_scores")[q])

            def scores4(s, tile, g, tiles=BLOCK, shift=True):
                hi, lo = (x[:, GROUP * g:GROUP * g + GROUP] for x in (qk_hi, qk_lo))
                for j in range(tiles):
                    o = bank[2 * s + j // 2][:, 256 * (j % 2):256 * (j % 2) + 256]
                    kh = ctxT_hi[:, bass.ds(tile + j, 1), :].rearrange("p t k -> p (t k)")
                    kl = ctxT_lo[:, bass.ds(tile + j, 1), :].rearrange("p t k -> p (t k)")
                    last = (j // 2 in vector_banks(g) and (g == LAST or tiles > 1)) and (j % 2 == 1 or tiles == 1)
                    mm(o, kh, hi, start=(j % 2 == 0), stop=False)
                    mm(o, kh, lo, start=False, stop=False)
                    ins = mm(o, kl, hi, start=False, stop=last)
                    if last:
                        ins.then_inc(sig(f"scores4_{j // 2}"), 1)
                if shift and g < LAST:
                    pe.wait_ge(sig("shiftrow"), g + 1)
                    shift_by_row(s, tiles)

            def shift_by_row(s, tiles=BLOCK):
                w = min(2, tiles)
                mm(bank[2 * s][:, 0:256 * w].rearrange("p (t q) -> p t q", t=w), up16[0:1, :],
                   over(shiftrow[:], w), start=False, stop=True).then_inc(sig("scores4_0"), 1)

            first_strips(0)
            queries(1)
            first_strips(1)
            queries(2)
            first_strips(2)
            pe.wait_ge(sig("edge4_max"), 1)
            queries(3)
            first_strips(3)
            pe.wait_ge(sig("qk4_lo"), 1)
            pe.wait_ge(sig("qk4_32"), 2)
            scores4(0, 0, 0, shift=False)
            first_strips(4)
            first_strips(5)
            pe.wait_ge(sig("qk4_32"), GROUPS)
            scores4(1, 4, 0, shift=False)
            assert CHUNKS == 6
            pe.wait_ge(sig("qk4_lo"), GROUPS)

            def tiles4(x, tile, tiles):
                return [x[:, bass.ds(tile + j, 1), :].rearrange("p t k -> p (t k)") for j in range(tiles)]

            def weighted_hi(s, m, tile, g, tiles=BLOCK, first=False):
                pe.wait_ge(sig("prob4"), m)
                o = bank[4 + g % 2][:, 0:256]
                for j, (kh, kl) in enumerate(zip(tiles4(ctx_hi, tile, tiles), tiles4(ctx_lo, tile, tiles))):
                    at = slice(256 * j, 256 * j + 256)
                    mm(o, kh, ph4[:, s, at], start=(first and j == 0), stop=False)
                    ins = mm(o, kl, ph4[:, s, at], start=False, stop=False)
                ins.then_inc(sig("weighted_hi"), 1)

            def weighted_lo(s, n, tile, g, tiles=BLOCK, last=False):
                pe.wait_ge(sig("prob4_lo"), n + 1)
                for j, kh in enumerate(tiles4(ctx_hi, tile, tiles)):
                    ins = mm(bank[4 + g % 2][:, 0:256], kh, pl4[:, s, 256 * j:256 * j + 256], start=False,
                             stop=(last and j == tiles - 1))
                ins.then_inc(sig("weighted_lo"), 1)

            def finish4(g):
                o = sums_place(g)
                pe.wait_ge(sig("sums4"), g + 1)
                for j in range(4):
                    ins = one(o[:, j:j + 1], acc[:, g % 2, 64 * j:64 * j + 64], ones[:, 0:1])
                ins.then_inc(sig("den4"), 1)

            def output4(g):
                pe.wait_ge(sig("u4"), g + 1)
                for j in range(4):
                    ins = one(bank[4 + g % 2][0:64, 128 * j:128 * j + 128], u4[:, 64 * j:64 * j + 64],
                              v4[:, 4 * g + j, :])
                ins.then_inc(sig("y4_part"), 1)

            for g in range(GROUPS):
                n0, m0 = BLOCKS * g, BANKS * g
                ahead = g + 1 < GROUPS
                even, odd = g % 2, (g + 1) % 2

                def strips(q, i):
                    for half in range(2 if ahead else 0):
                        n = i * 4 + (STRIPS * g + FIRST + 2 * q + half)
                        strip_scores(q, i * 2 + half, g + 1, 6 + half, free=n - 1)

                if g:
                    pe.wait_ge(sig("prob4"), m0 - 1)
                    scores4(even, 0, g)
                else:
                    pe.wait_ge(sig("first_copied"), FIRST)
                    busy(5, 4)
                    turn_shifts(0)
                    pe.wait_ge(sig("shiftrow"), 1)
                    shift_by_row(even)
                    shift_by_row(odd)
                if ahead:
                    pe.wait_ge(sig("shift4"), g + 1)
                strips(0, 0)
                if g:
                    weighted_hi(odd, m0, TILES - 1, g - 1, 1)
                    weighted_lo(even, n0 - 2, TILES - 5, g - 1)
                    pe.wait_ge(sig("prob4"), m0)
                    scores4(odd, 4, g)
                strips(1, 0)
                if g >= 2:
                    pe.wait_ge(sig("x4_part"), 4 * (g - 1))
                weighted_hi(even, m0 + 2, 0, g, first=True)
                if ahead:
                    pe.wait_ge(sig("strip_max"), STRIPS * g + FIRST + 3)
                    edge_scores(g + 1)
                if g:
                    weighted_lo(odd, n0 - 1, TILES - 1, g - 1, 1, last=True)
                    finish4(g - 1)

                def block4(s, i):
                    slot = (even, odd)[s]
                    n, m = i * 2 + (n0 + s), i * 4 + (m0 + 2 * s)
                    pe.wait_ge(sig("prob4"), m - 2)
                    scores4(slot, i * 8 + 4 * s, g)
                    if ahead and s == 0:
                        pe.wait_ge(sig("edge4_max"), g + 2)
                    strips(s, i)
                    weighted_hi(1 - slot, m, i * 8 + (4 * s - 4), g)
                    weighted_lo(slot, n - 2, i * 8 + (4 * s - 8), g)

                block4(0, 1)
                if g:
                    output4(g - 1)
                block4(1, 1)
                with pe.Fori(2, CHUNKS) as i:
                    for s in range(2):
                        block4(s, i)
                pe.wait_ge(sig("prob4"), m0 + BANKS - 3)
                scores4(even, TILES - 1, g, 1)
                weighted_hi(odd, m0 + BANKS - 1, TILES - 5, g)
                weighted_lo(even, n0 + BLOCKS - 3, TILES - 9, g)
                if ahead:
                    turn_shifts(g + 1)
            weighted_hi(LAST % 2, BANKS * GROUPS, TILES - 1, LAST, 1)
            weighted_lo(1 - LAST % 2, BLOCKS * GROUPS - 2, TILES - 5, LAST)
            weighted_lo(LAST % 2, BLOCKS * GROUPS - 1, TILES - 1, LAST, 1, last=True)
            busy(2, 1)
            output4(LAST)
            finish4(LAST)
            busy(6, 1)

            pe.wait_ge(sig("w6_loaded"), 16 * 9)
            pe.wait_ge(sig("w5_loaded"), 16)
            mm(bank[2][0:64, 0:128], ones[0:1, 0:64], row("L1_attn_bk"), start=True, stop=False)
            mm(bank[6][0:64, 0:128], ones[0:1, 0:64], row("L1_attn_bv"), start=True, stop=False)
            for half in range(2):
                mm(bank[3 + half][:, :].rearrange("p (c t) -> p c t", t=64), b16[:],
                   each(ident[0:16, 8 * half:8 * half + 8], 64), start=True, stop=False)
            busy(2, 1)
            pe.wait_ge(*after("xn5"))
            nc.tensor.transpose(bank[0][:, 0:64], xn[:], ident[0:64, 0:64]).then_inc(step("xnT5_ps"), 1)
            busy(2, 7)
            pe.wait_ge(*after("xnT5"))
            mm(bank[2][0:64, 0:128], xnT5[:], w5[:, 1, :], start=False, stop=True).then_inc(step("k5_ps"), 1)
            one(bank[1][:, 0:64], w5[:, 0, :], xnT5[:]).then_inc(step("q5_ps"), 1)
            mm(bank[6][0:64, 0:128], xnT5[:], w5[:, 2, :], start=False, stop=True).then_inc(step("v5_ps"), 1)
            mm(bank[5][:, :], k("halfrows", 2), b26[:], start=True, stop=False)
            busy(2, 0)
            pe.wait_ge(*after("k5"))
            pe.wait_ge(*after("vv5"))
            one(bank[7][:, 0:144], k5[:], vv5[:]).then_inc(step("kvsum5_ps"), 1)
            busy(2, 2)
            pe.wait_ge(*after("kv5"))
            pe.wait_ge(*after("q5"))
            one(bank[0][0:64, 0:144], q5[:], kv5[:]).then_inc(step("num5_ps"), 1)
            busy(4, 6)
            pe.wait_ge(*after("att5"))
            nc.tensor.transpose(bank[2][:, 0:64], att5[:], ident[0:64, 0:64]).then_inc(step("att5T_ps"), 1)
            busy(2, 6)
            pe.wait_ge(*after("attT5"))
            pe.wait_ge(*after("wo5"))
            one(bank[1][0:64, 0:128], attT5[:], wo5[:]).then_inc(step("o5_ps"), 1)

            busy(8, 7)
            pe.wait_ge(*after("xt6"))
            nc.tensor.transpose(bank[1][:, 0:64], xt6[:], ident[0:64, 0:64]).then_inc(step("xt6T_ps"), 1)
            mm(bank[5][:, :].rearrange("p (e f) -> p e f", e=4), k("dup", 64), over(xt6[:], 4), start=False,
               stop=False)
            pe.wait_ge(*after("xt6T"))
            lower = xt6T[:, 1:3, :].rearrange("p i t -> p (i t)")
            upper = xt6T[:, 0:2, :].rearrange("p i t -> p (i t)")
            for half in range(2):
                for c in range(8):
                    e, f = 4 * half + c // 2, c % 2
                    ins = mm(bank[3 + half][:, 64 * c:64 * c + 64], w16[:, e, 128 * f:128 * f + 128],
                             xt6T[:, 1, :], start=False, stop=(c == 7))
                ins.then_inc(sig("h6_ps"), 1)
            mm(bank[2][:, 0:8], lower, gate6[:], start=True, stop=False)
            mm(bank[2][:, 0:8], upper, gate6[:], start=False, stop=True).then_inc(step("lg6_ps"), 1)
            for half in range(2):
                pe.wait_ge(sig("hz6"), half + 1)
                for c in range(8):
                    e, f = c // 2, c % 2
                    ins = mm(bank[5][:, 128 * e:128 * e + 128], hz6[:, 8 * half + c, :],
                             w26[:, 4 * half + e, f, :], start=False, stop=(half == 1 and c == 7))
            ins.then_inc(step("o6_ps"), 1)
            pe.wait_ge(sig("wb6"), 1)
            for e in range(4):
                mm(bank[6][0:64, 0:128], k("fold"), wb6[:, e, :], start=(e == 0), stop=False)
            busy(5, 7)
            pe.wait_ge(*after("wf6"))
            for e in range(4):
                ins = mm(bank[6][0:64, 0:128], wf6[:, e, :], o6b[:, e, :], start=False, stop=(e == 3))
            ins.then_inc(step("out6_ps"), 1)


BLOCKS = (TILES + BLOCK - 1) // BLOCK
BANKS = (TILES + 1) // 2
STRIPS = 4 * CHUNKS
FIRST = 2 * CHUNKS
LAST = GROUPS - 1


def vector_banks(g):
    return (0, 1) if g == LAST else (1,)


def nth(g, i, s, j):
    return i * 2 + ((BLOCKS - j) * g + s + 1)


def nth_shifted(g, i, s, j):
    return nth(0 if j == 0 else g, i, s, j)


def kernel(**inputs):
    import numpy as _np
    import concourse.bacc as _bacc
    from concourse import mybir as _mybir
    from concourse.bass_utils import run_bass_kernel_spmd as _run

    a = {n: _np.asarray(v) for n, v in inputs.items()}

    def stack(*xs):
        return _np.stack(xs, 1)

    def pairs(w):
        return w.reshape(8, 2, 128, 64).transpose(1, 3, 0, 2).reshape(128, 8, 128)

    wqkv = a["L0_ffn_in_proj_w"]
    bqkv = a["L0_ffn_in_proj_b"]
    vectors = dict(a, in_bq=bqkv[0:128], in_bk=bqkv[128:256], in_bv=bqkv[256:384], gate_b=a["L0_ffn_gate_b"],
                   stdp=_np.repeat(a["L1_attn_stdp"], 8))
    lay = {
        "x": a["x"][0], "ctx": a["ctx_1024"][0], "const": CONST,
        "cols": _np.stack([vectors[n] for n in COLS], 1),
        "rows": _np.concatenate([vectors[n] for n in ROWS])[None],
        "wide": _np.broadcast_to(_np.stack([vectors[n] for n in WIDE])[None], (64, len(WIDE), 128)),
        "w0": stack(a["L0_xattn_Wq"], a["L0_xattn_Wk"], a["L0_xattn_Wv"], a["L0_xattn_Wo"].T),
        "w2": stack(a["L0_attn_Wq"], a["L0_attn_Wk"]),
        "L0_attn_Wv": a["L0_attn_Wv"],
        "w3": stack(wqkv[0:128].T, wqkv[128:256].T, wqkv[256:384].T, a["L0_ffn_out_proj_w"].T),
        "gate3": a["L0_ffn_gate_w"].T,
        "ew3": a["L0_ffn_expert_w"].transpose(2, 0, 1).reshape(128, 1024),
        "eb3": a["L0_ffn_expert_b"].reshape(2, 512),
        "wq4t": pairs(a["L1_xattn_w_q"]), "wk4t": pairs(a["L1_xattn_w_k"]), "wv4t": pairs(a["L1_xattn_w_v"]),
        "wp4t": a["L1_xattn_proj_w"].reshape(128, 8, 128).transpose(2, 1, 0),
        "w5": stack(a["L1_attn_Wq"].T, a["L1_attn_Wk"].T, a["L1_attn_Wv"].T, a["L1_attn_Wo"].T),
        "L1_ffn_gate_w": a["L1_ffn_gate_w"],
        "w16": a["L1_ffn_w1"].transpose(1, 0, 2),
        "w26": a["L1_ffn_w2"].reshape(8, 2, 128, 128).transpose(2, 0, 1, 3),
        "b16": a["L1_ffn_b1"].reshape(16, 128), "b26": a["L1_ffn_b2"].reshape(2, 512),
        "lng6": a["L1_ffn_ln_g"].reshape(2, 512), "lnb6": a["L1_ffn_ln_b"].reshape(2, 512),
    }
    nc = _bacc.Bacc("TRN2", target_bir_lowering=False, num_devices=1)
    arrays, t = {}, {}
    for name, v in lay.items():
        v = _np.ascontiguousarray(v)
        arrays[f"in_{name}"] = v
        t[name] = nc.dram_tensor(f"in_{name}", v.shape, _mybir.dt.from_np(v.dtype), kind="ExternalInput").ap()
    out = nc.dram_tensor("out", (64, 128), _mybir.dt.float32, kind="ExternalOutput").ap()
    build(nc, t, out)
    r = _run(nc, [arrays], core_ids=[0])
    return r.results[0]["out"].reshape(1, 64, 128)
```
